# Optimizing a Trainium2 kernel written in Bass

```python
import numpy as np
import jax
import jax.numpy as jnp

def _softmax(x, axis=-1):
    return jax.nn.softmax(x, axis=axis)

def _gelu(x):
    return jax.nn.gelu(x, approximate=True)

def _silu(x):
    return jax.nn.silu(x)

def _sigmoid(x):
    return jax.nn.sigmoid(x)

def _layernorm(x, axis=-1, eps=1e-05):
    m = jnp.mean(x, axis=axis, keepdims=True)
    v = jnp.var(x, axis=axis, keepdims=True)
    return (x - m) / jnp.sqrt(v + eps)

def _scatter_add(tgt, idx, src, axis=0):
    return tgt.at[idx].add(src)

def _segment_sum(src, seg, n):
    return jax.ops.segment_sum(src, seg, n)
kernel_name = 'mk_flamingo_gated_d4_seqx_r8_dfc532'

def setup_inputs(seed: int=0):
    np.random.seed(seed)
    _w = jnp.asarray

    def _rec_inputs():
        import jax
        import jax.numpy as jnp
        _rk = jax.random.key(seed)
        x = 0.0003765 + 1 * jax.random.normal(jax.random.fold_in(_rk, 1), (8, 128, 256), jnp.float32)
        _lenS = 128 - jax.random.randint(jax.random.fold_in(_rk, 7), (8,), 0, max(1, 128 // 4) + 1, jnp.int32)
        _lenS2 = 128 - jax.random.randint(jax.random.fold_in(_rk, 8), (8,), 0, max(1, 128 // 4) + 1, jnp.int32)
        _ctx_2048P = jax.random.normal(jax.random.fold_in(_rk, 11), (8, 16, 256), jnp.float32)
        _ctx_2048c = jax.random.dirichlet(jax.random.fold_in(_rk, 511), 0.3 * jnp.ones((16,), jnp.float32), (8, 128))
        _ctx_2048t = jnp.einsum('bsk,bkd->bsd', _ctx_2048c, _ctx_2048P)
        _ctx_2048t = _ctx_2048t * jax.lax.rsqrt(jnp.mean(jnp.square(_ctx_2048t)) + 1e-12) * 0.953939
        ctx_2048 = -0.000292821 + 1.00034 * (_ctx_2048t + 0.3 * jax.random.normal(jax.random.fold_in(_rk, 611), (8, 128, 256), jnp.float32))
        _validS = jnp.arange(128)[None, :] < _lenS[:, None]
        _validS2 = jnp.arange(128)[None, :] < _lenS2[:, None]
        _causal = jnp.tril(jnp.ones((128, 128), dtype=bool))
        mask_BxSxS2_ff0 = jnp.where(jnp.ones((8, 128, 128), dtype=bool), 0.0, -1000000000.0).astype(jnp.float32)
        mask_BxS2_bk0 = jnp.logical_not(jnp.broadcast_to(_validS2[:, :], (8, 128)))
        _g = jax.random.normal(jax.random.fold_in(_rk, 9001), (2, 4), jnp.float32)
        _g = jnp.sign(_g) * jnp.maximum(jnp.abs(_g), 1.0) + (_g == 0) * 1.0
        g_xattn = _g[0]
        g_ffn = _g[1]
        return (x, ctx_2048, mask_BxSxS2_ff0, mask_BxS2_bk0, g_xattn, g_ffn)
    x, ctx_2048, mask_BxSxS2_ff0, mask_BxS2_bk0, g_xattn, g_ffn = _rec_inputs()

    def _L0_xattn_setup():
        import jax, jax.numpy as jnp
        import numpy as np
        key = jax.random.key(seed)
        k1, k2, k3, k4, k5 = jax.random.split(key, 5)
        B, D_MODEL, L = (2, 128, 256)
        HEAD_DIM = 8
        H = D_MODEL // HEAD_DIM
        return {'k': jax.random.normal(k1, (B, D_MODEL, L), dtype=jnp.float32), 'v': jax.random.normal(k2, (B, D_MODEL, L), dtype=jnp.float32), 'q': jax.random.normal(k3, (B, D_MODEL, L), dtype=jnp.float32), 'ssm_kernel': jax.random.normal(k4, (H, L), dtype=jnp.float32), 'D': jax.random.normal(k5, (H,), dtype=jnp.float32), 'head_dim': HEAD_DIM}
    _L0_xattn_all = _L0_xattn_setup()
    _L0_xattn_in = {k: v for k, v in _L0_xattn_all.items() if k in ('ssm_kernel', 'D')}
    del _L0_xattn_all

    def _L0_ffn_setup():
        import math
        import jax, jax.numpy as jnp
        import numpy as np
        from jax import lax
        D = 256
        I = 128
        E = 32
        K = 4
        NG = 8
        TKG = 3
        NSH = 2
        SCALE = 2.5
        CF = 1.25
        B, S = (2, 256)

        def _router(x, router_w, e_bias):
            scores = jax.nn.sigmoid(x @ router_w.T)
            sc = scores + e_bias[None, :]
            T = x.shape[0]
            gs = sc.reshape(T, NG, E // NG)
            group_scores = lax.top_k(gs, 2)[0].sum(-1)
            _, gidx = lax.top_k(group_scores, TKG)
            gmask = jnp.zeros((T, NG), sc.dtype).at[jnp.arange(T)[:, None], gidx].set(1.0)
            smask = jnp.repeat(gmask, E // NG, axis=1)
            masked = jnp.where(smask > 0, sc, 0.0)
            _, topk_idx = lax.top_k(masked, K)
            topk_w = jnp.take_along_axis(scores, topk_idx, axis=1)
            topk_w = topk_w / (topk_w.sum(-1, keepdims=True) + 1e-20)
            topk_w = topk_w * SCALE
            return (topk_idx.astype(jnp.int32), topk_w)

        def _moe_forward(hidden_states, router_w, e_bias, W_gate, W_up, W_down, shared_gate, shared_up, shared_down):
            b, s, d = hidden_states.shape
            T = b * s
            C = int(math.ceil(CF * T / E))
            EC = E * C
            x = hidden_states.reshape(T, d)
            topk_idx, topk_w = _router(x, router_w, e_bias)
            expert_flat = topk_idx.reshape(-1)
            w_flat = topk_w.reshape(-1)
            tok_flat = jnp.repeat(jnp.arange(T, dtype=jnp.int32), K)
            sort_ix = jnp.argsort(expert_flat)
            e_sorted = expert_flat[sort_ix]
            tok_s = tok_flat[sort_ix]
            w_s = w_flat[sort_ix]
            counts = jnp.zeros(E, jnp.int32).at[e_sorted].add(1)
            group_start = jnp.concatenate([jnp.zeros(1, jnp.int32), jnp.cumsum(counts)[:-1].astype(jnp.int32)])
            pos = jnp.arange(T * K, dtype=jnp.int32) - group_start[e_sorted]
            valid = pos < C
            dest = e_sorted * C + jnp.where(valid, pos, 0)
            slots_token = jnp.zeros(EC, jnp.int32).at[dest].add(jnp.where(valid, tok_s, 0))
            slots_w = jnp.zeros(EC, w_s.dtype).at[dest].add(jnp.where(valid, w_s, 0.0))
            Xp = x[slots_token].reshape(E, C, d)
            G = jnp.einsum('ecd,edi->eci', Xp, W_gate)
            U = jnp.einsum('ecd,edi->eci', Xp, W_up)
            Y = jnp.einsum('eci,eid->ecd', jax.nn.silu(G) * U, W_down)
            Yf = Y.reshape(EC, d) * slots_w[:, None]
            out = jnp.zeros((T, d), x.dtype).at[slots_token].add(Yf)
            shared = jax.nn.silu(x @ shared_gate.T) * (x @ shared_up.T) @ shared_down.T
            return (out + shared).reshape(b, s, d)
        key = jax.random.key(seed)
        ks = jax.random.split(key, 8)

        def rn(k, shape, scale=0.02):
            return jax.random.normal(k, shape, jnp.float32) * scale
        return {'hidden_states': jax.random.normal(ks[0], (B, S, D), jnp.float32), 'router_w': rn(ks[1], (E, D)), 'e_bias': jnp.zeros((E,), jnp.float32), 'W_gate': rn(ks[2], (E, D, I)), 'W_up': rn(ks[3], (E, D, I)), 'W_down': rn(ks[4], (E, I, D)), 'shared_gate': rn(ks[5], (I * NSH, D)), 'shared_up': rn(ks[6], (I * NSH, D)), 'shared_down': rn(ks[7], (D, I * NSH))}
    _L0_ffn_all = _L0_ffn_setup()
    _L0_ffn_in = {k: v for k, v in _L0_ffn_all.items() if k in ('router_w', 'e_bias', 'W_gate', 'W_up', 'W_down', 'shared_gate', 'shared_up', 'shared_down')}
    del _L0_ffn_all

    def _L1_xattn_setup():
        import jax, jax.numpy as jnp
        import numpy as np
        D_MODEL = 256
        NUM_HEADS = 16
        HEAD_DIM = D_MODEL // NUM_HEADS

        def _fq_sym(x, axis):
            s = jnp.max(jnp.abs(x), axis=axis, keepdims=True) / 127.0
            s = jnp.maximum(s, 1e-08)
            q = jnp.clip(jnp.round(x / s), -127.0, 127.0) * s
            return x + jax.lax.stop_gradient(q - x)

        def _fq_unsigned(x, axis):
            s = jnp.max(x, axis=axis, keepdims=True) / 255.0
            s = jnp.maximum(s, 1e-08)
            q = jnp.clip(jnp.round(x / s), 0.0, 255.0) * s
            return x + jax.lax.stop_gradient(q - x)
        key = jax.random.key(seed)
        ks = jax.random.split(key, 8)
        B, N, M, C = (2, 256, 64, D_MODEL)
        return {'x': jax.random.normal(ks[0], (B, N, C), jnp.float32), 'cond': jax.random.normal(ks[1], (B, M, C), jnp.float32), 'Wq': jax.random.normal(ks[2], (C, C), jnp.float32) * 0.02, 'bq': jnp.zeros((C,), jnp.float32), 'Wkv': jax.random.normal(ks[3], (C, 2 * C), jnp.float32) * 0.02, 'bkv': jnp.zeros((2 * C,), jnp.float32), 'Wp': jax.random.normal(ks[4], (C, C), jnp.float32) * 0.02, 'bp': jnp.zeros((C,), jnp.float32)}
    _L1_xattn_all = _L1_xattn_setup()
    _L1_xattn_in = {k: v for k, v in _L1_xattn_all.items() if k in ('Wq', 'bq', 'Wkv', 'bkv', 'Wp', 'bp')}
    del _L1_xattn_all

    def _L1_ffn_setup():
        import jax, jax.numpy as jnp
        import numpy as np
        DIM = 256
        EXPERT_DIM = 128
        N_EXPERTS = 16
        TOPK = 2
        N_SHARED = 1
        B, T = (4, 256)
        key = jax.random.key(seed)
        ks = jax.random.split(key, 9)
        s = 0.02
        return {'x': jax.random.normal(ks[0], (B, T, DIM), jnp.float32), 'router_w': jax.random.normal(ks[1], (N_EXPERTS, DIM), jnp.float32) * s, 'router_bias': jnp.zeros((N_EXPERTS,), jnp.float32), 'Wu': jax.random.normal(ks[2], (N_EXPERTS, DIM, EXPERT_DIM), jnp.float32) * s, 'Wg': jax.random.normal(ks[3], (N_EXPERTS, DIM, EXPERT_DIM), jnp.float32) * s, 'Wd': jax.random.normal(ks[4], (N_EXPERTS, EXPERT_DIM, DIM), jnp.float32) * s, 'Su': jax.random.normal(ks[5], (N_SHARED, DIM, EXPERT_DIM * TOPK), jnp.float32) * s, 'Sg': jax.random.normal(ks[6], (N_SHARED, DIM, EXPERT_DIM * TOPK), jnp.float32) * s, 'Sd': jax.random.normal(ks[7], (N_SHARED, EXPERT_DIM * TOPK, DIM), jnp.float32) * s}
    _L1_ffn_all = _L1_ffn_setup()
    _L1_ffn_in = {k: v for k, v in _L1_ffn_all.items() if k in ('router_w', 'router_bias', 'Wu', 'Wg', 'Wd', 'Su', 'Sg', 'Sd')}
    del _L1_ffn_all

    def _L2_xattn_setup():
        import jax, jax.numpy as jnp
        import numpy as np
        B, Q_LEN, E = (8, 16, 256)
        CACHE_LEN = 512
        key = jax.random.key(seed)
        ks = jax.random.split(key, 9)
        s = 1.0 / np.sqrt(E)
        return {'x': jax.random.normal(ks[0], (B, Q_LEN, E), jnp.float32), 'attention_mask': jnp.zeros((B, Q_LEN, CACHE_LEN), jnp.float32), 'k_cache': jax.random.normal(ks[1], (B, CACHE_LEN, E), jnp.float32), 'v_cache': jax.random.normal(ks[2], (B, CACHE_LEN, E), jnp.float32), 'Wq': jax.random.normal(ks[3], (E, E), jnp.float32) * s, 'bq': jax.random.normal(ks[4], (E,), jnp.float32) * s, 'Wk': jax.random.normal(ks[5], (E, E), jnp.float32) * s, 'bk': jax.random.normal(ks[6], (E,), jnp.float32) * s, 'Wv': jax.random.normal(ks[7], (E, E), jnp.float32) * s, 'bv': jax.random.normal(ks[8], (E,), jnp.float32) * s}
    _L2_xattn_all = _L2_xattn_setup()
    _L2_xattn_in = {k: v for k, v in _L2_xattn_all.items() if k in ('Wq', 'bq', 'Wk', 'bk', 'Wv', 'bv')}
    del _L2_xattn_all

    def _L2_ffn_setup():
        import jax, jax.numpy as jnp
        import numpy as np
        D_MODEL = 256
        HIDDEN = 4 * D_MODEL
        B, S = (2, 512)

        def bit_linear(x, w, b):
            gamma_x = jnp.clip(jnp.max(jnp.abs(x), axis=-1, keepdims=True), 1e-05, None)
            scale_x = 127.0 / gamma_x
            x_dq = jnp.clip(jnp.round(x * scale_x), -128.0, 127.0) / scale_x
            x_ste = x + jax.lax.stop_gradient(x_dq - x)
            gamma_w = jnp.clip(jnp.mean(jnp.abs(w)), 1e-05, None)
            w_dq = jnp.clip(jnp.round(w / gamma_w), -1.0, 1.0) * gamma_w
            w_ste = w + jax.lax.stop_gradient(w_dq - w)
            return jnp.einsum('bsd,hd->bsh', x_ste, w_ste) + b
        key = jax.random.key(seed)
        ks = jax.random.split(key, 7)
        std = 0.02
        return {'x': jax.random.normal(ks[0], (B, S, D_MODEL), dtype=jnp.float32), 'gate_w': jax.random.normal(ks[1], (HIDDEN, D_MODEL), dtype=jnp.float32) * std, 'gate_b': jnp.zeros((HIDDEN,), dtype=jnp.float32), 'val_w': jax.random.normal(ks[2], (HIDDEN, D_MODEL), dtype=jnp.float32) * std, 'val_b': jnp.zeros((HIDDEN,), dtype=jnp.float32), 'out_w': jax.random.normal(ks[3], (D_MODEL, HIDDEN), dtype=jnp.float32) * std, 'out_b': jnp.zeros((D_MODEL,), dtype=jnp.float32)}
    _L2_ffn_all = _L2_ffn_setup()
    _L2_ffn_in = {k: v for k, v in _L2_ffn_all.items() if k in ('gate_w', 'gate_b', 'val_w', 'val_b', 'out_w', 'out_b')}
    del _L2_ffn_all

    def _L3_xattn_setup():
        import jax, jax.numpy as jnp
        import numpy as np
        key = jax.random.key(seed)
        k1, k2, k3 = jax.random.split(key, 3)
        B, S, D, M = (8, 256, 256, 128)
        hidden_states = jax.random.normal(k1, (B, S, D), dtype=jnp.float32)
        memory_tokens = jax.random.normal(k2, (B, M, D), dtype=jnp.float32)
        memory_mask = jax.random.randint(k3, (B, M), 0, 2).astype(jnp.bool_)
        return {'hidden_states': hidden_states, 'memory_tokens': memory_tokens, 'memory_mask': memory_mask}
    _L3_xattn_all = _L3_xattn_setup()
    _L3_xattn_in = {k: v for k, v in _L3_xattn_all.items() if k in ()}
    del _L3_xattn_all

    def _L3_ffn_setup():
        import jax, jax.numpy as jnp
        import numpy as np
        import math
        D_MODEL = 256
        D_FF = 1024
        NUM_EXPERTS = 8
        TOP_K = 2
        CAPACITY_FACTOR = 1.25
        BATCH, SEQ = (4, 256)

        def _moe_forward(x, Wg, w1, w2):
            B, T, d = x.shape
            S = B * T
            E, K = (NUM_EXPERTS, TOP_K)
            C = math.ceil(CAPACITY_FACTOR * S * K / E)
            xr = x.reshape(S, d)
            probs = jax.nn.softmax(xr @ Wg, axis=-1)
            gate_vals, expert_idx = jax.lax.top_k(probs, K)
            flat_e = expert_idx.reshape(-1)
            oh = jax.nn.one_hot(flat_e, E, dtype=jnp.int32)
            pos = jnp.sum((jnp.cumsum(oh, axis=0) - 1) * oh, axis=1)
            kept = pos < C
            i = jnp.arange(S * K)
            slot = i % K * S + i // K
            sentinel = S * K
            pos_w = jnp.where(kept, pos, C)
            dispatch_mask = jnp.full((E, C), sentinel, dtype=jnp.int32)
            dispatch_mask = dispatch_mask.at[flat_e, pos_w].set(slot.astype(jnp.int32), mode='drop')
            combine_weights = (gate_vals * kept.reshape(S, K)).T
            dispatched = xr[dispatch_mask.reshape(-1) % S].reshape(E, C, d)
            h = jax.nn.relu(jnp.einsum('ecd,edf->ecf', dispatched, w1))
            expert_out = jnp.einsum('ecf,efd->ecd', h, w2)
            rerouted = jnp.zeros((S * K + 1, d), dtype=expert_out.dtype)
            rerouted = rerouted.at[dispatch_mask.reshape(-1)].set(expert_out.reshape(-1, d))
            rerouted = rerouted[:-1].reshape(K, S, d)
            out = jnp.einsum('ks,ksm->sm', combine_weights, rerouted)
            return out.reshape(B, T, d)
        key = jax.random.key(seed)
        k1, k2, k3, k4 = jax.random.split(key, 4)
        x = jax.random.normal(k1, (BATCH, SEQ, D_MODEL), dtype=jnp.float32)
        Wg = jax.random.normal(k2, (D_MODEL, NUM_EXPERTS), dtype=jnp.float32) * 0.02
        w1 = jax.random.normal(k3, (NUM_EXPERTS, D_MODEL, D_FF), dtype=jnp.float32) * 0.02
        w2 = jax.random.normal(k4, (NUM_EXPERTS, D_FF, D_MODEL), dtype=jnp.float32) * 0.02
        return {'x': x, 'Wg': Wg, 'w1': w1, 'w2': w2}
    _L3_ffn_all = _L3_ffn_setup()
    _L3_ffn_in = {k: v for k, v in _L3_ffn_all.items() if k in ('Wg', 'w1', 'w2')}
    del _L3_ffn_all
    return {'x': x, 'ctx_2048': ctx_2048, 'mask_BxSxS2_ff0': mask_BxSxS2_ff0, 'mask_BxS2_bk0': mask_BxS2_bk0, 'g_xattn': g_xattn, 'g_ffn': g_ffn, 'L0_xattn_ssm_kernel': _L0_xattn_in['ssm_kernel'], 'L0_xattn_D': _L0_xattn_in['D'], 'L0_ffn_router_w': _L0_ffn_in['router_w'], 'L0_ffn_e_bias': _L0_ffn_in['e_bias'], 'L0_ffn_W_gate': _L0_ffn_in['W_gate'], 'L0_ffn_W_up': _L0_ffn_in['W_up'], 'L0_ffn_W_down': _L0_ffn_in['W_down'], 'L0_ffn_shared_gate': _L0_ffn_in['shared_gate'], 'L0_ffn_shared_up': _L0_ffn_in['shared_up'], 'L0_ffn_shared_down': _L0_ffn_in['shared_down'], 'L1_xattn_Wq': _L1_xattn_in['Wq'], 'L1_xattn_bq': _L1_xattn_in['bq'], 'L1_xattn_Wkv': _L1_xattn_in['Wkv'], 'L1_xattn_bkv': _L1_xattn_in['bkv'], 'L1_xattn_Wp': _L1_xattn_in['Wp'], 'L1_xattn_bp': _L1_xattn_in['bp'], 'L1_ffn_router_w': _L1_ffn_in['router_w'], 'L1_ffn_router_bias': _L1_ffn_in['router_bias'], 'L1_ffn_Wu': _L1_ffn_in['Wu'], 'L1_ffn_Wg': _L1_ffn_in['Wg'], 'L1_ffn_Wd': _L1_ffn_in['Wd'], 'L1_ffn_Su': _L1_ffn_in['Su'], 'L1_ffn_Sg': _L1_ffn_in['Sg'], 'L1_ffn_Sd': _L1_ffn_in['Sd'], 'L2_xattn_Wq': _L2_xattn_in['Wq'], 'L2_xattn_bq': _L2_xattn_in['bq'], 'L2_xattn_Wk': _L2_xattn_in['Wk'], 'L2_xattn_bk': _L2_xattn_in['bk'], 'L2_xattn_Wv': _L2_xattn_in['Wv'], 'L2_xattn_bv': _L2_xattn_in['bv'], 'L2_ffn_gate_w': _L2_ffn_in['gate_w'], 'L2_ffn_gate_b': _L2_ffn_in['gate_b'], 'L2_ffn_val_w': _L2_ffn_in['val_w'], 'L2_ffn_val_b': _L2_ffn_in['val_b'], 'L2_ffn_out_w': _L2_ffn_in['out_w'], 'L2_ffn_out_b': _L2_ffn_in['out_b'], 'L3_ffn_Wg': _L3_ffn_in['Wg'], 'L3_ffn_w1': _L3_ffn_in['w1'], 'L3_ffn_w2': _L3_ffn_in['w2']}

def reference(x, ctx_2048, mask_BxSxS2_ff0, mask_BxS2_bk0, g_xattn, g_ffn, L0_xattn_ssm_kernel, L0_xattn_D, L0_ffn_router_w, L0_ffn_e_bias, L0_ffn_W_gate, L0_ffn_W_up, L0_ffn_W_down, L0_ffn_shared_gate, L0_ffn_shared_up, L0_ffn_shared_down, L1_xattn_Wq, L1_xattn_bq, L1_xattn_Wkv, L1_xattn_bkv, L1_xattn_Wp, L1_xattn_bp, L1_ffn_router_w, L1_ffn_router_bias, L1_ffn_Wu, L1_ffn_Wg, L1_ffn_Wd, L1_ffn_Su, L1_ffn_Sg, L1_ffn_Sd, L2_xattn_Wq, L2_xattn_bq, L2_xattn_Wk, L2_xattn_bk, L2_xattn_Wv, L2_xattn_bv, L2_ffn_gate_w, L2_ffn_gate_b, L2_ffn_val_w, L2_ffn_val_b, L2_ffn_out_w, L2_ffn_out_b, L3_ffn_Wg, L3_ffn_w1, L3_ffn_w2):
    import jax
    import jax.numpy as jnp

    def _L0_xattn_ref(k, v, q, ssm_kernel, D, head_dim):
        import jax, jax.numpy as jnp
        import numpy as np
        B, HD, L = k.shape
        H = HD // head_dim
        fft_size = 2 * L
        k_ = k.reshape(B, H, head_dim, L)
        v_ = v.reshape(B, H, head_dim, L)
        q_ = q.reshape(B, H, head_dim, L)
        kv = jnp.einsum('bhil,bhjl->bijhl', k_, v_)
        kv_f = jnp.fft.rfft(kv, n=fft_size)
        kernel_f = jnp.fft.rfft(ssm_kernel, n=fft_size)
        y = jnp.fft.irfft(kv_f * kernel_f, n=fft_size)[..., :L]
        out = y + kv * D[None, None, None, :, None]
        out = jnp.einsum('bijhl,bhil->bjhl', out, q_)
        out = jnp.transpose(out, (0, 2, 1, 3)).reshape(B, H * head_dim, L)
        return out.astype(k.dtype)

    def _L0_ffn_ref(hidden_states, router_w, e_bias, W_gate, W_up, W_down, shared_gate, shared_up, shared_down):
        import math
        import jax, jax.numpy as jnp
        import numpy as np
        from jax import lax
        D = 256
        I = 128
        E = 32
        K = 4
        NG = 8
        TKG = 3
        NSH = 2
        SCALE = 2.5
        CF = 1.25
        B, S = (2, 256)

        def _router(x, router_w, e_bias):
            scores = jax.nn.sigmoid(x @ router_w.T)
            sc = scores + e_bias[None, :]
            T = x.shape[0]
            gs = sc.reshape(T, NG, E // NG)
            group_scores = lax.top_k(gs, 2)[0].sum(-1)
            _, gidx = lax.top_k(group_scores, TKG)
            gmask = jnp.zeros((T, NG), sc.dtype).at[jnp.arange(T)[:, None], gidx].set(1.0)
            smask = jnp.repeat(gmask, E // NG, axis=1)
            masked = jnp.where(smask > 0, sc, 0.0)
            _, topk_idx = lax.top_k(masked, K)
            topk_w = jnp.take_along_axis(scores, topk_idx, axis=1)
            topk_w = topk_w / (topk_w.sum(-1, keepdims=True) + 1e-20)
            topk_w = topk_w * SCALE
            return (topk_idx.astype(jnp.int32), topk_w)

        def _moe_forward(hidden_states, router_w, e_bias, W_gate, W_up, W_down, shared_gate, shared_up, shared_down):
            b, s, d = hidden_states.shape
            T = b * s
            C = int(math.ceil(CF * T / E))
            EC = E * C
            x = hidden_states.reshape(T, d)
            topk_idx, topk_w = _router(x, router_w, e_bias)
            expert_flat = topk_idx.reshape(-1)
            w_flat = topk_w.reshape(-1)
            tok_flat = jnp.repeat(jnp.arange(T, dtype=jnp.int32), K)
            sort_ix = jnp.argsort(expert_flat)
            e_sorted = expert_flat[sort_ix]
            tok_s = tok_flat[sort_ix]
            w_s = w_flat[sort_ix]
            counts = jnp.zeros(E, jnp.int32).at[e_sorted].add(1)
            group_start = jnp.concatenate([jnp.zeros(1, jnp.int32), jnp.cumsum(counts)[:-1].astype(jnp.int32)])
            pos = jnp.arange(T * K, dtype=jnp.int32) - group_start[e_sorted]
            valid = pos < C
            dest = e_sorted * C + jnp.where(valid, pos, 0)
            slots_token = jnp.zeros(EC, jnp.int32).at[dest].add(jnp.where(valid, tok_s, 0))
            slots_w = jnp.zeros(EC, w_s.dtype).at[dest].add(jnp.where(valid, w_s, 0.0))
            Xp = x[slots_token].reshape(E, C, d)
            G = jnp.einsum('ecd,edi->eci', Xp, W_gate)
            U = jnp.einsum('ecd,edi->eci', Xp, W_up)
            Y = jnp.einsum('eci,eid->ecd', jax.nn.silu(G) * U, W_down)
            Yf = Y.reshape(EC, d) * slots_w[:, None]
            out = jnp.zeros((T, d), x.dtype).at[slots_token].add(Yf)
            shared = jax.nn.silu(x @ shared_gate.T) * (x @ shared_up.T) @ shared_down.T
            return (out + shared).reshape(b, s, d)
        return _moe_forward(hidden_states, router_w, e_bias, W_gate, W_up, W_down, shared_gate, shared_up, shared_down)

    def _L1_xattn_ref(x, cond, Wq, bq, Wkv, bkv, Wp, bp):
        import jax, jax.numpy as jnp
        import numpy as np
        D_MODEL = 256
        NUM_HEADS = 16
        HEAD_DIM = D_MODEL // NUM_HEADS

        def _fq_sym(x, axis):
            s = jnp.max(jnp.abs(x), axis=axis, keepdims=True) / 127.0
            s = jnp.maximum(s, 1e-08)
            q = jnp.clip(jnp.round(x / s), -127.0, 127.0) * s
            return x + jax.lax.stop_gradient(q - x)

        def _fq_unsigned(x, axis):
            s = jnp.max(x, axis=axis, keepdims=True) / 255.0
            s = jnp.maximum(s, 1e-08)
            q = jnp.clip(jnp.round(x / s), 0.0, 255.0) * s
            return x + jax.lax.stop_gradient(q - x)
        B, N, C = x.shape
        H, hd = (NUM_HEADS, HEAD_DIM)
        q = (x @ Wq + bq).reshape(1, B * N, H, hd)
        kv = (cond @ Wkv + bkv).reshape(1, -1, 2, H, hd)
        k, v = (kv[:, :, 0], kv[:, :, 1])
        scale = 1.0 / np.sqrt(hd).astype(np.float32)
        q = jnp.transpose(q * scale, (0, 2, 1, 3))
        k = jnp.transpose(k, (0, 2, 1, 3))
        v = jnp.transpose(v, (0, 2, 1, 3))
        q = _fq_sym(q, axis=-1)
        k = _fq_sym(k, axis=-1)
        v = _fq_sym(v, axis=2)
        attn = jnp.einsum('bhqd,bhkd->bhqk', q, k)
        attn = jax.nn.softmax(attn.astype(jnp.float32), axis=-1)
        attn = _fq_unsigned(attn, axis=-1)
        out = jnp.einsum('bhqk,bhkd->bhqd', attn, v)
        out = jnp.transpose(out, (0, 2, 1, 3)).reshape(B, N, C)
        return out @ Wp + bp

    def _L1_ffn_ref(x, router_w, router_bias, Wu, Wg, Wd, Su, Sg, Sd):
        import jax, jax.numpy as jnp
        import numpy as np
        DIM = 256
        EXPERT_DIM = 128
        N_EXPERTS = 16
        TOPK = 2
        N_SHARED = 1
        B, T = (4, 256)
        Bx, Tx, D = x.shape
        flat = x.reshape(Bx * Tx, D)
        logits = flat @ router_w.T
        scores = jax.nn.softmax(logits, axis=-1)
        _, topk_idx = jax.lax.top_k(logits + router_bias, TOPK)
        topk_scores = jnp.take_along_axis(scores, topk_idx, axis=-1)
        topk_scores = topk_scores / topk_scores.sum(-1, keepdims=True)
        combine = jnp.einsum('nk,nke->ne', topk_scores, jax.nn.one_hot(topk_idx, N_EXPERTS, dtype=scores.dtype))
        out = jnp.zeros_like(flat)
        for e in range(N_EXPERTS):
            h = jax.nn.silu(flat @ Wu[e]) * (flat @ Wg[e])
            out = out + combine[:, e:e + 1] * (h @ Wd[e])
        for s in range(N_SHARED):
            out = out + jax.nn.silu(flat @ Su[s]) * (flat @ Sg[s]) @ Sd[s]
        return out.reshape(Bx, Tx, D)

    def _L2_xattn_ref(x, attention_mask, k_cache, v_cache, Wq, bq, Wk, bk, Wv, bv):
        import jax, jax.numpy as jnp
        import numpy as np
        B, Q_LEN, E = (8, 16, 256)
        CACHE_LEN = 512
        Q = jnp.einsum('bqe,fe->bqf', x, Wq) + bq
        K_new = jnp.einsum('bqe,fe->bqf', x, Wk) + bk
        V_new = jnp.einsum('bqe,fe->bqf', x, Wv) + bv
        q_len = x.shape[1]
        end_step = attention_mask.shape[-1]
        past_kv_len = end_step - q_len
        k_cache = jax.lax.dynamic_update_slice(k_cache, K_new, (0, past_kv_len, 0))
        v_cache = jax.lax.dynamic_update_slice(v_cache, V_new, (0, past_kv_len, 0))
        K = k_cache[:, :end_step, :]
        V = v_cache[:, :end_step, :]
        scale = 1.0 / jnp.sqrt(jnp.asarray(Q.shape[-1], Q.dtype))
        scores = jnp.einsum('bqe,bke->bqk', Q, K) * scale + attention_mask
        attn = jax.nn.softmax(scores, axis=-1)
        return jnp.einsum('bqk,bke->bqe', attn, V)

    def _L2_ffn_ref(x, gate_w, gate_b, val_w, val_b, out_w, out_b):
        import jax, jax.numpy as jnp
        import numpy as np
        D_MODEL = 256
        HIDDEN = 4 * D_MODEL
        B, S = (2, 512)

        def bit_linear(x, w, b):
            gamma_x = jnp.clip(jnp.max(jnp.abs(x), axis=-1, keepdims=True), 1e-05, None)
            scale_x = 127.0 / gamma_x
            x_dq = jnp.clip(jnp.round(x * scale_x), -128.0, 127.0) / scale_x
            x_ste = x + jax.lax.stop_gradient(x_dq - x)
            gamma_w = jnp.clip(jnp.mean(jnp.abs(w)), 1e-05, None)
            w_dq = jnp.clip(jnp.round(w / gamma_w), -1.0, 1.0) * gamma_w
            w_ste = w + jax.lax.stop_gradient(w_dq - w)
            return jnp.einsum('bsd,hd->bsh', x_ste, w_ste) + b
        gate = jax.nn.silu(bit_linear(x, gate_w, gate_b))
        val = bit_linear(x, val_w, val_b)
        return bit_linear(gate * val, out_w, out_b)

    def _L3_xattn_ref(hidden_states, memory_tokens, memory_mask):
        import jax, jax.numpy as jnp
        import numpy as np
        B, S, D = hidden_states.shape
        scale = 1.0 / jnp.sqrt(jnp.asarray(D, hidden_states.dtype))
        scores = jnp.einsum('bsd,bmd->bsm', hidden_states, memory_tokens) * scale
        neg_inf = jnp.asarray(-1e+30, scores.dtype)
        scores = jnp.where(memory_mask[:, None, :], scores, neg_inf)
        attn = jax.nn.softmax(scores, axis=-1)
        readout = jnp.einsum('bsm,bmd->bsd', attn, memory_tokens)
        valid_b = jnp.any(memory_mask, axis=-1)
        out = jnp.where(valid_b[:, None, None], readout, jnp.zeros_like(readout))
        return out

    def _L3_ffn_ref(x, Wg, w1, w2):
        import jax, jax.numpy as jnp
        import numpy as np
        import math
        D_MODEL = 256
        D_FF = 1024
        NUM_EXPERTS = 8
        TOP_K = 2
        CAPACITY_FACTOR = 1.25
        BATCH, SEQ = (4, 256)

        def _moe_forward(x, Wg, w1, w2):
            B, T, d = x.shape
            S = B * T
            E, K = (NUM_EXPERTS, TOP_K)
            C = math.ceil(CAPACITY_FACTOR * S * K / E)
            xr = x.reshape(S, d)
            probs = jax.nn.softmax(xr @ Wg, axis=-1)
            gate_vals, expert_idx = jax.lax.top_k(probs, K)
            flat_e = expert_idx.reshape(-1)
            oh = jax.nn.one_hot(flat_e, E, dtype=jnp.int32)
            pos = jnp.sum((jnp.cumsum(oh, axis=0) - 1) * oh, axis=1)
            kept = pos < C
            i = jnp.arange(S * K)
            slot = i % K * S + i // K
            sentinel = S * K
            pos_w = jnp.where(kept, pos, C)
            dispatch_mask = jnp.full((E, C), sentinel, dtype=jnp.int32)
            dispatch_mask = dispatch_mask.at[flat_e, pos_w].set(slot.astype(jnp.int32), mode='drop')
            combine_weights = (gate_vals * kept.reshape(S, K)).T
            dispatched = xr[dispatch_mask.reshape(-1) % S].reshape(E, C, d)
            h = jax.nn.relu(jnp.einsum('ecd,edf->ecf', dispatched, w1))
            expert_out = jnp.einsum('ecf,efd->ecd', h, w2)
            rerouted = jnp.zeros((S * K + 1, d), dtype=expert_out.dtype)
            rerouted = rerouted.at[dispatch_mask.reshape(-1)].set(expert_out.reshape(-1, d))
            rerouted = rerouted[:-1].reshape(K, S, d)
            out = jnp.einsum('ks,ksm->sm', combine_weights, rerouted)
            return out.reshape(B, T, d)
        return _moe_forward(x, Wg, w1, w2)
    x = x + jnp.tanh(g_xattn[0]) * _L0_xattn_ref(ctx_2048, ctx_2048, _layernorm(x, axis=-1), L0_xattn_ssm_kernel, L0_xattn_D, 8)
    x = x + jnp.tanh(g_ffn[0]) * _L0_ffn_ref(_layernorm(x, axis=-1), L0_ffn_router_w, L0_ffn_e_bias, L0_ffn_W_gate, L0_ffn_W_up, L0_ffn_W_down, L0_ffn_shared_gate, L0_ffn_shared_up, L0_ffn_shared_down)
    x = x + jnp.tanh(g_xattn[1]) * _L1_xattn_ref(_layernorm(x, axis=-1), ctx_2048, L1_xattn_Wq, L1_xattn_bq, L1_xattn_Wkv, L1_xattn_bkv, L1_xattn_Wp, L1_xattn_bp)
    x = x + jnp.tanh(g_ffn[1]) * _L1_ffn_ref(_layernorm(x, axis=-1), L1_ffn_router_w, L1_ffn_router_bias, L1_ffn_Wu, L1_ffn_Wg, L1_ffn_Wd, L1_ffn_Su, L1_ffn_Sg, L1_ffn_Sd)
    x = x + jnp.tanh(g_xattn[2]) * _L2_xattn_ref(_layernorm(x, axis=-1), mask_BxSxS2_ff0, ctx_2048, ctx_2048, L2_xattn_Wq, L2_xattn_bq, L2_xattn_Wk, L2_xattn_bk, L2_xattn_Wv, L2_xattn_bv)
    x = x + jnp.tanh(g_ffn[2]) * _L2_ffn_ref(_layernorm(x, axis=-1), L2_ffn_gate_w, L2_ffn_gate_b, L2_ffn_val_w, L2_ffn_val_b, L2_ffn_out_w, L2_ffn_out_b)
    x = x + jnp.tanh(g_xattn[3]) * _L3_xattn_ref(_layernorm(x, axis=-1), ctx_2048, mask_BxS2_bk0)
    x = x + jnp.tanh(g_ffn[3]) * _L3_ffn_ref(_layernorm(x, axis=-1), L3_ffn_Wg, L3_ffn_w1, L3_ffn_w2)
    return x

_drawn_inputs = setup_inputs


def setup_inputs(seed=0):
    import zlib

    import numpy as np

    out = dict(_drawn_inputs(seed))
    spreads = {'L0_ffn_e_bias': (0.0, 0.8),
     'L1_xattn_bq': (0.0, 0.8),
     'L1_xattn_bkv': (0.0, 0.8),
     'L1_xattn_bp': (0.0, 0.8),
     'L1_ffn_router_bias': (0.0, 0.8),
     'L2_ffn_gate_b': (0.0, 0.8),
     'L2_ffn_val_b': (0.0, 0.8),
     'L2_ffn_out_b': (0.0, 2.0)}
    factors = {'g_ffn': 8.0,
     'L0_ffn_router_w': 8.0,
     'L0_ffn_W_gate': 8.0,
     'L0_ffn_W_up': 8.0,
     'L0_ffn_W_down': 8.0,
     'L0_ffn_shared_gate': 8.0,
     'L0_ffn_shared_up': 8.0,
     'L0_ffn_shared_down': 8.0,
     'L1_xattn_Wq': 8.0,
     'L1_xattn_Wkv': 8.0,
     'L1_xattn_Wp': 8.0,
     'L1_ffn_router_w': 8.0,
     'L1_ffn_Wu': 8.0,
     'L1_ffn_Wg': 8.0,
     'L1_ffn_Wd': 8.0,
     'L1_ffn_Su': 8.0,
     'L1_ffn_Sg': 8.0,
     'L1_ffn_Sd': 8.0,
     'L2_xattn_Wq': 8.0,
     'L2_xattn_bq': 8.0,
     'L2_xattn_Wk': 8.0,
     'L2_xattn_bk': 64.0,
     'L2_xattn_Wv': 8.0,
     'L2_xattn_bv': 32.925,
     'L2_ffn_gate_w': 8.0,
     'L2_ffn_val_w': 8.0,
     'L2_ffn_out_w': 8.0,
     'L3_ffn_Wg': 8.0,
     'L3_ffn_w1': 8.0,
     'L3_ffn_w2': 8.0}
    for name, (base, spread) in spreads.items():
        noise = np.random.default_rng([zlib.crc32(name.encode()), seed]).standard_normal(out[name].shape)
        drawn = base * np.exp(spread * noise) if base else spread * noise
        out[name] = jnp.asarray(drawn.astype(out[name].dtype))
    for name, factor in factors.items():
        out[name] = (out[name] * factor).astype(out[name].dtype)
    return out
```

```python
from contextlib import ExitStack

import concourse.bass as bass
from concourse import mybir

P = 128
NT = 8
T = P * NT
D = 256
DC = D // P
LN_EPS = 1e-5
MAGIC = 12582912.0

F32 = mybir.dt.float32
BF16 = mybir.dt.bfloat16
I32 = mybir.dt.int32
U8 = mybir.dt.uint8
ALU = mybir.AluOpType
ACT = mybir.ActivationFunctionType
AX = mybir.AxisListType

ARENA = 25 * 1024


class Chain:

    def __init__(self, eng, sem):
        self.eng, self.sem, self.n = eng, sem, 0

    def mark(self, ins):
        self.n += 1
        return ins.then_inc(self.sem, 1)

    def wait(self):
        self.eng.wait_ge(self.sem, self.n)

    def step(self, ins):
        self.mark(ins)
        self.wait()


def build(nc, A, out):
    ctx = ExitStack()
    sems = {}

    def sem(name):
        if name not in sems:
            sems[name] = ctx.enter_context(nc.semaphore(name))
        return sems[name]

    def sb(name, shape, dt=F32):
        return ctx.enter_context(nc.sbuf_tensor(name, shape, dt))

    with ctx:
        psum = ctx.enter_context(nc.psum_tensor("psum", [P, 8 * 512], F32))
        bank = [psum[:, i * 512:(i + 1) * 512] for i in range(8)]

        x = sb("x", [P, NT, D])
        xn = sb("xn", [P, NT, D])
        xnT = sb("xnT", [P, DC, T])
        ctok = sb("ctok", [P, NT, D])
        cT = sb("cT", [P, DC, T])
        ident = sb("ident", [P, P])
        identb = sb("identb", [P, P], BF16)
        onesb = sb("onesb", [P, P], BF16)
        gates = sb("gates", [P, 8])
        tg = sb("tg", [P, 8])
        stats = sb("stats", [P, NT, 6])
        mv = sb("mv", [P, NT, 2])
        std = sb("std", [P, NT])
        rstd = sb("rstd", [P, NT])
        newt = sb("newt", [P, NT])
        var_eps = sb("var_eps", [P, NT])
        arena = sb("arena", [P, ARENA])
        wring = sb("wring", [P, 10 * 1024])

        class Region:

            def __init__(self, buf, size):
                self.buf, self.at, self.size = buf, 0, size

            def f32(self, *shape):
                n = 1
                for s in shape:
                    n *= s
                v = self.buf[:, self.at:self.at + n]
                self.at += n
                assert self.at <= self.size, self.at
                return shaped(v, shape)

            def bf16(self, *shape):
                n = 1
                for s in shape:
                    n *= s
                words = (n + 1) // 2
                v = self.buf[:, self.at:self.at + words].bitcast(BF16)
                self.at += words
                assert self.at <= self.size, self.at
                return shaped(v, shape)

        def shaped(v, shape):
            if len(shape) == 1:
                return v
            names = "abcd"[:len(shape)]
            return v.rearrange(f"p ({' '.join(names)}) -> p {' '.join(names)}",
                               **{m: s for m, s in zip(names[1:], shape[1:])})

        def bcast(ap, axis, n):
            dims = [list(d) for d in ap.ap]
            dims.insert(axis, [0, n])
            return bass.AP(tensor=ap.tensor, offset=ap.offset, ap=dims)

        def ln_vector(dve, seq, k):
            if k == 0:
                dve.wait_ge(sem("x_loaded"), 16)
            for t in range(NT):
                seq.mark(nc.vector.bn_stats(stats[:, t, :], x[:, t, :]))
            seq.wait()
            for t in range(NT):
                seq.mark(nc.vector.bn_aggr(mv[:, t, :], stats[:, t, :]))
            seq.wait()
            nc.vector.tensor_scalar(var_eps[:], mv[:, :, 1], LN_EPS, None, ALU.add).then_inc(sem("var_ready"), 1)
            dve.wait_ge(sem("std_ready"), k + 1)
            seq.step(nc.vector.reciprocal(rstd[:], std[:]))
            seq.step(nc.vector.tensor_tensor(newt[:], rstd[:], rstd[:], ALU.mult))
            seq.step(nc.vector.tensor_tensor(newt[:], newt[:], var_eps[:], ALU.mult))
            seq.step(nc.vector.tensor_scalar(newt[:], newt[:], -0.5, 1.5, ALU.mult, ALU.add))
            seq.step(nc.vector.tensor_tensor(rstd[:], rstd[:], newt[:], ALU.mult))
            for t in range(NT):
                nc.vector.tensor_scalar(xn[:, t, :], x[:, t, :], mv[:, t, 0:1], rstd[:, t:t + 1],
                                        ALU.subtract, ALU.mult).then_inc(sem("xn_ready"), 1)

        def ln_scalar(act, k):
            act.wait_ge(sem("var_ready"), k + 1)
            nc.scalar.activation(std[:], var_eps[:], ACT.Sqrt).then_inc(sem("std_ready"), 1)
            if k != 5:
                evacuate_T(act, xnT, sem("xnT_blocks"), sem("xnT_ready"), turned(k))

        def turned(k):
            return k if k < 5 else k - 1

        def evacuate_T(act, dst, blocks, ready, k):
            for half in range(2):
                for c in range(DC):
                    act.wait_ge(blocks, 4 * k + 2 * half + c + 1)
                    nc.scalar.copy(dst[:, c, half * 512:(half + 1) * 512], bank[2 * half + c][:]).then_inc(ready, 1)

        def transpose_T(pe, src, blocks):
            for half in range(2):
                for c in range(DC):
                    for t in range(4):
                        last = nc.tensor.transpose(bank[2 * half + c][:, t * P:(t + 1) * P],
                                                   src[:, half * 4 + t, c * P:(c + 1) * P], ident[:])
                    last.then_inc(blocks, 1)

        def ln_tensor(pe, k):
            pe.wait_ge(sem("xn_ready"), NT * (k + 1))
            transpose_T(pe, xn, sem("xnT_blocks"))

        H0, HD0, L = 16, 8, D
        r = Region(arena, ARENA)
        toep = r.f32(H0, L)
        cTr = r.f32(DC, T)
        flip = r.f32(P)
        KVS = 4
        kv = r.f32(KVS, DC, NT * HD0 * HD0)
        prod = r.f32(2, DC, NT * HD0 * HD0)
        z = r.f32(DC, T)
        kpad = sb("kpad", [H0, P + L])
        dcol = sb("dcol", [H0, 1])
        kpad_dram = nc.dram_tensor("kpad_dram", [H0, P + L], F32)

        def l0x_sync(sp):
            sp.dma_start(ctok[:], A["ctx"].rearrange("b s d -> s b d")).then_inc(sem("ctx_loaded"), 16)
            sp.dma_start(x[:], A["x"].rearrange("b s d -> s b d")).then_inc(sem("x_loaded"), 16)
            sp.wait_ge(sem("kpad_ready"), 2)
            sp.dma_start(kpad_dram[:], kpad[:]).then_inc(sem("kpad_stored"), 16)
            sp.wait_ge(sem("kpad_stored"), 16)
            sp.dma_start(toep, bass.AP(tensor=kpad_dram[:].tensor, offset=1,
                                       ap=[[1, P], [P + L, H0], [1, L]])).then_inc(sem("toep_loaded"), 16)

        def l0x_scalar(act):
            act.dma_start(gates[:, 0:4], A["g_xattn"].rearrange("(o n) -> o n", o=1).to_broadcast([P, 4])).then_inc(sem("gates_loaded"), 16)
            act.dma_start(gates[:, 4:8], A["g_ffn"].rearrange("(o n) -> o n", o=1).to_broadcast([P, 4])).then_inc(sem("gates_loaded"), 16)
            act.wait_ge(sem("gates_loaded"), 32)
            nc.scalar.activation(tg[:], gates[:], ACT.Tanh).then_inc(sem("tg_ready"), 1)
            evacuate_T(act, cT, sem("cT_blocks"), sem("cT_ready"), 0)
            for half in range(2):
                for c in range(DC):
                    act.wait_ge(sem("cTr_blocks"), 2 * half + c + 1)
                    nc.scalar.copy(cTr[:, c, half * 512:(half + 1) * 512], bank[4 + 2 * half + c]).then_inc(sem("cTr_ready"), 1)
            ln_scalar(act, 0)

        def l0x_gpsimd(pool):
            nc.gpsimd.memset(ident[:], 0.0).then_inc(sem("pool_consts"), 1)
            nc.gpsimd.memset(identb[:], 0.0).then_inc(sem("pool_consts"), 1)
            nc.gpsimd.memset(onesb[:], 1.0).then_inc(sem("pool_consts"), 1)
            nc.gpsimd.memset(kpad[:, :], 0.0).then_inc(sem("pool_consts"), 1)
            nc.gpsimd.memset(flip, 0.0).then_inc(sem("pool_consts"), 1)
            pool.wait_ge(sem("pool_consts"), 5)
            nc.gpsimd.affine_select(out=ident[:], in_=ident[:], compare_op=ALU.not_equal, fill=1.0, base=0,
                                    pattern=[[-1, P]], channel_multiplier=1).then_inc(sem("ident_ready"), 1)
            nc.gpsimd.affine_select(out=identb[:], in_=identb[:], compare_op=ALU.not_equal, fill=1.0, base=0,
                                    pattern=[[-1, P]], channel_multiplier=1).then_inc(sem("ident_ready"), 1)
            nc.gpsimd.affine_select(out=flip, in_=flip, compare_op=ALU.not_equal, fill=1.0, base=-(P - 1),
                                    pattern=[[1, P]], channel_multiplier=1).then_inc(sem("ident_ready"), 1)
            pool.dma_start(kpad[:, P:P + L], A["ssm"]).then_inc(sem("ssm_loaded"), 16)
            pool.dma_start(dcol[:], A["ssm_d"]).then_inc(sem("ssm_loaded"), 16)
            pool.wait_ge(sem("ssm_loaded"), 32)
            nc.gpsimd.tensor_tensor(kpad[:, P:P + 1], kpad[:, P:P + 1], dcol[:], ALU.add).then_inc(sem("kpad_ready"), 2)
            pool.wait_ge(sem("cTr_ready"), 4)
            for h in range(H0):
                if h >= KVS:
                    pool.wait_ge(sem("conv_done"), h - KVS + 1)
                for c in range(DC):
                    rows = cTr[:, c, :].rearrange("p (b s) -> p b s", b=NT)[:, :, h * HD0:(h + 1) * HD0]
                    nc.gpsimd.tensor_tensor(kv[:, h % KVS, c, :].rearrange("p (b j i) -> p b j i", b=NT, j=HD0),
                                            bcast(rows, 3, HD0), bcast(rows, 2, HD0),
                                            ALU.mult).then_inc(sem("kv_ready"), 1)

        def l0x_tensor(pe):
            pe.wait_ge(sem("ident_ready"), 3)
            pe.wait_ge(sem("ctx_loaded"), 16)
            transpose_T(pe, ctok, sem("cT_blocks"))
            pe.wait_ge(sem("cT_ready"), 4)
            for half in range(2):
                for c in range(DC):
                    nc.tensor.matmul(bank[4 + 2 * half + c], flip, cT[:, c, half * 512:(half + 1) * 512], start=True,
                                     stop=True).then_inc(sem("cTr_blocks"), 1)
            ln_tensor(pe, 0)
            pe.wait_ge(sem("xnT_ready"), 4)
            pe.wait_ge(sem("toep_loaded"), 16)
            pe.wait_ge(sem("cTr_ready"), 4)
            for h in range(H0):
                s = h % 2
                pe.wait_ge(sem("kv_ready"), DC * (h + 1))
                if h >= 2:
                    pe.wait_ge(sem("prod_ready"), DC * (h - 1))
                nc.tensor.matmul(bank[2 * s][:], toep[:, h, 0:P], kv[:, h % KVS, 0, :], start=True, stop=True)
                nc.tensor.matmul(bank[2 * s + 1][:], toep[:, h, P:L], kv[:, h % KVS, 0, :], start=True, stop=False)
                nc.tensor.matmul(bank[2 * s + 1][:], toep[:, h, 0:P], kv[:, h % KVS, 1, :], start=False,
                                 stop=True).then_inc(sem("conv_done"), 1)
            pe.wait_ge(sem("z_ready"), H0)
            for t in range(NT):
                for c in range(DC):
                    last = nc.tensor.transpose(bank[4 + t // 2][:, (t % 2 * DC + c) * P:(t % 2 * DC + c + 1) * P],
                                               z[:, c, t * P:(t + 1) * P], ident[:])
                last.then_inc(sem("conv_out"), 1)

        def l0x_vector(dve, seq):
            ln_vector(dve, seq, 0)
            dve.wait_ge(sem("xnT_ready"), 4)
            for h in range(H0):
                s = h % 2
                dve.wait_ge(sem("conv_done"), h + 1)
                if h >= 2:
                    dve.wait_ge(sem("z_ready"), h - 1)
                for c in range(DC):
                    q = xnT[:, c, :].rearrange("p (b s) -> p b s", b=NT)[:, :, h * HD0:(h + 1) * HD0]
                    nc.vector.tensor_tensor(prod[:, s, c, :].rearrange("p (b j i) -> p b j i", b=NT, j=HD0),
                                            bank[2 * s + c][:].rearrange("p (b j i) -> p b j i", b=NT, j=HD0),
                                            bcast(q, 2, HD0), ALU.mult).then_inc(sem("prod_ready"), 1)
                dve.wait_ge(sem("prod_ready"), DC * (h + 1))
                nc.vector.tensor_reduce(
                    z.rearrange("p c (b s) -> p (c b) s", b=NT)[:, :, h * HD0:(h + 1) * HD0],
                    prod[:, s].rearrange("p c (b j i) -> p (c b) j i", b=NT, j=HD0),
                    AX.X, ALU.add).then_inc(sem("z_ready"), 1)
            dve.wait_ge(sem("tg_ready"), 1)
            for t in range(0, NT, 2):
                dve.wait_ge(sem("conv_out"), t + 2)
                seq.mark(nc.vector.scalar_tensor_tensor(x[:, t:t + 2, :].rearrange("p a d -> p (a d)"),
                                                        bank[4 + t // 2][:], tg[:, 0:1],
                                                        x[:, t:t + 2, :].rearrange("p a d -> p (a d)"),
                                                        ALU.mult, ALU.add))
            seq.wait()

        class Moe:

            BIG = 8192.0

            def __init__(self, name, E, K, C, gate, rows_buf, r, stores, earlier=None):
                self.name, self.E, self.K, self.C, self.gate = name, E, K, C, gate
                self.slots = E * C
                self.y_done = 16 * stores
                self.before = earlier.totals() if earlier else {}
                self.blocks = self.slots // P
                assert self.slots % P == 0
                self.x_dram = nc.dram_tensor(f"{name}_x_dram", [self.slots + K * T, D], F32)
                self.y_dram = nc.dram_tensor(f"{name}_y_dram", [self.slots, D], F32)
                self.rows = rows_buf
                self.rowsT = r.f32(DC, self.slots)
                self.weight = r.f32(NT, E)
                self.sel = r.f32(NT, E)
                self.selb = r.bf16(NT, E)
                self.keep = r.f32(NT, E)
                self.code = r.f32(NT, E)
                self.wkeep = r.f32(NT, E)
                self.code8 = r.f32(NT, 8)
                self.kcode = r.f32(NT, K)
                self.kept = r.f32(NT, K)
                self.slot = r.f32(NT, K)
                self.idx_f = r.f32(NT, K)
                self.match = r.f32(NT, K, E)
                self.kweight = r.f32(NT, K)
                self.gathered = r.f32(8, D)
                self.code_base = sb(f"{name}_code_base", [P, E])
                self.spare = sb(f"{name}_spare", [P, NT, K])
                self.idx_to = sb(f"{name}_idx_to", [P, NT, K], I32)
                self.idx_from = sb(f"{name}_idx_from", [P, NT, K], I32)

            def sem(self, what):
                return sem(f"moe_{what}")

            def wait(self, eng, what, n):
                eng.wait_ge(self.sem(what), n + self.before.get(what, 0))

            def totals(self):
                groups = (self.blocks + 3) // 4 * DC
                return dict(consts=2, sel_ready=1, pos_ready=1, idx_ready=2, cleared=16, scattered=16 * NT * self.K,
                            rows_loaded=16, rowsT_blocks=groups, rowsT_ready=groups, y_stored=self.y_done, added=NT * self.K,
                            gathered=16 * (NT * self.K // 8))

            def clear_rows(self, sp):
                sp.wait_ge(sem("zeros_ready"), 1)
                sp.dma_start(self.x_dram[0:self.slots, :].rearrange("(g p) d -> p g d", p=P),
                             bcast(zeros[:], 1, self.blocks)).then_inc(self.sem("cleared"), 16)

            def constants(self, pool):
                nc.gpsimd.iota(self.code_base[:], pattern=[[-self.C, self.E]], base=int(self.BIG), channel_multiplier=0,
                               allow_small_or_imprecise_dtypes=True).then_inc(self.sem("consts"), 1)
                nc.gpsimd.iota(self.spare[:], pattern=[[P, NT], [T, self.K]], base=self.slots, channel_multiplier=1,
                               allow_small_or_imprecise_dtypes=True).then_inc(self.sem("consts"), 1)

            def positions_tensor(self, pe, ps):
                E = self.E
                self.wait(pe, "sel_ready", 1)
                pe.wait_ge(sem("before_ready"), 1)
                nc.tensor.matmul(ps[:, 0:NT * E], before[:], self.selb.rearrange("p t e -> p (t e)"),
                                 start=True, stop=False, skip_group_check=True)
                for j in range(NT - 1):
                    last = nc.tensor.matmul(ps[:, (j + 1) * E:NT * E], onesb[:], bcast(self.selb[:, j, :], 1, NT - 1 - j),
                                            start=False, stop=(j == NT - 2), skip_group_check=True)
                last.then_inc(self.sem("pos_ready"), 1)

            def slots_vector(self, dve, seq, ps):
                E, K = self.E, self.K
                pos = ps[:, 0:NT * E].rearrange("p (t e) -> p t e", t=NT)
                self.wait(dve, "pos_ready", 1)
                self.wait(dve, "consts", 2)
                seq.mark(nc.vector.scalar_tensor_tensor(self.keep, pos, float(self.C), self.sel, ALU.is_lt, ALU.mult))
                seq.step(nc.vector.scalar_tensor_tensor(self.code, pos, -1.0, bcast(self.code_base[:], 1, NT), ALU.mult, ALU.add))
                seq.mark(nc.vector.tensor_tensor(self.code, self.code, self.keep, ALU.mult))
                seq.step(nc.vector.tensor_tensor(self.wkeep, self.weight, self.keep, ALU.mult))
                for t in range(NT):
                    seq.mark(nc.vector.max(self.code8[:, t, :], self.code[:, t, :]))
                seq.wait()
                seq.step(nc.vector.tensor_copy(self.kcode, self.code8[:, :, 0:K]))
                seq.mark(nc.vector.tensor_scalar(self.kept, self.kcode, 0.0, None, ALU.is_gt))
                seq.step(nc.vector.tensor_scalar(self.slot, self.kcode, -1.0, self.BIG, ALU.mult, ALU.add))
                seq.step(nc.vector.tensor_tensor(self.idx_f, self.slot, self.spare[:], ALU.subtract))
                seq.step(nc.vector.tensor_tensor(self.idx_f, self.idx_f, self.kept, ALU.mult))
                nc.vector.tensor_tensor(self.idx_to[:], self.idx_f, self.spare[:], ALU.add).then_inc(self.sem("idx_ready"), 1)
                nc.vector.tensor_tensor(self.idx_from[:], self.slot, self.kept, ALU.mult).then_inc(self.sem("idx_ready"), 1)
                seq.step(nc.vector.tensor_tensor(self.match, bcast(self.code, 2, K), bcast(self.kcode, 3, E), ALU.is_equal))
                seq.step(nc.vector.tensor_tensor(self.match, self.match, bcast(self.wkeep, 2, K), ALU.mult))
                seq.step(nc.vector.tensor_reduce(self.kweight, self.match, AX.X, ALU.add))
                seq.step(nc.vector.tensor_scalar(self.kweight, self.kweight, tg[:, self.gate:self.gate + 1], None, ALU.mult))

            def scatter_gpsimd(self, pool):
                self.wait(pool, "idx_ready", 2)
                self.wait(pool, "cleared", 16)
                for t in range(NT):
                    for k in range(self.K):
                        nc.gpsimd.indirect_dma_start(
                            out=self.x_dram[:, :], out_offset=bass.IndirectOffsetOnAxis(ap=self.idx_to[:, t, k:k + 1], axis=0),
                            in_=xn[:, t, :], in_offset=None).then_inc(self.sem("scattered"), 16)

            def load_rows_sync(self, sp):
                self.wait(sp, "scattered", 16 * NT * self.K)
                sp.dma_start(self.rows, self.x_dram[0:self.slots, :].rearrange("(g p) d -> p g d", p=P))\
                  .then_inc(self.sem("rows_loaded"), 16)

            def rows_tensor(self, pe):
                self.wait(pe, "rows_loaded", 16)
                n = 0
                for g0 in range(0, self.blocks, 4):
                    for c in range(DC):
                        if n >= 2:
                            self.wait(pe, "rowsT_ready", n - 1)
                        for g in range(g0, min(g0 + 4, self.blocks)):
                            last = nc.tensor.transpose(bank[2 + n % 2][:, (g - g0) * P:(g - g0 + 1) * P],
                                                       self.rows[:, g, c * P:(c + 1) * P], ident[:])
                        last.then_inc(self.sem("rowsT_blocks"), 1)
                        n += 1
                self.wait(pe, "rowsT_ready", n)

            def rows_scalar(self, act):
                n = 0
                for g0 in range(0, self.blocks, 4):
                    for c in range(DC):
                        self.wait(act, "rowsT_blocks", n + 1)
                        w = min(4, self.blocks - g0) * P
                        nc.scalar.copy(self.rowsT[:, c, g0 * P:g0 * P + w], bank[2 + n % 2][:, 0:w]).then_inc(self.sem("rowsT_ready"), 1)
                        n += 1

            def gather_gpsimd(self, pool):
                if self.y_done:
                    self.wait(pool, "y_stored", self.y_done)
                n = 0
                for t in range(NT):
                    for k in range(self.K):
                        if n >= 8:
                            self.wait(pool, "added", n - 7)
                        nc.gpsimd.indirect_dma_start(
                            out=self.gathered[:, n % 8, :], out_offset=None, in_=self.y_dram[:, :],
                            in_offset=bass.IndirectOffsetOnAxis(ap=self.idx_from[:, t, k:k + 1], axis=0))\
                            .then_inc(sem(f"gathered{n % 8}"), 16)
                        n += 1

            def combine_vector(self, dve):
                n = 0
                for t in range(NT):
                    for k in range(self.K):
                        dve.wait_ge(sem(f"gathered{n % 8}"), 16 * (n // 8 + 1) + self.before.get("gathered", 0))
                        if k:
                            self.wait(dve, "added", n)
                        nc.vector.scalar_tensor_tensor(x[:, t, :], self.gathered[:, n % 8, :], self.kweight[:, t, k:k + 1],
                                                       x[:, t, :], ALU.mult, ALU.add).then_inc(self.sem("added"), 1)
                        n += 1
                self.wait(dve, "added", n)

        class Dense:

            def __init__(self, name, n, gate, w, loaded, hid, scratch, scale=None, earlier=0):
                self.name, self.n, self.gate, self.w, self.loaded = name, n, gate, w, loaded
                self.hid, self.scratch, self.scale, self.earlier = hid, scratch, scale, earlier

            def sem(self, what):
                return sem(f"dense_{what}")

            def wait(self, eng, what, n):
                per_chunk = 4 if what in ("down_done", "x_added") else 2
                eng.wait_ge(self.sem(what), n + per_chunk * self.earlier)

            def up_tensor(self, pe, m):
                w = self.w(m)
                self.loaded(pe, m)
                for half in range(2):
                    u = 2 * m + half
                    if u >= 2:
                        self.wait(pe, "h_ready", u - 1)
                    for j in range(2):
                        for c in range(DC):
                            last = nc.tensor.matmul(bank[2 * half + j][:], w[:, (j * DC + c) * P:(j * DC + c + 1) * P],
                                                    xnT[:, c, half * 512:(half + 1) * 512], start=(c == 0), stop=(c == DC - 1))
                    last.then_inc(self.sem("up_done"), 1)

            def down_tensor(self, pe, m):
                w = self.w(m)
                for half in range(2):
                    self.wait(pe, "h_ready", 2 * m + half + 1)
                    for t2 in range(2):
                        v = 4 * m + 2 * half + t2
                        if v >= 4:
                            self.wait(pe, "x_added", v - 3)
                        for i in range(2):
                            t = half * 4 + t2 * 2 + i
                            last = nc.tensor.matmul(bank[4 + v % 4][:, i * D:(i + 1) * D], self.hid[:, m % 2, t * P:(t + 1) * P],
                                                    w[:, 2 * DC * P:2 * DC * P + D], start=True, stop=True)
                        last.then_inc(self.sem("down_done"), 1)

            def tensor(self, pe):
                for m in range(self.n + 1):
                    if m < self.n:
                        self.up_tensor(pe, m)
                    if m:
                        self.down_tensor(pe, m - 1)

            def scalar(self, act):
                for m in range(self.n):
                    for half in range(2):
                        u = 2 * m + half
                        self.wait(act, "up_done", u + 1)
                        if u >= 2:
                            self.wait(act, "h_ready", u - 1)
                        nc.scalar.activation(self.scratch[:, half, :], bank[2 * half][:], ACT.Silu).then_inc(self.sem("silu_done"), 1)

            def vector(self, dve, seq):
                def up(m):
                    for half in range(2):
                        u = 2 * m + half
                        self.wait(dve, "silu_done", u + 1)
                        if m >= 2:
                            self.wait(dve, "down_done", 4 * (m - 2) + 2 * half + 2)
                        nc.vector.tensor_tensor(self.hid[:, m % 2, half * 512:(half + 1) * 512], self.scratch[:, half, :],
                                                bank[2 * half + 1][:], ALU.mult).then_inc(self.sem("h_ready"), 1)

                def down(m):
                    for v in range(4 * m, 4 * m + 4):
                        t = 2 * (v % 4)
                        self.wait(dve, "down_done", v + 1)
                        if v >= 4:
                            self.wait(dve, "x_added", v - 3)
                        if self.scale is None:
                            nc.vector.scalar_tensor_tensor(x[:, t:t + 2, :].rearrange("p a d -> p (a d)"), bank[4 + v % 4][:],
                                                           tg[:, self.gate:self.gate + 1],
                                                           x[:, t:t + 2, :].rearrange("p a d -> p (a d)"),
                                                           ALU.mult, ALU.add).then_inc(self.sem("x_added"), 1)
                        else:
                            for i in range(2):
                                ins = nc.vector.scalar_tensor_tensor(x[:, t + i, :], bank[4 + v % 4][:, i * D:(i + 1) * D],
                                                                     self.scale(m, t + i), x[:, t + i, :], ALU.mult, ALU.add)
                                if i == 0:
                                    seq.mark(ins)
                            seq.wait()
                            ins.then_inc(self.sem("x_added"), 1)

                for m in range(self.n + 1):
                    if m < self.n:
                        up(m)
                    if m:
                        down(m - 1)
                self.wait(dve, "x_added", 4 * self.n)

        zeros = sb("zeros", [P, D])
        before = sb("before", [P, P], BF16)
        rw0 = sb("rw0", [P, DC, 32])
        ebias = sb("ebias", [P, 32])
        SH0 = sb("sh0", [P, 2, 768])
        E0, K0, C0, NG0, TOPG = 32, 4, 40, 8, 3
        GE = E0 // NG0
        r = Region(arena, ARENA)
        moe0 = Moe("moe0", E0, K0, C0, 4, r.f32(E0 * C0 // P, D), r, 4)
        scores0 = r.f32(NT, E0)
        biased = r.f32(NT, E0)
        gtmp = [r.f32(NT * NG0) for _ in range(8)]
        NONE, TAKEN = -3.0e38, 3.0e38
        gval = r.f32(NT, 2 * NG0)
        gtop = r.f32(NT, 8)
        grep = r.f32(NT, 2 * NG0)
        gmask = r.f32(NT, NG0)
        mval = r.f32(NT, E0 + 8)
        mtop = r.f32(NT, 8)
        mrep = r.f32(NT, E0 + 8)
        wsum = r.f32(NT)
        sh_hid = r.f32(2, T)
        sh_scr = r.f32(2, 512)
        exp_s = r.f32(2, C0)
        exp_h = r.f32(2, C0)
        y0 = r.f32(E0, D)
        RING0 = 8
        w0 = wring[:, 0:RING0 * 768].rearrange("p (s n) -> p s n", s=RING0)

        def dense_small_loaded(pe, m):
            pe.wait_ge(sem("l0f_small_loaded"), 16 * 3)

        shared0 = Dense("shared0", 2, 4, lambda m: SH0[:, m, :], dense_small_loaded, sh_hid, sh_scr)

        def l0f_sync(sp):
            sp.dma_start(rw0[:], A["l0_router"].rearrange("(c p) e -> p c e", p=P)).then_inc(sem("l0f_small_loaded"), 16)
            sp.dma_start(ebias[:], A["l0_ebias"].rearrange("(o n) -> o n", o=1).to_broadcast([P, E0])).then_inc(sem("l0f_small_loaded"), 16)
            sp.dma_start(SH0[:], A["l0_shared"].rearrange("m p n -> p m n")).then_inc(sem("l0f_small_loaded"), 16)
            moe0.clear_rows(sp)
            for s in range(RING0):
                sp.dma_start(w0[:, s, :], A["l0_experts"][s]).then_inc(sem(f"ring_loaded{s}"), 16)

        def l0f_sync2(sp):
            moe0.load_rows_sync(sp)
            with sp.Fori(1, E0 // RING0) as it:
                for s in range(RING0):
                    sp.wait_ge(sem("w0_used"), (it - 1) * RING0 + s + 1)
                    sp.dma_start(w0[:, s, :], A["l0_experts"][bass.ds(it * RING0 + s, 1)].rearrange("o p n -> p (o n)"))\
                      .then_inc(sem(f"ring_loaded{s}"), 16)

        def l0f_gpsimd(pool):
            nc.gpsimd.memset(zeros[:], 0.0).then_inc(sem("zeros_ready"), 1)
            nc.gpsimd.affine_select(out=before[:], in_=onesb[:], compare_op=ALU.is_ge, fill=0.0, base=-1,
                                    pattern=[[1, P]], channel_multiplier=-1).then_inc(sem("before_ready"), 1)
            moe0.constants(pool)

        def l0f_gpsimd2(pool):
            moe0.scatter_gpsimd(pool)
            moe0.gather_gpsimd(pool)

        def l0f_tensor(pe):
            ln_tensor(pe, 1)
            pe.wait_ge(sem("xnT_ready"), 8)
            pe.wait_ge(sem("l0f_small_loaded"), 48)
            for t in range(NT):
                for c in range(DC):
                    last = nc.tensor.matmul(bank[4][:, t * E0:(t + 1) * E0], xnT[:, c, t * P:(t + 1) * P], rw0[:, c, :],
                                            start=(c == 0), stop=(c == DC - 1))
            last.then_inc(sem("router0_done"), 1)
            moe0.positions_tensor(pe, bank[5])
            moe0.wait(pe, "idx_ready", 2)
            shared0.tensor(pe)
            moe0.rows_tensor(pe)
            with pe.Fori(0, E0 // RING0) as it:
                def up(s):
                    e = it * RING0 + s
                    pe.wait_ge(sem(f"ring_loaded{s}"), (it + 1) * 16)
                    if s >= 2:
                        pe.wait_ge(sem("h0_ready"), e - 1)
                    for j in range(2):
                        for c in range(DC):
                            last = nc.tensor.matmul(bank[s % 2][:, j * 64:j * 64 + C0], w0[:, s, (j * DC + c) * P:(j * DC + c + 1) * P],
                                                    moe0.rowsT[:, c, bass.ds(e * C0, C0)], start=(c == 0), stop=(c == DC - 1))
                    last.then_inc(sem("up0_done"), 1)

                def down(s):
                    e = it * RING0 + s
                    pe.wait_ge(sem("h0_ready"), e + 1)
                    if s >= 2:
                        pe.wait_ge(sem("y0_ready"), e - 1)
                    nc.tensor.matmul(bank[2 + s % 2][0:C0, 0:D], exp_h[:, s % 2, :], w0[:, s, 2 * DC * P:2 * DC * P + D],
                                     start=True, stop=True).then_inc(sem("w0_used"), 1)

                for s in range(RING0 + 1):
                    if s < RING0:
                        up(s)
                    if s:
                        down(s - 1)
                pe.wait_ge(sem("y0_ready"), it * RING0 + RING0)

        def l0f_scalar(act):
            ln_scalar(act, 1)
            act.wait_ge(sem("router0_done"), 1)
            nc.scalar.activation(scores0.rearrange("p t e -> p (t e)"), bank[4][:, 0:NT * E0], ACT.Sigmoid).then_inc(sem("scores0_ready"), 1)
            shared0.scalar(act)
            moe0.rows_scalar(act)
            with act.Fori(0, E0 // RING0) as it:
                for s in range(RING0 + 1):
                    e = it * RING0 + s
                    if s < RING0:
                        act.wait_ge(sem("up0_done"), e + 1)
                        if s >= 2:
                            act.wait_ge(sem("h0_ready"), e - 1)
                        nc.scalar.activation(exp_s[:, s % 2, :], bank[s % 2][:, 0:C0], ACT.Silu).then_inc(sem("silu0_done"), 1)
                    if s:
                        act.wait_ge(sem("w0_used"), e)
                        nc.scalar.copy(y0[0:C0, bass.ds(e - 1, 1), :].rearrange("p o d -> p (o d)"), bank[2 + (s - 1) % 2][0:C0, 0:D])\
                          .then_inc(sem("y0_ready"), 1)
                act.wait_ge(sem("y0_ready"), it * RING0 + RING0)
                act.dma_start(moe0.y_dram[bass.ds(it * RING0 * C0, RING0 * C0), :].rearrange("(e c) d -> c e d", c=C0),
                              y0[0:C0, bass.ds(it * RING0, RING0), :]).then_inc(moe0.sem("y_stored"), 16)

        def l0f_vector(dve, seq):
            ln_vector(dve, seq, 1)
            dve.wait_ge(sem("scores0_ready"), 1)
            dve.wait_ge(sem("l0f_small_loaded"), 48)
            seq.mark(nc.vector.memset(gval[:, :, NG0:2 * NG0], NONE))
            seq.mark(nc.vector.memset(mval[:, :, E0:E0 + 8], NONE))
            seq.step(nc.vector.tensor_tensor(biased, scores0, bcast(ebias[:], 1, NT), ALU.add))
            m = biased.rearrange("p t (g m) -> p (t g) m", m=GE)
            hi1, lo1, hi2, lo2, top, mid, low, second = gtmp
            seq.mark(nc.vector.tensor_tensor(hi1, m[:, :, 0], m[:, :, 1], ALU.max))
            seq.mark(nc.vector.tensor_tensor(lo1, m[:, :, 0], m[:, :, 1], ALU.min))
            seq.mark(nc.vector.tensor_tensor(hi2, m[:, :, 2], m[:, :, 3], ALU.max))
            seq.step(nc.vector.tensor_tensor(lo2, m[:, :, 2], m[:, :, 3], ALU.min))
            seq.mark(nc.vector.tensor_tensor(top, hi1, hi2, ALU.max))
            seq.mark(nc.vector.tensor_tensor(mid, hi1, hi2, ALU.min))
            seq.step(nc.vector.tensor_tensor(low, lo1, lo2, ALU.max))
            seq.step(nc.vector.tensor_tensor(second, mid, low, ALU.max))
            seq.step(nc.vector.tensor_tensor(gval[:, :, 0:NG0], top.rearrange("p (t g) -> p t g", t=NT),
                                             second.rearrange("p (t g) -> p t g", t=NT), ALU.add))
            top_mask(seq, gval, gtop, grep, NG0, TOPG, gmask)
            seq.step(nc.vector.tensor_tensor(mval[:, :, 0:E0].rearrange("p t (g m) -> p t g m", m=GE),
                                             biased.rearrange("p t (g m) -> p t g m", m=GE), bcast(gmask, 3, GE), ALU.mult))
            seq.step(nc.vector.tensor_scalar(mval[:, :, 0:E0], mval[:, :, 0:E0], 0.0, None, ALU.add))
            top_mask(seq, mval, mtop, mrep, E0, K0, moe0.sel)
            nc.vector.tensor_copy(moe0.selb, moe0.sel).then_inc(moe0.sem("sel_ready"), 1)
            seq.step(nc.vector.tensor_tensor(moe0.weight, moe0.sel, scores0, ALU.mult))
            seq.step(nc.vector.tensor_reduce(wsum, moe0.weight, AX.X, ALU.add))
            seq.step(nc.vector.tensor_scalar(wsum, wsum, 1e-20, None, ALU.add))
            seq.step(nc.vector.reciprocal(wsum, wsum))
            seq.step(nc.vector.scalar_tensor_tensor(moe0.weight, moe0.weight, 2.5, bcast(wsum, 2, E0), ALU.mult, ALU.mult))
            moe0.slots_vector(dve, seq, bank[5])
            shared0.vector(dve, seq)
            with dve.Fori(0, E0 // RING0) as it:
                for s in range(RING0):
                    e = it * RING0 + s
                    dve.wait_ge(sem("silu0_done"), e + 1)
                    if s >= 2:
                        dve.wait_ge(sem("w0_used"), e - 1)
                    nc.vector.tensor_tensor(exp_h[:, s % 2, :], exp_s[:, s % 2, :], bank[s % 2][:, 64:64 + C0], ALU.mult)\
                      .then_inc(sem("h0_ready"), 1)
            moe0.combine_vector(dve)

        def top_mask(seq, val, top8, rep, n, k, mask):
            for t in range(NT):
                seq.mark(nc.vector.max(top8[:, t, :], val[:, t, 0:n]))
            seq.wait()
            seq.step(nc.vector.memset(top8[:, :, k:8], NONE))
            for t in range(NT):
                seq.mark(nc.vector.match_replace(rep[:, t, :], top8[:, t, :], val[:, t, :], TAKEN))
            seq.wait()
            seq.step(nc.vector.tensor_scalar(mask, rep[:, :, 0:n], TAKEN, None, ALU.is_equal))

        H2, HD2 = 16, 16
        ROWS = 64
        LN255 = 5.541263545158426
        wq2 = sb("wq2", [P, DC, D])
        wkv2 = sb("wkv2", [P, DC, 2 * D])
        wp2 = sb("wp2", [P, DC, D])
        bqk2 = sb("bqk2", [P, 2, D])
        bv2 = sb("bv2", [P, DC])
        bp2 = sb("bp2", [1, D])
        ones_row = sb("ones_row", [1, P])
        r = Region(arena, ARENA)
        qT2 = r.bf16(H2 // 2, T)
        kT2 = r.bf16(H2 // 2, T)
        v2 = r.bf16(NT, D)
        vT2 = r.f32(DC, T)
        sv2 = r.f32(DC)
        isv2 = r.f32(DC)
        am2 = r.f32(2, NT * H2)
        s2 = r.f32(2, NT * H2)
        is2 = r.f32(2, NT * H2)
        zs2 = r.f32(H2, NT)
        rz2 = r.f32(H2, NT)
        nmax2 = r.f32(H2 * NT)
        bias2 = r.f32(H2 * NT)
        overlay = r.at
        qf2 = r.f32(NT, D)
        kf2 = r.f32(NT, D)
        tmp2 = xn[:]
        qa2 = r.bf16(NT, H2, ROWS)
        ka2 = r.bf16(NT, H2, ROWS)
        r = Region(arena, ARENA)
        r.at = overlay
        vi2 = r.bf16(DC, T)
        SLOTS2 = 3
        e2 = r.f32(SLOTS2, T)
        r2 = r.bf16(SLOTS2, T)
        rT2 = r.bf16(SLOTS2, T)
        o2 = r.f32(NT, D)
        oT2 = r.f32(DC, T)

        def bf(i):
            return bank[i].bitcast(BF16)

        GH2 = 512 // (NT * HD2)

        def l1x_sync(sp):
            for dst, src in ((wq2[:], A["l1_wq"].rearrange("(c p) n -> p c n", p=P)),
                             (wkv2[:], A["l1_wkv"].rearrange("(c p) n -> p c n", p=P)),
                             (wp2[:], A["l1_wp"].rearrange("(c p) n -> p c n", p=P)),
                             (bqk2[:, 0, :], A["l1_bq"].rearrange("(o n) -> o n", o=1).to_broadcast([P, D])),
                             (bqk2[:, 1, :], A["l1_bkv"][0:D].rearrange("(o n) -> o n", o=1).to_broadcast([P, D])),
                             (bv2[:], A["l1_bv"]),
                             (bp2[:], A["l1_bp"].rearrange("(o n) -> o n", o=1))):
                sp.dma_start(dst, src).then_inc(sem("l1x_loaded"), 16)

        L1X_LOADS = 16 * 7

        def l1x_gpsimd(pool):
            nc.gpsimd.memset(ones_row[:], 1.0).then_inc(sem("ones_row_ready"), 1)

        def l1x_tensor(pe):
            ln_tensor(pe, 2)
            pe.wait_ge(sem("xnT_ready"), 12)
            pe.wait_ge(sem("l1x_loaded"), L1X_LOADS)
            for j, (src, w) in enumerate(((xnT, wq2[:, :, :]), (cT, wkv2[:, :, 0:D]))):
                for t in range(NT):
                    for c in range(DC):
                        last = nc.tensor.matmul(bank[4 * j + t // 2][:, t % 2 * D:(t % 2 + 1) * D], src[:, c, t * P:(t + 1) * P],
                                                w[:, c, :], start=(c == 0), stop=(c == DC - 1))
                    if t % 2:
                        last.then_inc(sem("qk2_done"), 1)
            pe.wait_ge(sem("qkf2_ready"), 4)
            for f in range(DC):
                for half in range(2):
                    for c in range(DC):
                        last = nc.tensor.matmul(bank[2 * f + half], wkv2[:, c, D + f * P:D + (f + 1) * P],
                                                cT[:, c, half * 512:(half + 1) * 512], start=(c == 0), stop=(c == DC - 1))
                    last.then_inc(sem("v2_done"), 1)
            for n in range(H2):
                src = qa2 if n < H2 // 2 else ka2
                if n == 0:
                    pe.wait_ge(sem("qkf2_ready"), 8)
                if n % (H2 // 2) == 0:
                    pe.wait_ge(sem("qa2_ready"), 3) if n == 0 else pe.wait_ge(sem("ka2_ready"), 4)
                if n >= 4:
                    pe.wait_ge(sem("qkT2_ready"), n - 3)
                for t in range(NT):
                    last = nc.tensor.transpose(bf(4 + n % 4)[:, t * P:(t + 1) * P],
                                               src[:, t, 2 * (n % 8):2 * (n % 8) + 2, :].rearrange("p a b -> p (a b)"), identb[:])
                last.then_inc(sem("qkT2_blocks"), 1)
            pe.wait_ge(sem("vi2_ready"), 1)
            for t in range(NT):
                for c in range(DC):
                    last = nc.tensor.transpose(bf(t // 4)[:, (t % 4 * DC + c) * P:(t % 4 * DC + c + 1) * P],
                                               vi2[:, c, t * P:(t + 1) * P], identb[:])
                if t % 4 == 3:
                    last.then_inc(sem("v2_blocks"), 1)
            pe.wait_ge(sem("v2_ready"), 2)
            pe.wait_ge(sem("qkT2_ready"), H2)

            def scores(n):
                h, t = n // NT, n % NT
                lo = ROWS * (h % 2)
                if n >= 2:
                    pe.wait_ge(sem("e2_ready"), n - 1)
                for half in range(2):
                    last = nc.tensor.matmul(bank[2 * (n % 2) + half], qT2[lo:lo + 3 * HD2, h // 2, t * P:(t + 1) * P],
                                            kT2[lo:lo + 3 * HD2, h // 2, half * 512:(half + 1) * 512], start=True, stop=True)
                last.then_inc(sem("scores2_done"), 1)

            def turn(n):
                pe.wait_ge(sem("r2_ready"), n + 1)
                if n >= SLOTS2:
                    pe.wait_ge(sem("rT2_ready"), n - SLOTS2 + 1)
                for j in range(NT):
                    last = nc.tensor.transpose(bf(4 + n % SLOTS2)[:, j * P:(j + 1) * P], r2[:, n % SLOTS2, j * P:(j + 1) * P], identb[:])
                last.then_inc(sem("rT2_blocks"), 1)

            def values(n):
                h, t = n // NT, n % NT
                pe.wait_ge(sem("rT2_ready"), n + 1)
                if t == 0 and h % GH2 == 0 and h:
                    pe.wait_ge(sem("o2_ready"), h // GH2)
                for j in range(NT):
                    last = nc.tensor.matmul(bank[7][:, (h % GH2 * NT + t) * HD2:(h % GH2 * NT + t + 1) * HD2], rT2[:, n % SLOTS2, j * P:(j + 1) * P],
                                            v2[:, j, h * HD2:(h + 1) * HD2], start=(j == 0), stop=(j == NT - 1))
                last.then_inc(sem("values2_done"), 1)

            U = H2 * NT
            for n in range(U + 4):
                if n < U:
                    scores(n)
                if 2 <= n < U + 2:
                    turn(n - 2)
                if n >= 4:
                    values(n - 4)
            pe.wait_ge(sem("o2_ready"), H2 // GH2)
            pe.wait_ge(sem("ones_row_ready"), 1)
            transpose_T(pe, o2, sem("oT2_blocks"))
            pe.wait_ge(sem("oT2_ready"), 4)
            for t in range(NT):
                ps = bank[4 + t // 2][:, t % 2 * D:(t % 2 + 1) * D]
                nc.tensor.matmul(ps, ones_row[:], bp2[:], start=True, stop=False)
                for c in range(DC):
                    last = nc.tensor.matmul(ps, oT2[:, c, t * P:(t + 1) * P], wp2[:, c, :], start=False, stop=(c == DC - 1))
                if t % 2:
                    last.then_inc(sem("proj2_done"), 1)

        def l1x_scalar(act):
            ln_scalar(act, 2)
            act.wait_ge(sem("l1x_loaded"), L1X_LOADS)
            for f in range(DC):
                for half in range(2):
                    act.wait_ge(sem("v2_done"), 2 * f + half + 1)
                    nc.scalar.activation(vT2[:, f, half * 512:(half + 1) * 512], bank[2 * f + half], ACT.Identity,
                                         bias=bv2[:, f:f + 1]).then_inc(sem("vf2_ready"), 1)
            act.wait_ge(sem("kd2_ready"), 1)
            kd = kf2.rearrange("p t (h d) -> p (t h) d", h=H2)
            ka = ka2.rearrange("p t h r -> p (t h) r")
            nc.scalar.copy(ka[:, :, 0:HD2], kd).then_inc(sem("ka2_high"), 1)
            act.wait_ge(sem("kd2_ready"), 2)
            nc.scalar.copy(ka[:, :, HD2:2 * HD2], tmp2.rearrange("p t (h d) -> p (t h) d", h=H2)).then_inc(sem("ka2_high"), 1)
            for n in range(H2):
                act.wait_ge(sem("qkT2_blocks"), n + 1)
                dst = (qT2 if n < H2 // 2 else kT2)[:, n % 8, :]
                nc.scalar.copy(dst, bf(4 + n % 4)).then_inc(sem("qkT2_ready"), 1)

            def exp(n):
                h, t = n // NT, n % NT
                act.wait_ge(sem("bias2_ready"), n + 1)
                if n >= SLOTS2:
                    act.wait_ge(sem("r2_ready"), n - SLOTS2 + 1)
                nc.scalar.activation(e2[:, n % SLOTS2, :], psum[:, n % 2 * T:(n % 2 + 1) * T], ACT.Exp, bias=bias2[:, n:n + 1],
                                     scale=s2[:, 0, t * H2 + h:t * H2 + h + 1], accum_out=zs2[:, h, t:t + 1]).then_inc(sem("e2_ready"), 1)

            def copy_T(n):
                act.wait_ge(sem("rT2_blocks"), n + 1)
                if n >= SLOTS2:
                    act.wait_ge(sem("values2_done"), n - SLOTS2 + 1)
                nc.scalar.copy(rT2[:, n % SLOTS2, :], bf(4 + n % SLOTS2)).then_inc(sem("rT2_ready"), 1)

            U = H2 * NT
            for n in range(U + 2):
                if n < U:
                    exp(n)
                if n >= 2:
                    copy_T(n - 2)
            for half in range(2):
                for c in range(DC):
                    act.wait_ge(sem("oT2_blocks"), 2 * half + c + 1)
                    nc.scalar.activation(oT2[:, c, half * 512:(half + 1) * 512], bank[2 * half + c], ACT.Copy,
                                         scale=sv2[:, c:c + 1]).then_inc(sem("oT2_ready"), 1)

        def l1x_vector(dve, seq):
            ln_vector(dve, seq, 2)
            dve.wait_ge(sem("l1x_loaded"), L1X_LOADS)
            seq.mark(nc.vector.memset(qa2, 0.0))
            seq.mark(nc.vector.memset(ka2, 0.0))
            for j, dst in enumerate((qf2, kf2)):
                for b in range(4):
                    dve.wait_ge(sem("qk2_done"), 4 * j + b + 1)
                    nc.vector.tensor_tensor(dst[:, 2 * b:2 * b + 2, :], bank[4 * j + b].rearrange("p (a d) -> p a d", a=2),
                                            bcast(bqk2[:, j, :], 1, 2), ALU.add).then_inc(sem("qkf2_ready"), 1)
            dve.wait_ge(sem("qkf2_ready"), 8)
            for j, src in enumerate((qf2, kf2)):
                seq.mark(nc.vector.tensor_reduce(am2[:, j, :], src.rearrange("p t (h d) -> p (t h) d", h=H2), AX.X, ALU.max,
                                                 apply_absolute_value=True))
            seq.wait()
            for j, by in enumerate((HD2 ** -0.5 / 127.0, 1.0 / 127.0)):
                seq.mark(nc.vector.tensor_scalar(s2[:, j, :], am2[:, j, :], by, 1e-8, ALU.mult, ALU.max))
            seq.wait()
            seq.step(nc.vector.reciprocal(is2[:].rearrange("p j n -> p (j n)"), s2[:].rearrange("p j n -> p (j n)")))
            seq.step(nc.vector.tensor_scalar(is2[:, 0, :], is2[:, 0, :], HD2 ** -0.5, None, ALU.mult))

            def integers(j, src):
                v3 = src.rearrange("p t (h d) -> p (t h) d", h=H2)
                flat = src.rearrange("p t d -> p (t d)")
                seq.step(nc.vector.tensor_tensor(v3, v3, bcast(is2[:, j, :], 2, HD2), ALU.mult))
                seq.step(nc.vector.tensor_scalar(flat, flat, 127.0, -127.0, ALU.min, ALU.max))
                seq.step(nc.vector.tensor_scalar(flat, flat, MAGIC, MAGIC, ALU.add, ALU.subtract))

            integers(0, qf2)
            qa = qa2.rearrange("p t h r -> p (t h) r")
            nc.vector.tensor_copy(qa[:, :, 0:3 * HD2].rearrange("p n (a d) -> p n a d", a=3),
                                  bcast(qf2.rearrange("p t (h d) -> p (t h) d", h=H2), 2, 3)).then_inc(sem("qa2_ready"), 3)
            integers(1, kf2)
            k3 = kf2.rearrange("p t (h d) -> p (t h) d", h=H2)
            t3 = tmp2.rearrange("p t (h d) -> p (t h) d", h=H2)
            ka = ka2.rearrange("p t h r -> p (t h) r")
            nc.vector.tensor_tensor(k3, k3, bcast(s2[:, 1, :], 2, HD2), ALU.mult).then_inc(sem("kd2_ready"), 1)
            dve.wait_ge(sem("ka2_high"), 1)
            nc.vector.tensor_tensor(t3, k3, ka[:, :, 0:HD2], ALU.subtract).then_inc(sem("kd2_ready"), 1)
            dve.wait_ge(sem("ka2_high"), 2)
            dve.wait_ge(sem("kd2_ready"), 2)
            nc.vector.tensor_tensor(ka[:, :, 2 * HD2:3 * HD2], t3, ka[:, :, HD2:2 * HD2], ALU.subtract).then_inc(sem("ka2_ready"), 4)
            dve.wait_ge(sem("vf2_ready"), 4)
            seq.step(nc.vector.tensor_reduce(sv2, vT2, AX.X, ALU.max, apply_absolute_value=True))
            seq.step(nc.vector.tensor_scalar(sv2, sv2, 1.0 / 127.0, 1e-8, ALU.mult, ALU.max))
            seq.step(nc.vector.reciprocal(isv2, sv2))
            for c in range(DC):
                seq.mark(nc.vector.tensor_scalar(vT2[:, c, :], vT2[:, c, :], isv2[:, c:c + 1], 127.0, ALU.mult, ALU.min))
            seq.wait()
            seq.step(nc.vector.tensor_scalar(vT2, vT2, -127.0, MAGIC, ALU.max, ALU.add))
            dve.wait_ge(sem("qa2_ready"), 3)
            nc.vector.tensor_scalar(vi2, vT2, MAGIC, None, ALU.subtract).then_inc(sem("vi2_ready"), 1)
            for b in range(2):
                dve.wait_ge(sem("v2_blocks"), b + 1)
                nc.vector.tensor_copy(v2[:, 4 * b:4 * b + 4, :].rearrange("p t d -> p (t d)"), bf(b)).then_inc(sem("v2_ready"), 1)

            def top(n):
                h, t = n // NT, n % NT
                dve.wait_ge(sem("scores2_done"), n + 1)
                seq.step(nc.vector.tensor_reduce(nmax2[:, n:n + 1], psum[:, n % 2 * T:(n % 2 + 1) * T], AX.X, ALU.max, negate=True))
                nc.vector.tensor_scalar(bias2[:, n:n + 1], nmax2[:, n:n + 1], s2[:, 0, t * H2 + h:t * H2 + h + 1], LN255,
                                        ALU.mult, ALU.add).then_inc(sem("bias2_ready"), 1)

            def to_integers(n):
                dve.wait_ge(sem("e2_ready"), n + 1)
                if n >= SLOTS2:
                    dve.wait_ge(sem("rT2_blocks"), n - SLOTS2 + 1)
                nc.vector.tensor_scalar(r2[:, n % SLOTS2, :], e2[:, n % SLOTS2, :], MAGIC, MAGIC, ALU.add, ALU.subtract)\
                  .then_inc(sem("r2_ready"), 1)

            def scale_out(g):
                seq.step(nc.vector.reciprocal(rz2[:, g * GH2:(g + 1) * GH2, :], zs2[:, g * GH2:(g + 1) * GH2, :]))
                dve.wait_ge(sem("values2_done"), GH2 * NT * (g + 1))
                nc.vector.tensor_tensor(
                    o2.rearrange("p t (h d) -> p h t d", d=HD2)[:, g * GH2:(g + 1) * GH2],
                    bank[7].rearrange("p (h t d) -> p h t d", h=GH2, t=NT),
                    bcast(rz2[:, g * GH2:(g + 1) * GH2, :], 3, HD2), ALU.mult).then_inc(sem("o2_ready"), 1)

            dve.wait_ge(sem("qkT2_ready"), H2)
            dve.wait_ge(sem("vi2_ready"), 1)
            U = H2 * NT
            for n in range(U + 1):
                if n < U:
                    top(n)
                if n:
                    to_integers(n - 1)
                if n > 4 and (n - 4) % (GH2 * NT) == 0:
                    scale_out((n - 4) // (GH2 * NT) - 1)
            scale_out(H2 // GH2 - 1)
            for b in range(4):
                dve.wait_ge(sem("proj2_done"), b + 1)
                seq.mark(nc.vector.scalar_tensor_tensor(x[:, 2 * b:2 * b + 2, :].rearrange("p a d -> p (a d)"), bank[4 + b],
                                                        tg[:, 1:2], x[:, 2 * b:2 * b + 2, :].rearrange("p a d -> p (a d)"),
                                                        ALU.mult, ALU.add))
            seq.wait()

        def small_softmax_vector(dve, seq, n, E, ps, shifted, probs, mx, total):
            dve.wait_ge(sem("router_logits"), n)
            lg = ps[:, 0:NT * E].rearrange("p (t e) -> p t e", t=NT)
            seq.step(nc.vector.tensor_reduce(mx, lg, AX.X, ALU.max))
            nc.vector.tensor_tensor(shifted, lg, bcast(mx, 2, E), ALU.subtract).then_inc(sem("router_shifted"), 1)
            dve.wait_ge(sem("router_exp"), n)
            seq.step(nc.vector.tensor_reduce(total, probs, AX.X, ALU.add))
            seq.step(nc.vector.reciprocal(total, total))
            seq.step(nc.vector.tensor_tensor(probs, probs, bcast(total, 2, E), ALU.mult))

        def small_softmax_scalar(act, n, shifted, probs):
            act.wait_ge(sem("router_shifted"), n)
            nc.scalar.activation(probs, shifted, ACT.Exp).then_inc(sem("router_exp"), 1)

        def router_tensor(pe, E, w, ps):
            for t in range(NT):
                for c in range(DC):
                    last = nc.tensor.matmul(ps[:, t * E:(t + 1) * E], xnT[:, c, t * P:(t + 1) * P], w[:, c, :],
                                            start=(c == 0), stop=(c == DC - 1))
            last.then_inc(sem("router_logits"), 1)

        E3, N3 = 16, 18
        rw3 = sb("rw3", [P, DC, E3])
        rbias3 = sb("rbias3", [P, E3])
        r = Region(arena, ARENA)
        probs3 = r.f32(NT, E3)
        shifted3 = r.f32(NT, E3)
        mx3 = r.f32(NT)
        total3 = r.f32(NT)
        val3 = r.f32(NT, E3 + 8)
        top3 = r.f32(NT, 8)
        rep3 = r.f32(NT, E3 + 8)
        mix3 = r.f32(NT, E3)
        hid3 = r.f32(2, T)
        scr3 = r.f32(2, 512)
        W3 = 10 * 1024 // 768
        w3_at = [(RING0 + s) % W3 for s in range(W3)]

        def w3(m):
            a = w3_at[m % W3] * 768
            return wring[:, a:a + 768]

        def loaded3(pe, m):
            slot = w3_at[m % W3]
            pe.wait_ge(sem(f"ring_loaded{slot}"), 16 * (m // W3 + 1 + (E0 // RING0 if slot < RING0 else 0)))

        def scale3(m, t):
            return mix3[:, t, m:m + 1] if m < E3 else tg[:, 5:6]

        dense3 = Dense("dense3", N3, 5, w3, loaded3, hid3, scr3, scale=scale3, earlier=2)

        def l1f_sync(sp):
            sp.dma_start(rw3[:], A["l1_router"].rearrange("(c p) e -> p c e", p=P)).then_inc(sem("l1f_small_loaded"), 16)
            sp.dma_start(rbias3[:], A["l1_rbias"].rearrange("(o n) -> o n", o=1).to_broadcast([P, E3])).then_inc(sem("l1f_small_loaded"), 16)

        def l1f_sync2(sp):
            for m in range(N3):
                if m == W3 - RING0:
                    sp.wait_ge(sem("w0_used"), E0)
                if m >= W3:
                    dense3.wait(sp, "down_done", 4 * (m - W3) + 4)
                sp.dma_start(w3(m), A["l1_experts"][m]).then_inc(sem(f"ring_loaded{w3_at[m % W3]}"), 16)

        def l1f_tensor(pe):
            ln_tensor(pe, 3)
            pe.wait_ge(sem("xnT_ready"), 16)
            pe.wait_ge(sem("l1f_small_loaded"), 32)
            router_tensor(pe, E3, rw3, bank[6])
            dense3.tensor(pe)

        def l1f_scalar(act):
            ln_scalar(act, 3)
            small_softmax_scalar(act, 1, shifted3, probs3)
            dense3.scalar(act)

        def l1f_vector(dve, seq):
            ln_vector(dve, seq, 3)
            dve.wait_ge(sem("l1f_small_loaded"), 32)
            small_softmax_vector(dve, seq, 1, E3, bank[6], shifted3, probs3, mx3, total3)
            seq.mark(nc.vector.memset(val3[:, :, E3:E3 + 8], NONE))
            seq.step(nc.vector.tensor_tensor(val3[:, :, 0:E3], bank[6][:, 0:NT * E3].rearrange("p (t e) -> p t e", t=NT),
                                             bcast(rbias3[:], 1, NT), ALU.add))
            top_mask(seq, val3, top3, rep3, E3, 2, mix3)
            seq.step(nc.vector.tensor_tensor(mix3, mix3, probs3, ALU.mult))
            seq.step(nc.vector.tensor_reduce(total3, mix3, AX.X, ALU.add))
            seq.step(nc.vector.reciprocal(total3, total3))
            seq.step(nc.vector.scalar_tensor_tensor(mix3, mix3, tg[:, 5:6], bcast(total3, 2, E3), ALU.mult, ALU.mult))
            nc.vector.engine_nop().then_inc(sem("mix3_ready"), 1)
            dense3.vector(dve, seq)

        wx4 = SH0[:].rearrange("p m n -> p (m n)").rearrange("p (j c n) -> p j c n", j=3, c=DC)
        bqk4 = sb("bqk4", [P, 2, DC])
        bv4 = sb("bv4", [1, D])
        HID = 4 * D
        r = Region(arena, ARENA)
        r.at = 19 * 1024
        mask4 = r.f32(NT, P)
        mask6u = r.f32(NT * P // 4).bitcast(U8)
        mask6 = r.f32(NT, P)
        off6 = r.f32(NT, P)
        bias5 = r.f32(2, HID)
        bout5 = r.f32(D)
        r = Region(arena, ARENA)
        qT4 = r.f32(DC, T)
        kT4 = r.f32(DC, T)
        v4 = r.f32(NT, D)
        s4 = r.f32(NT, P)
        p4 = r.f32(NT, P)
        pT4 = r.f32(NT, P)
        nmax4 = r.f32(NT)
        sum4 = r.f32(NT)
        coef4 = r.f32(NT)
        valid6 = r.f32(NT)

        class Attention:

            def __init__(self, name, gate, q, k, v, earlier):
                self.name, self.gate, self.q, self.k, self.v, self.earlier = name, gate, q, k, v, earlier

            def sem(self, what):
                return sem(f"attn_{what}")

            def wait(self, eng, what, n):
                per_run = NT if what in ("p_ready", "out_done") else 2
                eng.wait_ge(self.sem(what), n + per_run * self.earlier)

            def tensor(self, pe):
                for b in range(NT):
                    for c in range(DC):
                        last = nc.tensor.matmul(bank[4 + b // 4][:, b % 4 * P:(b % 4 + 1) * P], self.q[:, c, b * P:(b + 1) * P],
                                                self.k[:, c, b * P:(b + 1) * P], start=(c == 0), stop=(c == DC - 1))
                    if b % 4 == 3:
                        last.then_inc(self.sem("scores_done"), 1)
                for b in range(NT):
                    self.wait(pe, "p_ready", b + 1)
                    last = nc.tensor.transpose(bank[6 + b // 4][:, b % 4 * P:(b % 4 + 1) * P], p4[:, b, :], ident[:])
                    if b % 4 == 3:
                        last.then_inc(self.sem("p_blocks"), 1)
                for b in range(NT):
                    self.wait(pe, "pT_ready", b // 4 + 1)
                    nc.tensor.matmul(bank[b // 2][:, b % 2 * D:(b % 2 + 1) * D], pT4[:, b, :], self.v[:, b, :],
                                     start=True, stop=True).then_inc(self.sem("out_done"), 1)

            def scalar(self, act):
                for b in range(NT):
                    self.wait(act, "nmax_ready", b // 4 + 1)
                    nc.scalar.activation(p4[:, b, :], s4[:, b, :], ACT.Exp, bias=nmax4[:, b:b + 1],
                                         accum_out=sum4[:, b:b + 1]).then_inc(self.sem("p_ready"), 1)
                for i in range(2):
                    self.wait(act, "p_blocks", i + 1)
                    nc.scalar.copy(pT4[:, 4 * i:4 * i + 4, :].rearrange("p b q -> p (b q)"), bank[6 + i]).then_inc(self.sem("pT_ready"), 1)

            def vector(self, dve, seq, mask, offset=None, valid=None):
                for i in range(2):
                    four = slice(4 * i, 4 * i + 4)
                    self.wait(dve, "scores_done", i + 1)
                    seq.step(nc.vector.scalar_tensor_tensor(s4[:, four, :], bank[4 + i].rearrange("p (b k) -> p b k", b=4), D ** -0.5,
                                                            mask[:, four, :], ALU.mult, ALU.add if offset is None else ALU.mult))
                    if offset is not None:
                        seq.step(nc.vector.tensor_tensor(s4[:, four, :], s4[:, four, :], offset[:, four, :], ALU.add))
                    nc.vector.tensor_reduce(nmax4[:, four], s4[:, four, :], AX.X, ALU.max, negate=True).then_inc(self.sem("nmax_ready"), 1)
                self.wait(dve, "p_ready", NT)
                seq.step(nc.vector.reciprocal(coef4, sum4))
                seq.step(nc.vector.tensor_scalar(coef4, coef4, tg[:, self.gate:self.gate + 1], None, ALU.mult))
                if valid is not None:
                    seq.step(nc.vector.tensor_tensor(coef4, coef4, valid, ALU.mult))
                for b in range(NT):
                    self.wait(dve, "out_done", b // 2 * 2 + 2)
                    seq.mark(nc.vector.scalar_tensor_tensor(x[:, b, :], bank[b // 2][:, b % 2 * D:(b % 2 + 1) * D], coef4[:, b:b + 1],
                                                            x[:, b, :], ALU.mult, ALU.add))
                seq.wait()

        attn4 = Attention("attn4", 2, qT4, kT4, v4, 0)
        attn6 = Attention("attn6", 3, xnT[:], cT[:], ctok[:], 1)

        def l2x_sync(sp):
            sp.wait_ge(sem("proj2_done"), 4)
            for dst, src in ((mask4, A["mask4"].rearrange("b q k -> q b k")),
                             (mask6u, A["mask6"].rearrange("(o b) k -> o (b k)", o=1).to_broadcast([P, NT * P])),
                             (bqk4[:, 0, :], A["l2_bq"]), (bqk4[:, 1, :], A["l2_bk"]),
                             (bv4[:], A["l2_bv"].rearrange("(o n) -> o n", o=1))):
                sp.dma_start(dst, src).then_inc(sem("l2x_loaded"), 16)

        def l2x_sync2(sp):
            shared0.wait(sp, "down_done", 8)
            for j, name in enumerate(("l2_wq", "l2_wk", "l2_wv")):
                sp.dma_start(wx4[:, j], A[name].rearrange("(c p) n -> p c n", p=P)).then_inc(sem("l2x_loaded"), 16)

        L2X_LOADS = 16 * 8

        def l2x_tensor(pe):
            ln_tensor(pe, 4)
            pe.wait_ge(sem("xnT_ready"), 20)
            pe.wait_ge(sem("l2x_loaded"), L2X_LOADS)
            for j in range(2):
                for f in range(DC):
                    for half in range(2):
                        for c in range(DC):
                            last = nc.tensor.matmul(bank[4 * j + 2 * f + half], wx4[:, j, c, f * P:(f + 1) * P],
                                                    xnT[:, c, half * 512:(half + 1) * 512], start=(c == 0), stop=(c == DC - 1))
                        last.then_inc(sem("qk4_done"), 1)
            for t in range(NT):
                if t % 2 == 0:
                    pe.wait_ge(sem("qk4_ready"), t // 2 + 1)
                ps = bank[t // 2][:, t % 2 * D:(t % 2 + 1) * D]
                nc.tensor.matmul(ps, ones_row[:], bv4[:], start=True, stop=False)
                for c in range(DC):
                    last = nc.tensor.matmul(ps, xnT[:, c, t * P:(t + 1) * P], wx4[:, 2, c, :], start=False, stop=(c == DC - 1))
                if t % 2:
                    last.then_inc(sem("v4_done"), 1)
            pe.wait_ge(sem("qk4_ready"), 8)
            pe.wait_ge(sem("v4_ready"), 4)
            attn4.tensor(pe)
            wsum_tensor(pe)

        def l2x_scalar(act):
            ln_scalar(act, 4)
            act.wait_ge(sem("l2x_loaded"), L2X_LOADS)
            for j, dst in enumerate((qT4, kT4)):
                for f in range(DC):
                    for half in range(2):
                        act.wait_ge(sem("qk4_done"), 4 * j + 2 * f + half + 1)
                        nc.scalar.activation(dst[:, f, half * 512:(half + 1) * 512], bank[4 * j + 2 * f + half], ACT.Identity,
                                             bias=bqk4[:, j, f:f + 1]).then_inc(sem("qk4_ready"), 1)
            for b in range(4):
                act.wait_ge(sem("v4_done"), b + 1)
                nc.scalar.copy(v4[:, 2 * b:2 * b + 2, :].rearrange("p t d -> p (t d)"), bank[b]).then_inc(sem("v4_ready"), 1)
            wabs_scalar(act)
            attn4.scalar(act)

        def l2x_vector(dve, seq):
            ln_vector(dve, seq, 4)
            dve.wait_ge(sem("l2x_loaded"), L2X_LOADS)
            attn4.vector(dve, seq, mask4)

        HC = HID // P
        NW = DC * HID
        w5 = wring[:, 0:3 * NW].rearrange("p (j n) -> p j n", j=3)
        w5q = wring[:, 3 * NW:3 * NW + 3 * NW // 2].bitcast(BF16).rearrange("p (j n) -> p j n", j=3)
        onesf = sb("onesf", [P, P])
        wabs5 = sb("wabs5", [P, 3])
        gam5 = sb("gam5", [P, 3])
        igam5 = sb("igam5", [P, 3])
        r = Region(arena, ARENA)
        r.at = 14 * 1024
        wjunk5 = r.f32(NW)
        xq5 = r.bf16(NT, D)
        xqT5 = r.bf16(DC, T)
        gx5 = r.f32(NT)
        igx5 = r.f32(NT)
        sx5 = r.f32(2, NT)
        r = Region(arena, 14 * 1024)
        g5 = r.f32(2, HID)
        v5 = r.f32(2, HID)
        h5 = r.f32(2, HID)
        hq5 = r.bf16(2, HID)
        hqT5 = r.bf16(2, HID)
        gh5 = r.f32(2)
        igh5 = r.f32(2)
        so5 = r.f32(2)
        y5 = r.f32(2, D)

        def l2f_sync(sp):
            for j in range(2):
                sp.dma_start(bias5[:, j, :], A[("l2_gate_b", "l2_val_b")[j]].rearrange("(o n) -> o n", o=1).to_broadcast([P, HID]))\
                  .then_inc(sem("l2f_bias_loaded"), 16)
            sp.dma_start(bout5, A["l2_out_b"].rearrange("(o n) -> o n", o=1).to_broadcast([P, D])).then_inc(sem("l2f_bias_loaded"), 16)

        def l2f_sync2(sp):
            dense3.wait(sp, "down_done", 4 * N3)
            for j, name in enumerate(("l2_gate_w", "l2_val_w", "l2_out_w")):
                sp.dma_start(w5[:, j, :].rearrange("p (c n) -> p c n", n=HID if j < 2 else D),
                             A[name].rearrange("(c p) n -> p c n", p=P)).then_inc(sem(f"w5_loaded{j}"), 16)

        def wabs_scalar(act):
            for j in range(3):
                act.wait_ge(sem(f"w5_loaded{j}"), 16)
                if j:
                    act.wait_ge(sem("wabs_done"), j)
                nc.scalar.activation(wjunk5, w5[:, j, :], ACT.Abs, accum_out=wabs5[:, j:j + 1]).then_inc(sem("wabs_done"), 1)

        def wsum_tensor(pe):
            pe.wait_ge(sem("wabs_done"), 3)
            pe.wait_ge(sem("onesf_ready"), 1)
            attn4.wait(pe, "p_ready", NT)
            nc.tensor.matmul(bank[4][:, 0:3], onesf[:], wabs5[:], start=True, stop=True).then_inc(sem("wsum_done"), 1)

        def l2f_gpsimd(pool):
            nc.gpsimd.memset(onesf[:], 1.0).then_inc(sem("onesf_ready"), 1)

        def l2f_gpsimd2(pool):
            pool.wait_ge(sem("gam5_ready"), 1)
            for j in range(3):
                nc.gpsimd.tensor_scalar(w5[:, j, :], w5[:, j, :], igam5[:, j:j + 1], 1.0, ALU.mult, ALU.min).then_inc(sem("w5_steps"), 1)
                pool.wait_ge(sem("w5_steps"), 2 * j + 1)
                nc.gpsimd.tensor_scalar(w5[:, j, :], w5[:, j, :], -1.0, MAGIC, ALU.max, ALU.add).then_inc(sem("w5_steps"), 1)
                pool.wait_ge(sem("w5_steps"), 2 * j + 2)
                nc.gpsimd.tensor_scalar(w5q[:, j, :], w5[:, j, :], MAGIC, None, ALU.subtract).then_inc(sem("w5q_ready"), 1)

        def l2f_tensor(pe):
            for n in range(2):
                pe.wait_ge(sem("xq5_ready"), 1)
                for t in range(4):
                    for c in range(DC):
                        last = nc.tensor.transpose(bf(n)[:, (c * 4 + t) * P:(c * 4 + t + 1) * P], xq5[:, 4 * n + t, c * P:(c + 1) * P], identb[:])
                last.then_inc(sem("xqT5_blocks"), 1)
            pe.wait_ge(sem("xqT5_ready"), 2)
            pe.wait_ge(sem("w5q_ready"), 2)

            def up(t):
                if t:
                    pe.wait_ge(sem("gv5_ready"), 2 * t)
                for j in range(2):
                    for half in range(2):
                        for c in range(DC):
                            last = nc.tensor.matmul(bank[2 * j + half], xqT5[:, c, t * P:(t + 1) * P],
                                                    w5q[:, j, c * HID + half * 512:c * HID + (half + 1) * 512],
                                                    start=(c == 0), stop=(c == DC - 1))
                    last.then_inc(sem("up5_done"), 1)

            def turn(t):
                pe.wait_ge(sem("hq5_ready"), t + 1)
                if t >= 2:
                    pe.wait_ge(sem("hqT5_ready"), t - 1)
                for c in range(HC):
                    last = nc.tensor.transpose(bf(4 + t % 2)[:, c * P:(c + 1) * P], hq5[:, t % 2, c * P:(c + 1) * P], identb[:])
                last.then_inc(sem("hqT5_blocks"), 1)

            def down(t):
                pe.wait_ge(sem("hqT5_ready"), t + 1)
                if t == 0:
                    pe.wait_ge(sem("w5q_ready"), 3)
                if t >= 2:
                    pe.wait_ge(sem("y5_ready"), t - 1)
                for c in range(HC):
                    last = nc.tensor.matmul(bank[6 + t % 2][:, 0:D], hqT5[:, t % 2, c * P:(c + 1) * P],
                                            w5q[:, 2, c * D:(c + 1) * D], start=(c == 0), stop=(c == HC - 1))
                last.then_inc(sem("down5_done"), 1)

            for t in range(NT + 1):
                if t < NT:
                    up(t)
                if t:
                    turn(t - 1)
                    down(t - 1)

        def l2f_scalar(act):
            ln_scalar(act, 5)
            for n in range(2):
                act.wait_ge(sem("xqT5_blocks"), n + 1)
                nc.scalar.copy(xqT5[:, :, n * 512:(n + 1) * 512], bf(n).rearrange("p (c t) -> p c t", c=DC)).then_inc(sem("xqT5_ready"), 1)
            for t in range(NT + 1):
                if t < NT:
                    act.wait_ge(sem("g5_ready"), t + 1)
                    nc.scalar.activation(g5[:, t % 2, :], g5[:, t % 2, :], ACT.Silu).then_inc(sem("silu5_ready"), 1)
                if t:
                    act.wait_ge(sem("hqT5_blocks"), t)
                    if t >= 3:
                        act.wait_ge(sem("down5_done"), t - 2)
                    nc.scalar.copy(hqT5[:, (t - 1) % 2, :], bf(4 + (t - 1) % 2)).then_inc(sem("hqT5_ready"), 1)

        def round_clip(seq, dst, buf, inv, lo, hi, last):
            seq.step(nc.vector.tensor_scalar(buf, buf, inv, hi, ALU.mult, ALU.min))
            seq.step(nc.vector.tensor_scalar(buf, buf, lo, MAGIC, ALU.max, ALU.add))
            last(nc.vector.tensor_scalar(dst, buf, MAGIC, None, ALU.subtract))

        def gam_vector(dve, seq):
            dve.wait_ge(sem("wsum_done"), 1)
            seq.step(nc.vector.tensor_scalar(gam5[:], bank[4][:, 0:3], 1.0 / (D * HID), 1e-5, ALU.mult, ALU.max))
            nc.vector.reciprocal(igam5[:], gam5[:]).then_inc(sem("gam5_ready"), 1)

        def l2f_vector(dve, seq):
            gam_vector(dve, seq)
            ln_vector(dve, seq, 5)
            dve.wait_ge(sem("xn_ready"), NT * 6)
            seq.step(nc.vector.tensor_reduce(gx5, xn[:], AX.X, ALU.max, apply_absolute_value=True))
            seq.step(nc.vector.tensor_scalar(gx5, gx5, 1e-5, None, ALU.max))
            seq.step(nc.vector.reciprocal(igx5, gx5))
            seq.mark(nc.vector.tensor_scalar(igx5, igx5, 127.0, None, ALU.mult))
            for j in range(2):
                seq.mark(nc.vector.tensor_scalar(sx5[:, j, :], gx5, gam5[:, j:j + 1], 1.0 / 127.0, ALU.mult, ALU.mult))
            seq.wait()
            for t in range(NT):
                seq.mark(nc.vector.tensor_scalar(xn[:, t, :], xn[:, t, :], igx5[:, t:t + 1], 127.0, ALU.mult, ALU.min))
            seq.wait()
            flat = xn[:].rearrange("p t d -> p (t d)")
            seq.step(nc.vector.tensor_scalar(flat, flat, -128.0, MAGIC, ALU.max, ALU.add))
            nc.vector.tensor_scalar(xq5.rearrange("p t d -> p (t d)"), flat, MAGIC, None, ALU.subtract).then_inc(sem("xq5_ready"), 1)
            dve.wait_ge(sem("l2f_bias_loaded"), 48)

            def linear(t, j, dst, ready):
                dve.wait_ge(sem("up5_done"), 2 * t + j + 1)
                ins = nc.vector.scalar_tensor_tensor(dst[:, t % 2, :], psum[:, j * HID:(j + 1) * HID], sx5[:, j, t:t + 1],
                                                     bias5[:, j, :], ALU.mult, ALU.add)
                ins.then_inc(sem("gv5_ready"), 1)
                if ready:
                    dve.wait_ge(sem("gv5_ready"), 2 * t + j + 1)
                    nc.vector.engine_nop().then_inc(sem(ready), 1)

            def hidden(t):
                i = t % 2
                dve.wait_ge(sem("silu5_ready"), t + 1)
                dve.wait_ge(sem("gv5_ready"), 2 * t + 2)
                seq.step(nc.vector.tensor_tensor(h5[:, i, :], g5[:, i, :], v5[:, i, :], ALU.mult))
                seq.step(nc.vector.tensor_reduce(gh5[:, i:i + 1], h5[:, i, :], AX.X, ALU.max, apply_absolute_value=True))
                seq.step(nc.vector.tensor_scalar(gh5[:, i:i + 1], gh5[:, i:i + 1], 1e-5, None, ALU.max))
                seq.mark(nc.vector.reciprocal(igh5[:, i:i + 1], gh5[:, i:i + 1]))
                seq.step(nc.vector.tensor_scalar(so5[:, i:i + 1], gh5[:, i:i + 1], gam5[:, 2:3], 1.0 / 127.0, ALU.mult, ALU.mult))
                seq.step(nc.vector.tensor_scalar(igh5[:, i:i + 1], igh5[:, i:i + 1], 127.0, None, ALU.mult))
                if t >= 2:
                    dve.wait_ge(sem("hqT5_blocks"), t - 1)
                round_clip(seq, hq5[:, i, :], h5[:, i, :], igh5[:, i:i + 1], -128.0, 127.0,
                           lambda ins: ins.then_inc(sem("hq5_ready"), 1))

            def output(t):
                i = t % 2
                dve.wait_ge(sem("down5_done"), t + 1)
                nc.vector.scalar_tensor_tensor(y5[:, i, :], bank[6 + i][:, 0:D], so5[:, i:i + 1], bout5, ALU.mult, ALU.add)\
                  .then_inc(sem("y5_ready"), 1)
                dve.wait_ge(sem("y5_ready"), t + 1)
                seq.step(nc.vector.scalar_tensor_tensor(x[:, t, :], y5[:, i, :], tg[:, 6:7], x[:, t, :], ALU.mult, ALU.add))

            for t in range(NT + 1):
                if t < NT:
                    linear(t, 0, g5, "g5_ready")
                    linear(t, 1, v5, None)
                if t:
                    output(t - 1)
                if t < NT:
                    hidden(t)

        def l3x_gpsimd(pool):
            pool.wait_ge(sem("l2x_loaded"), L2X_LOADS)
            nc.gpsimd.tensor_copy(mask6.rearrange("p b k -> p (b k)"), mask6u).then_inc(sem("mask6_steps"), 1)
            pool.wait_ge(sem("mask6_steps"), 1)
            nc.gpsimd.tensor_scalar(off6, mask6, -1.0, 1e30, ALU.add, ALU.mult).then_inc(sem("mask6_steps"), 1)

        def l3x_tensor(pe):
            ln_tensor(pe, 6)
            pe.wait_ge(sem("xnT_ready"), 24)
            attn6.tensor(pe)

        def l3x_scalar(act):
            ln_scalar(act, 6)
            attn6.scalar(act)

        def l3x_vector(dve, seq):
            ln_vector(dve, seq, 6)
            dve.wait_ge(sem("mask6_steps"), 2)
            seq.step(nc.vector.tensor_reduce(valid6, mask6, AX.X, ALU.max))
            attn6.vector(dve, seq, mask6, off6, valid6)

        E7, K7, C7, FF7 = 8, 2, 320, 1024
        FC7 = FF7 // P
        JT7 = [(0, P), (P, P), (2 * P, C7 - 2 * P)]
        rw7 = sb("rw7", [P, DC, E7])
        WN7 = DC * FF7 + FC7 * D
        w7 = wring[:, 0:2 * WN7].rearrange("p (s n) -> p s n", s=2)
        r = Region(arena, ARENA)
        moe7 = Moe("moe7", E7, K7, C7, 7, r.f32(E7 * C7 // P, D), r, 0, earlier=moe0)
        probs7 = r.f32(NT, E7)
        shifted7 = r.f32(NT, E7)
        mx7 = r.f32(NT)
        total7 = r.f32(NT)
        val7 = r.f32(NT, E7 + 8)
        top7 = r.f32(NT, 8)
        rep7 = r.f32(NT, E7 + 8)
        h7 = r.f32(2, FC7, C7)
        y7 = r.f32(2, 3, D)

        def l3f_sync(sp):
            sp.dma_start(rw7[:], A["l3_router"].rearrange("(c p) e -> p c e", p=P)).then_inc(sem("rw7_loaded"), 16)
            moe7.clear_rows(sp)

        def l3f_sync2(sp):
            sp.wait_ge(sem("down5_done"), NT)
            for i in range(2):
                sp.dma_start(w7[:, i, :], A["l3_experts"][i]).then_inc(sem(f"w7_loaded{i}"), 16)
            moe7.load_rows_sync(sp)
            with sp.Fori(1, E7 // 2) as it:
                for i in range(2):
                    sp.wait_ge(sem("down7_done"), (it - 1) * 6 + 3 * i + 3)
                    sp.dma_start(w7[:, i, :], A["l3_experts"][bass.ds(it * 2 + i, 1)].rearrange("o p n -> p (o n)"))\
                      .then_inc(sem(f"w7_loaded{i}"), 16)

        def l3f_tensor(pe):
            ln_tensor(pe, 7)
            pe.wait_ge(sem("xnT_ready"), 28)
            pe.wait_ge(sem("rw7_loaded"), 16)
            router_tensor(pe, E7, rw7, bank[4])
            moe7.positions_tensor(pe, bank[5])
            moe7.rows_tensor(pe)
            with pe.Fori(0, E7 // 2) as it:
                for i in range(2):
                    pe.wait_ge(sem(f"w7_loaded{i}"), (it + 1) * 16)
                    for f in range(FC7):
                        u = (it * 2 + i) * FC7 + f
                        if i or f >= 4:
                            pe.wait_ge(sem("h7_ready"), u - 3)
                        for c in range(DC):
                            last = nc.tensor.matmul(bank[f % 4][:, 0:C7], w7[:, i, c * FF7 + f * P:c * FF7 + (f + 1) * P],
                                                    moe7.rowsT[:, c, bass.ds((it * 2 + i) * C7, C7)], start=(c == 0), stop=(c == DC - 1))
                        last.then_inc(sem("up7_done"), 1)
                for i in range(2):
                    pe.wait_ge(sem("h7_ready"), (it * 2 + i + 1) * FC7)
                    for j, (lo, n) in enumerate(JT7):
                        if i:
                            pe.wait_ge(sem("y7_ready"), it * 6 + j + 1)
                        for f in range(FC7):
                            last = nc.tensor.matmul(bank[4 + j][0:n, 0:D], h7[:, i, f, lo:lo + n],
                                                    w7[:, i, DC * FF7 + f * D:DC * FF7 + (f + 1) * D], start=(f == 0), stop=(f == FC7 - 1))
                        last.then_inc(sem("down7_done"), 1)
                    last = nc.tensor.nop() if False else last
                pe.wait_ge(sem("y7_ready"), it * 6 + 6)

        def l3f_scalar(act):
            ln_scalar(act, 7)
            small_softmax_scalar(act, 2, shifted7, probs7)
            moe7.rows_scalar(act)
            with act.Fori(0, E7 // 2) as it:
                for i in range(2):
                    for f in range(FC7):
                        act.wait_ge(sem("up7_done"), (it * 2 + i) * FC7 + f + 1)
                        nc.scalar.activation(h7[:, i, f, :], bank[f % 4][:, 0:C7], ACT.Relu).then_inc(sem("h7_ready"), 1)

        def l3f_vector(dve, seq):
            ln_vector(dve, seq, 7)
            small_softmax_vector(dve, seq, 2, E7, bank[4], shifted7, probs7, mx7, total7)
            seq.mark(nc.vector.memset(val7[:, :, E7:E7 + 8], NONE))
            seq.step(nc.vector.tensor_copy(val7[:, :, 0:E7], probs7))
            top_mask(seq, val7, top7, rep7, E7, K7, moe7.sel)
            nc.vector.tensor_copy(moe7.selb, moe7.sel).then_inc(moe7.sem("sel_ready"), 1)
            seq.step(nc.vector.tensor_tensor(moe7.weight, moe7.sel, probs7, ALU.mult))
            moe7.slots_vector(dve, seq, bank[5])
            with dve.Fori(0, E7 // 2) as it:
                for i in range(2):
                    for j, (lo, n) in enumerate(JT7):
                        dve.wait_ge(sem("down7_done"), (it * 2 + i) * 3 + j + 1)
                        dve.wait_ge(sem(f"y7_stored{i}"), it * 32)
                        nc.vector.tensor_copy(y7[0:n, i, j, :], bank[4 + j][0:n, 0:D]).then_inc(sem("y7_ready"), 1)
            moe7.combine_vector(dve)

        def l3f_gpsimd(pool):
            moe7.constants(pool)

        def l3f_gpsimd2(pool):
            moe7.scatter_gpsimd(pool)
            with pool.Fori(0, E7 // 2) as it:
                for i in range(2):
                    pool.wait_ge(sem("y7_ready"), (it * 2 + i) * 3 + 3)
                    row = (it * 2 + i) * C7
                    pool.dma_start(moe7.y_dram[bass.ds(row, 2 * P), :].rearrange("(j p) d -> p j d", p=P), y7[:, i, 0:2, :])\
                        .then_inc(sem(f"y7_stored{i}"), 16)
                    pool.dma_start(moe7.y_dram[bass.ds(row + 2 * P, C7 - 2 * P), :], y7[0:C7 - 2 * P, i, 2, :])\
                        .then_inc(sem(f"y7_stored{i}"), 16)
            for i in range(2):
                pool.wait_ge(sem(f"y7_stored{i}"), 32 * (E7 // 2))
            moe7.gather_gpsimd(pool)


        block = ctx.enter_context(nc.Block())

        @block.sync
        def _(sp):
            l0x_sync(sp)
            l0f_sync(sp)
            l0f_sync2(sp)
            l1x_sync(sp)
            l1f_sync(sp)
            l1f_sync2(sp)
            l2x_sync(sp)
            l2x_sync2(sp)
            l2f_sync(sp)
            l2f_sync2(sp)
            l3f_sync(sp)
            l3f_sync2(sp)
            sp.wait_ge(sem("x_final"), 1)
            sp.dma_start(out.rearrange("b s d -> s b d"), x[:]).then_inc(sem("out_stored"), 16)
            sp.wait_ge(sem("out_stored"), 16)

        @block.gpsimd
        def _(pool):
            l0x_gpsimd(pool)
            l0f_gpsimd(pool)
            l0f_gpsimd2(pool)
            l1x_gpsimd(pool)
            l2f_gpsimd(pool)
            l2f_gpsimd2(pool)
            l3x_gpsimd(pool)
            l3f_gpsimd(pool)
            l3f_gpsimd2(pool)

        @block.scalar
        def _(act):
            l0x_scalar(act)
            l0f_scalar(act)
            l1x_scalar(act)
            l1f_scalar(act)
            l2x_scalar(act)
            l2f_scalar(act)
            l3x_scalar(act)
            l3f_scalar(act)

        @block.tensor
        def _(pe):
            l0x_tensor(pe)
            l0f_tensor(pe)
            l1x_tensor(pe)
            l1f_tensor(pe)
            l2x_tensor(pe)
            l2f_tensor(pe)
            l3x_tensor(pe)
            l3f_tensor(pe)

        @block.vector
        def _(dve):
            seq = Chain(dve, sem("vector_steps"))
            l0x_vector(dve, seq)
            l0f_vector(dve, seq)
            l1x_vector(dve, seq)
            l1f_vector(dve, seq)
            l2x_vector(dve, seq)
            l2f_vector(dve, seq)
            l3x_vector(dve, seq)
            l3f_vector(dve, seq)
            dve.engine_nop().then_inc(sem("x_final"), 1)


def kernel(**inputs):
    import numpy as np
    import concourse.bacc as bacc
    from concourse.bass_utils import run_bass_kernel_spmd

    def tr(name):
        return np.ascontiguousarray(np.asarray(inputs[name]).T)

    def same(name):
        return np.ascontiguousarray(inputs[name])

    def columns(b):
        return np.ascontiguousarray(b.reshape(-1, P).T)

    def chunks(w):
        return w.reshape(D, -1, P).transpose(1, 0, 2)

    def packed(a, b, down):
        n = a.shape[0]
        parts = [w.reshape(n, DC, P, P).transpose(0, 2, 1, 3).reshape(n, P, DC * P) for w in (a, b)]
        return np.ascontiguousarray(np.concatenate([*parts, down], axis=2))

    given = {
        "x": same("x"), "ctx": same("ctx_2048"), "g_xattn": same("g_xattn"), "g_ffn": same("g_ffn"),
        "ssm": same("L0_xattn_ssm_kernel"), "ssm_d": same("L0_xattn_D").reshape(16, 1),
        "l0_router": tr("L0_ffn_router_w"), "l0_ebias": same("L0_ffn_e_bias"),
        "l0_experts": packed(same("L0_ffn_W_gate"), same("L0_ffn_W_up"), same("L0_ffn_W_down")),
        "l0_shared": packed(*(chunks(tr("L0_ffn_shared_gate")), chunks(tr("L0_ffn_shared_up")), tr("L0_ffn_shared_down").reshape(2, P, D))),
        "l1_wq": same("L1_xattn_Wq"), "l1_wkv": same("L1_xattn_Wkv"), "l1_wp": same("L1_xattn_Wp"),
        "l1_bq": same("L1_xattn_bq"), "l1_bkv": same("L1_xattn_bkv"), "l1_bp": same("L1_xattn_bp"),
        "l1_bv": columns(same("L1_xattn_bkv")[D:]),
        "l1_router": tr("L1_ffn_router_w"), "l1_rbias": same("L1_ffn_router_bias"),
        "l1_experts": np.concatenate([
            packed(same("L1_ffn_Wu"), same("L1_ffn_Wg"), same("L1_ffn_Wd")),
            packed(chunks(same("L1_ffn_Su")[0]), chunks(same("L1_ffn_Sg")[0]), same("L1_ffn_Sd")[0].reshape(2, P, D))]),
        "l2_wq": tr("L2_xattn_Wq"), "l2_wk": tr("L2_xattn_Wk"), "l2_wv": tr("L2_xattn_Wv"),
        "l2_bq": columns(same("L2_xattn_bq")), "l2_bk": columns(same("L2_xattn_bk")), "l2_bv": same("L2_xattn_bv"),
        "mask4": same("mask_BxSxS2_ff0"), "mask6": same("mask_BxS2_bk0"),
        "l2_gate_w": tr("L2_ffn_gate_w"), "l2_val_w": tr("L2_ffn_val_w"), "l2_out_w": tr("L2_ffn_out_w"),
        "l2_gate_b": same("L2_ffn_gate_b"), "l2_val_b": same("L2_ffn_val_b"), "l2_out_b": same("L2_ffn_out_b"),
        "l3_router": same("L3_ffn_Wg"),
        "l3_experts": np.ascontiguousarray(np.concatenate([
            same("L3_ffn_w1").reshape(8, DC, P, 4 * D).transpose(0, 2, 1, 3).reshape(8, P, -1),
            same("L3_ffn_w2").reshape(8, 4 * D // P, P, D).transpose(0, 2, 1, 3).reshape(8, P, -1)], axis=2)),
    }
    nc = bacc.Bacc("TRN2", target_bir_lowering=False, num_devices=1)
    arrays, aps = {}, {}
    for name, a in given.items():
        arrays[f"in_{name}"] = a
        aps[name] = nc.dram_tensor(f"in_{name}", a.shape, mybir.dt.from_np(a.dtype), kind="ExternalInput").ap()
    out = nc.dram_tensor("out_0", (NT, P, D), F32, kind="ExternalOutput").ap()
    build(nc, aps, out)
    r = run_bass_kernel_spmd(nc, [arrays], core_ids=[0])
    return r.results[0]["out_0"]
```

```python
from contextlib import ExitStack

import concourse.bass as bass
from concourse import mybir

P = 128
NT = 8
T = P * NT
D = 256
DC = D // P
LN_EPS = 1e-5
MAGIC = 12582912.0

F32 = mybir.dt.float32
BF16 = mybir.dt.bfloat16
I32 = mybir.dt.int32
U8 = mybir.dt.uint8
ALU = mybir.AluOpType
ACT = mybir.ActivationFunctionType
AX = mybir.AxisListType

ARENA = 25 * 1024


class Chain:

    def __init__(self, eng, sem):
        self.eng, self.sem, self.n = eng, sem, 0

    def mark(self, ins):
        self.n += 1
        return ins.then_inc(self.sem, 1)

    def wait(self):
        self.eng.wait_ge(self.sem, self.n)

    def step(self, ins):
        self.mark(ins)
        self.wait()


def build(nc, A, out):
    ctx = ExitStack()
    sems = {}

    def sem(name):
        if name not in sems:
            sems[name] = ctx.enter_context(nc.semaphore(name))
        return sems[name]

    def sb(name, shape, dt=F32):
        return ctx.enter_context(nc.sbuf_tensor(name, shape, dt))

    with ctx:
        psum = ctx.enter_context(nc.psum_tensor("psum", [P, 8 * 512], F32))
        bank = [psum[:, i * 512:(i + 1) * 512] for i in range(8)]

        x = sb("x", [P, NT, D])
        xn = sb("xn", [P, NT, D])
        xnT = sb("xnT", [P, DC, T])
        ctok = sb("ctok", [P, NT, D])
        cT = sb("cT", [P, DC, T])
        ident = sb("ident", [P, P])
        identb = sb("identb", [P, P], BF16)
        onesb = sb("onesb", [P, P], BF16)
        gates = sb("gates", [P, 8])
        tg = sb("tg", [P, 8])
        stats = sb("stats", [P, NT, 6])
        mv = sb("mv", [P, NT, 2])
        std = sb("std", [P, NT])
        rstd = sb("rstd", [P, NT])
        newt = sb("newt", [P, NT])
        var_eps = sb("var_eps", [P, NT])
        arena = sb("arena", [P, ARENA])
        wring = sb("wring", [P, 10 * 1024])

        class Region:

            def __init__(self, buf, size):
                self.buf, self.at, self.size = buf, 0, size

            def f32(self, *shape):
                n = 1
                for s in shape:
                    n *= s
                v = self.buf[:, self.at:self.at + n]
                self.at += n
                assert self.at <= self.size, self.at
                return shaped(v, shape)

            def bf16(self, *shape):
                n = 1
                for s in shape:
                    n *= s
                words = (n + 1) // 2
                v = self.buf[:, self.at:self.at + words].bitcast(BF16)
                self.at += words
                assert self.at <= self.size, self.at
                return shaped(v, shape)

        def shaped(v, shape):
            if len(shape) == 1:
                return v
            names = "abcd"[:len(shape)]
            return v.rearrange(f"p ({' '.join(names)}) -> p {' '.join(names)}",
                               **{m: s for m, s in zip(names[1:], shape[1:])})

        def bcast(ap, axis, n):
            dims = [list(d) for d in ap.ap]
            dims.insert(axis, [0, n])
            return bass.AP(tensor=ap.tensor, offset=ap.offset, ap=dims)

        unmerged = []

        def merge_stats(seq):
            if unmerged:
                seq.wait()
            for t in unmerged:
                seq.mark(nc.vector.bn_aggr(mv[:, t, :], stats[:, t, :]))
            unmerged.clear()

        def tile_stats(seq, tiles):
            merge_stats(seq)
            for t in tiles:
                seq.mark(nc.vector.bn_stats(stats[:, t, :], x[:, t, :]))
            unmerged.extend(tiles)

        def ln_vector(dve, seq, k):
            if k == 0:
                dve.wait_ge(sem("x_loaded"), 16)
                tile_stats(seq, range(NT))
            merge_stats(seq)
            seq.wait()
            nc.vector.tensor_scalar(var_eps[:], mv[:, :, 1], LN_EPS, None, ALU.add).then_inc(sem("var_ready"), 1)
            dve.wait_ge(sem("std_ready"), k + 1)
            seq.step(nc.vector.reciprocal(rstd[:], std[:]))
            seq.step(nc.vector.scalar_tensor_tensor(newt[:], rstd[:], -0.5, rstd[:], ALU.mult, ALU.mult))
            seq.step(nc.vector.tensor_tensor(newt[:], newt[:], var_eps[:], ALU.mult))
            seq.step(nc.vector.scalar_tensor_tensor(rstd[:], newt[:], 1.5, rstd[:], ALU.add, ALU.mult))
            for t in range(NT):
                nc.vector.tensor_scalar(xn[:, t, :], x[:, t, :], mv[:, t, 0:1], rstd[:, t:t + 1],
                                        ALU.subtract, ALU.mult).then_inc(sem("xn_ready"), 1)

        def ln_scalar(act, k, meanwhile=None):
            act.wait_ge(sem("var_ready"), k + 1)
            nc.scalar.activation(std[:], var_eps[:], ACT.Sqrt).then_inc(sem("std_ready"), 1)
            if meanwhile:
                meanwhile()
            if k != 5:
                evacuate_T(act, xnT, sem("xnT_blocks"), sem("xnT_ready"), turned(k))

        def turned(k):
            return k if k < 5 else k - 1

        def evacuate_T(act, dst, blocks, ready, k):
            for half in range(2):
                for c in range(DC):
                    act.wait_ge(blocks, 4 * k + 2 * half + c + 1)
                    nc.scalar.copy(dst[:, c, half * 512:(half + 1) * 512], bank[2 * half + c][:]).then_inc(ready, 1)

        def transpose_T(pe, src, blocks, before_tile=None):
            for half in range(2):
                for t in range(4):
                    if before_tile:
                        before_tile(half * 4 + t)
                    for c in range(DC):
                        last = nc.tensor.transpose(bank[2 * half + c][:, t * P:(t + 1) * P],
                                                   src[:, half * 4 + t, c * P:(c + 1) * P], ident[:])
                        if t == 3:
                            last.then_inc(blocks, 1)

        def ln_tensor(pe, k):
            transpose_T(pe, xn, sem("xnT_blocks"), lambda t: pe.wait_ge(sem("xn_ready"), NT * k + t + 1))

        H0, HD0, L = 16, 8, D
        r = Region(arena, ARENA)
        toep = r.f32(H0, L)
        cTr = r.f32(DC, T)
        flip = r.f32(P)
        KVS = 4
        kv = r.f32(KVS, DC, NT * HD0 * HD0)
        prod = r.f32(2, DC, NT * HD0 * HD0)
        z = r.f32(DC, T)
        kpad = sb("kpad", [H0, P + L])
        dcol = sb("dcol", [H0, 1])
        kpad_dram = nc.dram_tensor("kpad_dram", [H0, P + L], F32)

        def l0x_sync(sp):
            sp.dma_start(ctok[:], A["ctx"].rearrange("b s d -> s b d")).then_inc(sem("ctx_loaded"), 16)
            sp.dma_start(x[:], A["x"].rearrange("b s d -> s b d")).then_inc(sem("x_loaded"), 16)
            sp.wait_ge(sem("kpad_ready"), 2)
            sp.dma_start(kpad_dram[:], kpad[:]).then_inc(sem("kpad_stored"), 16)
            sp.wait_ge(sem("kpad_stored"), 16)
            sp.dma_start(toep, bass.AP(tensor=kpad_dram[:].tensor, offset=1,
                                       ap=[[1, P], [P + L, H0], [1, L]])).then_inc(sem("toep_loaded"), 16)

        def l0x_scalar(act):
            act.dma_start(gates[:, 0:4], A["g_xattn"].rearrange("(o n) -> o n", o=1).to_broadcast([P, 4])).then_inc(sem("gates_loaded"), 16)
            act.dma_start(gates[:, 4:8], A["g_ffn"].rearrange("(o n) -> o n", o=1).to_broadcast([P, 4])).then_inc(sem("gates_loaded"), 16)
            act.wait_ge(sem("gates_loaded"), 32)
            nc.scalar.activation(tg[:], gates[:], ACT.Tanh).then_inc(sem("tg_ready"), 1)
            evacuate_T(act, cT, sem("cT_blocks"), sem("cT_ready"), 0)
            def copy_cTr():
                for half in range(2):
                    for c in range(DC):
                        act.wait_ge(sem("cTr_blocks"), 2 * half + c + 1)
                        nc.scalar.copy(cTr[:, c, half * 512:(half + 1) * 512], bank[4 + 2 * half + c]).then_inc(sem("cTr_ready"), 1)

            ln_scalar(act, 0, copy_cTr)

        def l0x_gpsimd(pool):
            nc.gpsimd.memset(ident[:], 0.0).then_inc(sem("pool_consts"), 1)
            nc.gpsimd.memset(identb[:], 0.0).then_inc(sem("pool_consts"), 1)
            nc.gpsimd.memset(onesb[:], 1.0).then_inc(sem("pool_consts"), 1)
            nc.gpsimd.memset(kpad[:, :], 0.0).then_inc(sem("pool_consts"), 1)
            nc.gpsimd.memset(flip, 0.0).then_inc(sem("pool_consts"), 1)
            pool.wait_ge(sem("pool_consts"), 5)
            nc.gpsimd.affine_select(out=ident[:], in_=ident[:], compare_op=ALU.not_equal, fill=1.0, base=0,
                                    pattern=[[-1, P]], channel_multiplier=1).then_inc(sem("ident_ready"), 1)
            nc.gpsimd.affine_select(out=identb[:], in_=identb[:], compare_op=ALU.not_equal, fill=1.0, base=0,
                                    pattern=[[-1, P]], channel_multiplier=1).then_inc(sem("ident_ready"), 1)
            nc.gpsimd.affine_select(out=flip, in_=flip, compare_op=ALU.not_equal, fill=1.0, base=-(P - 1),
                                    pattern=[[1, P]], channel_multiplier=1).then_inc(sem("ident_ready"), 1)
            pool.dma_start(kpad[:, P:P + L], A["ssm"]).then_inc(sem("ssm_loaded"), 16)
            pool.dma_start(dcol[:], A["ssm_d"]).then_inc(sem("ssm_loaded"), 16)
            pool.wait_ge(sem("ssm_loaded"), 32)
            nc.gpsimd.tensor_tensor(kpad[:, P:P + 1], kpad[:, P:P + 1], dcol[:], ALU.add).then_inc(sem("kpad_ready"), 2)
            pool.wait_ge(sem("cTr_ready"), 4)
            for h in range(H0):
                if h >= KVS:
                    pool.wait_ge(sem("conv_done"), h - KVS + 1)
                for c in range(DC):
                    rows = cTr[:, c, :].rearrange("p (b s) -> p b s", b=NT)[:, :, h * HD0:(h + 1) * HD0]
                    nc.gpsimd.tensor_tensor(kv[:, h % KVS, c, :].rearrange("p (b j i) -> p b j i", b=NT, j=HD0),
                                            bcast(rows, 3, HD0), bcast(rows, 2, HD0),
                                            ALU.mult).then_inc(sem("kv_ready"), 1)

        def l0x_tensor(pe):
            pe.wait_ge(sem("ident_ready"), 3)
            pe.wait_ge(sem("ctx_loaded"), 16)
            transpose_T(pe, ctok, sem("cT_blocks"))
            pe.wait_ge(sem("cT_ready"), 4)
            for half in range(2):
                for c in range(DC):
                    nc.tensor.matmul(bank[4 + 2 * half + c], flip, cT[:, c, half * 512:(half + 1) * 512], start=True,
                                     stop=True).then_inc(sem("cTr_blocks"), 1)
            ln_tensor(pe, 0)
            pe.wait_ge(sem("xnT_ready"), 4)
            pe.wait_ge(sem("toep_loaded"), 16)
            pe.wait_ge(sem("cTr_ready"), 4)
            for h in range(H0):
                s = h % 2
                pe.wait_ge(sem("kv_ready"), DC * (h + 1))
                if h >= 2:
                    pe.wait_ge(sem("prod_ready"), DC * (h - 1))
                nc.tensor.matmul(bank[2 * s][:], toep[:, h, 0:P], kv[:, h % KVS, 0, :], start=True, stop=True)
                nc.tensor.matmul(bank[2 * s + 1][:], toep[:, h, P:L], kv[:, h % KVS, 0, :], start=True, stop=False)
                nc.tensor.matmul(bank[2 * s + 1][:], toep[:, h, 0:P], kv[:, h % KVS, 1, :], start=False,
                                 stop=True).then_inc(sem("conv_done"), 1)
            pe.wait_ge(sem("z_ready"), H0)
            for t in range(NT):
                for c in range(DC):
                    last = nc.tensor.transpose(bank[4 + t // 2][:, (t % 2 * DC + c) * P:(t % 2 * DC + c + 1) * P],
                                               z[:, c, t * P:(t + 1) * P], ident[:])
                last.then_inc(sem("conv_out"), 1)

        def l0x_vector(dve, seq):
            ln_vector(dve, seq, 0)
            dve.wait_ge(sem("xnT_ready"), 4)
            for h in range(H0):
                s = h % 2
                dve.wait_ge(sem("conv_done"), h + 1)
                if h >= 2:
                    dve.wait_ge(sem("z_ready"), h - 1)
                for c in range(DC):
                    q = xnT[:, c, :].rearrange("p (b s) -> p b s", b=NT)[:, :, h * HD0:(h + 1) * HD0]
                    nc.vector.tensor_tensor(prod[:, s, c, :].rearrange("p (b j i) -> p b j i", b=NT, j=HD0),
                                            bank[2 * s + c][:].rearrange("p (b j i) -> p b j i", b=NT, j=HD0),
                                            bcast(q, 2, HD0), ALU.mult).then_inc(sem("prod_ready"), 1)
                dve.wait_ge(sem("prod_ready"), DC * (h + 1))
                nc.vector.tensor_reduce(
                    z.rearrange("p c (b s) -> p (c b) s", b=NT)[:, :, h * HD0:(h + 1) * HD0],
                    prod[:, s].rearrange("p c (b j i) -> p (c b) j i", b=NT, j=HD0),
                    AX.X, ALU.add).then_inc(sem("z_ready"), 1)
            dve.wait_ge(sem("tg_ready"), 1)
            for t in range(0, NT, 2):
                if t:
                    seq.wait()
                    tile_stats(seq, (t - 2, t - 1))
                dve.wait_ge(sem("conv_out"), t + 2)
                seq.mark(nc.vector.scalar_tensor_tensor(x[:, t:t + 2, :].rearrange("p a d -> p (a d)"),
                                                        bank[4 + t // 2][:], tg[:, 0:1],
                                                        x[:, t:t + 2, :].rearrange("p a d -> p (a d)"),
                                                        ALU.mult, ALU.add))
            seq.wait()
            tile_stats(seq, (NT - 2, NT - 1))

        class Moe:

            BIG = 8192.0

            def __init__(self, name, E, K, C, gate, rows_buf, r, stores, earlier=None):
                self.name, self.E, self.K, self.C, self.gate = name, E, K, C, gate
                self.slots = E * C
                self.y_done = 16 * stores
                self.before = earlier.totals() if earlier else {}
                self.blocks = self.slots // P
                self.part = 4 * ((self.blocks + 11) // 12)
                assert self.slots % P == 0
                self.x_dram = nc.dram_tensor(f"{name}_x_dram", [self.slots + K * T, D], F32)
                self.y_dram = nc.dram_tensor(f"{name}_y_dram", [self.slots, D], F32)
                self.rows = rows_buf
                self.rowsT = r.f32(DC, self.slots)
                self.weight = r.f32(NT, E)
                self.sel = r.f32(NT, E)
                self.selb = r.bf16(NT, E)
                self.keep = r.f32(NT, E)
                self.code = r.f32(NT, E)
                self.wkeep = r.f32(NT, E)
                self.code8 = r.f32(NT, 8)
                self.kcode = r.f32(NT, K)
                self.kept = r.f32(NT, K)
                self.slot = r.f32(NT, K)
                self.idx_f = r.f32(NT, K)
                self.match = r.f32(NT, K, E)
                self.kweight = r.f32(NT, K)
                self.gathered = r.f32(8, D)
                self.code_base = sb(f"{name}_code_base", [P, E])
                self.spare = sb(f"{name}_spare", [P, NT, K])
                self.idx_to = sb(f"{name}_idx_to", [P, NT, K], I32)
                self.idx_from = sb(f"{name}_idx_from", [P, NT, K], I32)

            def sem(self, what):
                return sem(f"moe_{what}")

            def wait(self, eng, what, n):
                eng.wait_ge(self.sem(what), n + self.before.get(what, 0))

            def totals(self):
                groups = (self.blocks + 3) // 4 * DC
                return dict(consts=2, sel_ready=1, pos_ready=1, idx_ready=2, cleared=16, scattered=16 * NT * self.K,
                            rowsT_blocks=groups, rowsT_ready=groups, y_stored=self.y_done, added=NT * self.K,
                            **{f"part{n}_loaded": 16 for n in range(3)}, **{f"gathered{n}": 16 * (NT * self.K // 8) for n in range(8)})

            def clear_rows(self, sp):
                sp.wait_ge(sem("small_consts"), 1)
                sp.dma_start(self.x_dram[0:self.slots, :].rearrange("(g p) d -> p g d", p=P),
                             bcast(zeros[:], 1, self.blocks)).then_inc(self.sem("cleared"), 16)

            def constants(self, pool):
                nc.gpsimd.iota(self.code_base[:], pattern=[[-self.C, self.E]], base=int(self.BIG), channel_multiplier=0,
                               allow_small_or_imprecise_dtypes=True).then_inc(self.sem("consts"), 1)
                nc.gpsimd.iota(self.spare[:], pattern=[[P, NT], [T, self.K]], base=self.slots, channel_multiplier=1,
                               allow_small_or_imprecise_dtypes=True).then_inc(self.sem("consts"), 1)

            def positions_tensor(self, pe, ps):
                E = self.E
                self.wait(pe, "sel_ready", 1)
                pe.wait_ge(sem("small_consts"), 2)
                nc.tensor.matmul(ps[:, 0:NT * E], before[:], self.selb.rearrange("p t e -> p (t e)"),
                                 start=True, stop=False, skip_group_check=True)
                for j in range(NT - 1):
                    last = nc.tensor.matmul(ps[:, (j + 1) * E:NT * E], onesb[:], bcast(self.selb[:, j, :], 1, NT - 1 - j),
                                            start=False, stop=(j == NT - 2), skip_group_check=True)
                last.then_inc(self.sem("pos_ready"), 1)

            def slots_vector(self, dve, seq, ps):
                E, K = self.E, self.K
                pos = ps[:, 0:NT * E].rearrange("p (t e) -> p t e", t=NT)
                self.wait(dve, "pos_ready", 1)
                self.wait(dve, "consts", 2)
                seq.mark(nc.vector.scalar_tensor_tensor(self.keep, pos, float(self.C), self.sel, ALU.is_lt, ALU.mult))
                seq.step(nc.vector.scalar_tensor_tensor(self.code, pos, -1.0, bcast(self.code_base[:], 1, NT), ALU.mult, ALU.add))
                seq.mark(nc.vector.tensor_tensor(self.code, self.code, self.keep, ALU.mult))
                seq.step(nc.vector.tensor_tensor(self.wkeep, self.weight, self.keep, ALU.mult))
                for t in range(NT):
                    seq.mark(nc.vector.max(self.code8[:, t, :], self.code[:, t, :]))
                seq.wait()
                seq.step(nc.vector.tensor_copy(self.kcode, self.code8[:, :, 0:K]))
                seq.mark(nc.vector.tensor_scalar(self.kept, self.kcode, 0.0, None, ALU.is_gt))
                seq.step(nc.vector.tensor_scalar(self.slot, self.kcode, -1.0, self.BIG, ALU.mult, ALU.add))
                seq.step(nc.vector.tensor_tensor(self.idx_f, self.slot, self.spare[:], ALU.subtract))
                seq.step(nc.vector.tensor_tensor(self.idx_f, self.idx_f, self.kept, ALU.mult))
                nc.vector.tensor_tensor(self.idx_to[:], self.idx_f, self.spare[:], ALU.add).then_inc(self.sem("idx_ready"), 1)
                nc.vector.tensor_tensor(self.idx_from[:], self.slot, self.kept, ALU.mult).then_inc(self.sem("idx_ready"), 1)
                seq.step(nc.vector.tensor_tensor(self.match, bcast(self.code, 2, K), bcast(self.kcode, 3, E), ALU.is_equal))
                seq.step(nc.vector.tensor_tensor(self.match, self.match, bcast(self.wkeep, 2, K), ALU.mult))
                seq.step(nc.vector.tensor_reduce(self.kweight, self.match, AX.X, ALU.add))
                seq.step(nc.vector.tensor_scalar(self.kweight, self.kweight, tg[:, self.gate:self.gate + 1], None, ALU.mult))

            def scatter_gpsimd(self, pool):
                self.wait(pool, "idx_ready", 2)
                self.wait(pool, "cleared", 16)
                for t in range(NT):
                    for k in range(self.K):
                        nc.gpsimd.indirect_dma_start(
                            out=self.x_dram[:, :], out_offset=bass.IndirectOffsetOnAxis(ap=self.idx_to[:, t, k:k + 1], axis=0),
                            in_=xn[:, t, :], in_offset=None).then_inc(self.sem("scattered"), 16)

            def load_rows_sync(self, sp):
                self.wait(sp, "scattered", 16 * NT * self.K)
                rows = self.x_dram[0:self.slots, :].rearrange("(g p) d -> p g d", p=P)
                for n in range(3):
                    some = slice(self.part * n, min(self.part * (n + 1), self.blocks))
                    sp.dma_start(self.rows[:, some, :], rows[:, some, :]).then_inc(self.sem(f"part{n}_loaded"), 16)

            def rows_tensor(self, pe):
                n = 0
                for g0 in range(0, self.blocks, 4):
                    self.wait(pe, f"part{g0 // self.part}_loaded", 16)
                    for c in range(DC):
                        if n >= 2:
                            self.wait(pe, "rowsT_ready", n - 1)
                        for g in range(g0, min(g0 + 4, self.blocks)):
                            last = nc.tensor.transpose(bank[2 + n % 2][:, (g - g0) * P:(g - g0 + 1) * P],
                                                       self.rows[:, g, c * P:(c + 1) * P], ident[:])
                        last.then_inc(self.sem("rowsT_blocks"), 1)
                        n += 1
                self.wait(pe, "rowsT_ready", n)

            def rows_scalar(self, act):
                n = 0
                for g0 in range(0, self.blocks, 4):
                    for c in range(DC):
                        self.wait(act, "rowsT_blocks", n + 1)
                        w = min(4, self.blocks - g0) * P
                        nc.scalar.copy(self.rowsT[:, c, g0 * P:g0 * P + w], bank[2 + n % 2][:, 0:w]).then_inc(self.sem("rowsT_ready"), 1)
                        n += 1

            def gather_gpsimd(self, pool):
                if self.y_done:
                    self.wait(pool, "y_stored", self.y_done)
                n = 0
                for t in range(NT):
                    for k in range(self.K):
                        if n >= 8:
                            self.wait(pool, "added", n - 7)
                        nc.gpsimd.indirect_dma_start(
                            out=self.gathered[:, n % 8, :], out_offset=None, in_=self.y_dram[:, :],
                            in_offset=bass.IndirectOffsetOnAxis(ap=self.idx_from[:, t, k:k + 1], axis=0))\
                            .then_inc(self.sem(f"gathered{n % 8}"), 16)
                        n += 1

            def combine_vector(self, dve, first=0, end=None, seq=None):
                end = end or NT * self.K
                n = first
                for t in range(NT):
                    for k in range(self.K):
                        if not first <= t * self.K + k < end:
                            continue
                        self.wait(dve, f"gathered{n % 8}", 16 * (n // 8 + 1))
                        if k:
                            self.wait(dve, "added", n)
                        nc.vector.scalar_tensor_tensor(x[:, t, :], self.gathered[:, n % 8, :], self.kweight[:, t, k:k + 1],
                                                       x[:, t, :], ALU.mult, ALU.add).then_inc(self.sem("added"), 1)
                        n += 1
                        if seq and k == self.K - 1:
                            self.wait(dve, "added", n)
                            tile_stats(seq, (t,))
                self.wait(dve, "added", n)

        class Dense:

            def __init__(self, name, n, gate, w, loaded, hid, scratch, scale=None, earlier=0, ends=False):
                self.name, self.n, self.gate, self.w, self.loaded = name, n, gate, w, loaded
                self.hid, self.scratch, self.scale, self.earlier = hid, scratch, scale, earlier
                self.ends = ends

            def sem(self, what):
                return sem(f"dense_{what}")

            def wait(self, eng, what, n):
                per_chunk = 4 if what in ("down_done", "x_added") else 2
                eng.wait_ge(self.sem(what), n + per_chunk * self.earlier)

            def up_tensor(self, pe, m):
                w = self.w(m)
                self.loaded(pe, m)
                for half in range(2):
                    u = 2 * m + half
                    if u >= 2:
                        self.wait(pe, "h_ready", u - 1)
                    for j in range(2):
                        for c in range(DC):
                            last = nc.tensor.matmul(bank[2 * half + j][:], w[:, (j * DC + c) * P:(j * DC + c + 1) * P],
                                                    xnT[:, c, half * 512:(half + 1) * 512], start=(c == 0), stop=(c == DC - 1))
                    last.then_inc(self.sem("up_done"), 1)

            def down_tensor(self, pe, m):
                w = self.w(m)
                for half in range(2):
                    self.wait(pe, "h_ready", 2 * m + half + 1)
                    for t2 in range(2):
                        v = 4 * m + 2 * half + t2
                        if v >= 4:
                            self.wait(pe, "x_added", v - 3)
                        for i in range(2):
                            t = half * 4 + t2 * 2 + i
                            last = nc.tensor.matmul(bank[4 + v % 4][:, i * D:(i + 1) * D], self.hid[:, m % 2, t * P:(t + 1) * P],
                                                    w[:, 2 * DC * P:2 * DC * P + D], start=True, stop=True)
                        last.then_inc(self.sem("down_done"), 1)

            def tensor(self, pe):
                for m in range(self.n + 1):
                    if m < self.n:
                        self.up_tensor(pe, m)
                    if m:
                        self.down_tensor(pe, m - 1)

            def scalar(self, act):
                for m in range(self.n):
                    for half in range(2):
                        u = 2 * m + half
                        self.wait(act, "up_done", u + 1)
                        if u >= 2:
                            self.wait(act, "h_ready", u - 1)
                        nc.scalar.activation(self.scratch[:, half, :], bank[2 * half][:], ACT.Silu).then_inc(self.sem("silu_done"), 1)

            def vector(self, dve, seq):
                def up(m):
                    for half in range(2):
                        u = 2 * m + half
                        self.wait(dve, "silu_done", u + 1)
                        if m >= 2:
                            self.wait(dve, "down_done", 4 * (m - 2) + 2 * half + 2)
                        nc.vector.tensor_tensor(self.hid[:, m % 2, half * 512:(half + 1) * 512], self.scratch[:, half, :],
                                                bank[2 * half + 1][:], ALU.mult).then_inc(self.sem("h_ready"), 1)

                def down(m):
                    for v in range(4 * m, 4 * m + 4):
                        t = 2 * (v % 4)
                        if self.ends and m == self.n - 1 and t:
                            self.wait(dve, "x_added", v)
                            tile_stats(seq, (t - 2, t - 1))
                        self.wait(dve, "down_done", v + 1)
                        if v >= 4:
                            self.wait(dve, "x_added", v - 3)
                        if self.scale is None:
                            nc.vector.scalar_tensor_tensor(x[:, t:t + 2, :].rearrange("p a d -> p (a d)"), bank[4 + v % 4][:],
                                                           tg[:, self.gate:self.gate + 1],
                                                           x[:, t:t + 2, :].rearrange("p a d -> p (a d)"),
                                                           ALU.mult, ALU.add).then_inc(self.sem("x_added"), 1)
                        else:
                            for i in range(2):
                                ins = nc.vector.scalar_tensor_tensor(x[:, t + i, :], bank[4 + v % 4][:, i * D:(i + 1) * D],
                                                                     self.scale(m, t + i), x[:, t + i, :], ALU.mult, ALU.add)
                                if i == 0:
                                    seq.mark(ins)
                            seq.wait()
                            ins.then_inc(self.sem("x_added"), 1)

                for m in range(self.n + 1):
                    if m < self.n:
                        up(m)
                    if m:
                        down(m - 1)
                self.wait(dve, "x_added", 4 * self.n)
                if self.ends:
                    tile_stats(seq, (NT - 2, NT - 1))

        zeros = sb("zeros", [P, D])
        before = sb("before", [P, P], BF16)
        rw0 = sb("rw0", [P, DC, 32])
        ebias = sb("ebias", [P, 32])
        SH0 = sb("sh0", [P, 2, 768])
        E0, K0, C0, NG0, TOPG = 32, 4, 40, 8, 3
        GE = E0 // NG0
        r = Region(arena, ARENA)
        moe0 = Moe("moe0", E0, K0, C0, 4, r.f32(E0 * C0 // P, D), r, 4)
        scores0 = r.f32(NT, E0)
        biased = r.f32(NT, E0)
        gtmp = [r.f32(NT * NG0) for _ in range(8)]
        NONE, TAKEN = -3.0e38, 3.0e38
        gval = r.f32(NT, 2 * NG0)
        gtop = r.f32(NT, 8)
        grep = r.f32(NT, 2 * NG0)
        gmask = r.f32(NT, NG0)
        mval = r.f32(NT, E0 + 8)
        mtop = r.f32(NT, 8)
        mrep = r.f32(NT, E0 + 8)
        wsum = r.f32(NT)
        sh_hid = r.f32(2, T)
        sh_scr = r.f32(2, 512)
        exp_x = r.f32(4, DC, C0)
        exp_s = r.f32(2, P)
        exp_h = r.f32(2, P)
        exp_hT = r.f32(2, C0)
        y0 = r.f32(E0, D)
        RING0 = 8
        w0 = wring[:, 0:RING0 * 768].rearrange("p (s n) -> p s n", s=RING0)

        def dense_small_loaded(pe, m):
            pe.wait_ge(sem("l0f_small_loaded"), 16 * 3)

        shared0 = Dense("shared0", 2, 4, lambda m: SH0[:, m, :], dense_small_loaded, sh_hid, sh_scr)

        def l0f_sync(sp):
            sp.dma_start(rw0[:], A["l0_router"].rearrange("(c p) e -> p c e", p=P)).then_inc(sem("l0f_small_loaded"), 16)
            sp.dma_start(ebias[:], A["l0_ebias"].rearrange("(o n) -> o n", o=1).to_broadcast([P, E0])).then_inc(sem("l0f_small_loaded"), 16)
            sp.dma_start(SH0[:], A["l0_shared"].rearrange("m p n -> p m n")).then_inc(sem("l0f_small_loaded"), 16)
            moe0.clear_rows(sp)
            for s in range(RING0):
                sp.dma_start(w0[:, s, :], A["l0_experts"][s]).then_inc(sem(f"ring_loaded{s}"), 16)

        def l0f_sync2(sp):
            moe0.load_rows_sync(sp)
            with sp.Fori(1, E0 // RING0) as it:
                for s in range(RING0):
                    sp.wait_ge(sem("w0_used"), (it - 1) * RING0 + s + 1)
                    sp.dma_start(w0[:, s, :], A["l0_experts"][bass.ds(it * RING0 + s, 1)].rearrange("o p n -> p (o n)"))\
                      .then_inc(sem(f"ring_loaded{s}"), 16)

        def l0f_gpsimd(pool):
            nc.gpsimd.memset(zeros[:], 0.0).then_inc(sem("small_consts"), 1)
            nc.gpsimd.affine_select(out=before[:], in_=onesb[:], compare_op=ALU.is_ge, fill=0.0, base=-1,
                                    pattern=[[1, P]], channel_multiplier=-1).then_inc(sem("small_consts"), 1)
            moe0.constants(pool)

        def l0f_gpsimd2(pool):
            moe0.scatter_gpsimd(pool)
            moe0.gather_gpsimd(pool)

        def l0f_tensor(pe):
            ln_tensor(pe, 1)
            pe.wait_ge(sem("xnT_ready"), 8)
            pe.wait_ge(sem("l0f_small_loaded"), 48)
            for t in range(NT):
                for c in range(DC):
                    last = nc.tensor.matmul(bank[4][:, t * E0:(t + 1) * E0], xnT[:, c, t * P:(t + 1) * P], rw0[:, c, :],
                                            start=(c == 0), stop=(c == DC - 1))
            last.then_inc(sem("router0_done"), 1)
            moe0.positions_tensor(pe, bank[5])
            moe0.wait(pe, "idx_ready", 2)
            shared0.tensor(pe)
            l1x_values_tensor(pe)
            moe0.rows_tensor(pe)
            with pe.Fori(0, E0 // RING0) as it:
                def up(s):
                    e = it * RING0 + s
                    pe.wait_ge(sem(f"ring_loaded{s}"), (it + 1) * 16)
                    pe.wait_ge(sem("exp_x_ready"), e + 1)
                    if s >= 2:
                        pe.wait_ge(sem("h0_ready"), e - 1)
                    w = w0[:, s, 0:2 * DC * P].rearrange("p (j c n) -> p j c n", j=2, c=DC)
                    for c in range(DC):
                        last = nc.tensor.matmul(bank[s % 2][0:C0, 0:2 * P].rearrange("p (j n) -> p j n", j=2), exp_x[:, s % 4, c, :],
                                                w[:, :, c, :], start=(c == 0), stop=(c == DC - 1))
                    last.then_inc(sem("up0_done"), 1)

                def turn(s):
                    e = it * RING0 + s
                    pe.wait_ge(sem("h0_ready"), e + 1)
                    if s >= 2:
                        pe.wait_ge(sem("hT0_ready"), e - 1)
                    nc.tensor.transpose(bank[4 + s % 2][:, 0:P], exp_h[:, s % 2, :], ident[:]).then_inc(sem("h0_turned"), 1)

                def down(s):
                    e = it * RING0 + s
                    pe.wait_ge(sem("hT0_ready"), e + 1)
                    if s >= 2:
                        pe.wait_ge(sem("y0_ready"), e - 1)
                    nc.tensor.matmul(bank[2 + s % 2][0:C0, 0:D], exp_hT[:, s % 2, :], w0[:, s, 2 * DC * P:2 * DC * P + D],
                                     start=True, stop=True).then_inc(sem("w0_used"), 1)

                for s in range(RING0 + 2):
                    if s < RING0:
                        up(s)
                    if 1 <= s <= RING0:
                        turn(s - 1)
                    if s >= 2:
                        down(s - 2)
                pe.wait_ge(sem("y0_ready"), it * RING0 + RING0)

        def l0f_scalar(act):
            ln_scalar(act, 1)
            act.wait_ge(sem("router0_done"), 1)
            nc.scalar.activation(scores0.rearrange("p t e -> p (t e)"), bank[4][:, 0:NT * E0], ACT.Sigmoid).then_inc(sem("scores0_ready"), 1)
            shared0.scalar(act)
            l1x_values_scalar(act)
            moe0.rows_scalar(act)
            with act.Fori(0, E0 // RING0) as it:
                for s in range(RING0 + 2):
                    e = it * RING0 + s
                    if s < RING0:
                        act.wait_ge(sem("up0_done"), e + 1)
                        if s >= 2:
                            act.wait_ge(sem("h0_ready"), e - 1)
                        nc.scalar.activation(exp_s[0:C0, s % 2, :], bank[s % 2][0:C0, 0:P], ACT.Silu).then_inc(sem("silu0_done"), 1)
                    if s >= 2:
                        act.wait_ge(sem("w0_used"), e - 1)
                        nc.scalar.copy(y0[0:C0, bass.ds(e - 2, 1), :].rearrange("p o d -> p (o d)"), bank[2 + s % 2][0:C0, 0:D])\
                          .then_inc(sem("y0_ready"), 1)
                act.wait_ge(sem("y0_ready"), it * RING0 + RING0)
                act.dma_start(moe0.y_dram[bass.ds(it * RING0 * C0, RING0 * C0), :].rearrange("(e c) d -> c e d", c=C0),
                              y0[0:C0, bass.ds(it * RING0, RING0), :]).then_inc(moe0.sem("y_stored"), 16)

        def l0f_vector(dve, seq):
            ln_vector(dve, seq, 1)
            dve.wait_ge(sem("scores0_ready"), 1)
            dve.wait_ge(sem("l0f_small_loaded"), 48)
            seq.mark(nc.vector.memset(gval[:, :, NG0:2 * NG0], NONE))
            seq.mark(nc.vector.memset(mval[:, :, E0:E0 + 8], NONE))
            seq.step(nc.vector.tensor_tensor(biased, scores0, bcast(ebias[:], 1, NT), ALU.add))
            m = biased.rearrange("p t (g m) -> p (t g) m", m=GE)
            hi1, lo1, hi2, lo2, top, mid, low, second = gtmp
            seq.mark(nc.vector.tensor_tensor(hi1, m[:, :, 0], m[:, :, 1], ALU.max))
            seq.mark(nc.vector.tensor_tensor(lo1, m[:, :, 0], m[:, :, 1], ALU.min))
            seq.mark(nc.vector.tensor_tensor(hi2, m[:, :, 2], m[:, :, 3], ALU.max))
            seq.step(nc.vector.tensor_tensor(lo2, m[:, :, 2], m[:, :, 3], ALU.min))
            seq.mark(nc.vector.tensor_tensor(top, hi1, hi2, ALU.max))
            seq.mark(nc.vector.tensor_tensor(mid, hi1, hi2, ALU.min))
            seq.step(nc.vector.tensor_tensor(low, lo1, lo2, ALU.max))
            seq.step(nc.vector.tensor_tensor(second, mid, low, ALU.max))
            seq.step(nc.vector.tensor_tensor(gval[:, :, 0:NG0], top.rearrange("p (t g) -> p t g", t=NT),
                                             second.rearrange("p (t g) -> p t g", t=NT), ALU.add))
            top_mask(seq, gval, gtop, grep, NG0, TOPG, gmask)
            seq.step(nc.vector.tensor_tensor(mval[:, :, 0:E0].rearrange("p t (g m) -> p t g m", m=GE),
                                             biased.rearrange("p t (g m) -> p t g m", m=GE), bcast(gmask, 3, GE), ALU.mult))
            seq.step(nc.vector.tensor_scalar(mval[:, :, 0:E0], mval[:, :, 0:E0], 0.0, None, ALU.add))
            top_mask(seq, mval, mtop, mrep, E0, K0, moe0.sel)
            nc.vector.tensor_copy(moe0.selb, moe0.sel).then_inc(moe0.sem("sel_ready"), 1)
            seq.step(nc.vector.tensor_tensor(moe0.weight, moe0.sel, scores0, ALU.mult))
            seq.step(nc.vector.tensor_reduce(wsum, moe0.weight, AX.X, ALU.add))
            seq.step(nc.vector.tensor_scalar(wsum, wsum, 1e-20, None, ALU.add))
            seq.step(nc.vector.reciprocal(wsum, wsum))
            seq.step(nc.vector.scalar_tensor_tensor(moe0.weight, moe0.weight, 2.5, bcast(wsum, 2, E0), ALU.mult, ALU.mult))
            moe0.slots_vector(dve, seq, bank[5])
            shared0.vector(dve, seq)
            l1x_values_vector(dve, seq)
            seq.step(nc.vector.memset(exp_h, 0.0))
            moe0.wait(dve, "rowsT_ready", (moe0.blocks + 3) // 4 * DC)
            with dve.Fori(0, E0 // RING0) as it:
                def slots(s):
                    nc.vector.tensor_copy(exp_x[:, s % 4], moe0.rowsT[:, :, bass.ds((it * RING0 + s) * C0, C0)]).then_inc(sem("exp_x_ready"), 1)

                slots(0)
                slots(1)
                for s in range(RING0 + 1):
                    e = it * RING0 + s
                    if s + 2 < RING0:
                        slots(s + 2)
                    if s < RING0:
                        dve.wait_ge(sem("silu0_done"), e + 1)
                        if s >= 2:
                            dve.wait_ge(sem("h0_turned"), e - 1)
                        nc.vector.tensor_tensor(exp_h[0:C0, s % 2, :], exp_s[0:C0, s % 2, :], bank[s % 2][0:C0, P:2 * P], ALU.mult)\
                          .then_inc(sem("h0_ready"), 1)
                    if s:
                        dve.wait_ge(sem("h0_turned"), e)
                        if s >= 3:
                            dve.wait_ge(sem("w0_used"), e - 2)
                        nc.vector.tensor_copy(exp_hT[:, (s - 1) % 2, :], bank[4 + (s - 1) % 2][:, 0:C0]).then_inc(sem("hT0_ready"), 1)
            combine0_vector(dve, seq)

        def top_mask(seq, val, top8, rep, n, k, mask):
            for t in range(NT):
                seq.mark(nc.vector.max(top8[:, t, :], val[:, t, 0:n]))
            seq.wait()
            seq.step(nc.vector.memset(top8[:, :, k:8], NONE))
            for t in range(NT):
                seq.mark(nc.vector.match_replace(rep[:, t, :], top8[:, t, :], val[:, t, :], TAKEN))
            seq.wait()
            seq.step(nc.vector.tensor_scalar(mask, rep[:, :, 0:n], TAKEN, None, ALU.is_equal))

        H2, HD2 = 16, 16
        ROWS = 64
        LN255 = 5.541263545158426
        wq2 = sb("wq2", [P, DC, D])
        wkv2 = sb("wkv2", [P, DC, 2 * D])
        wp2 = sb("wp2", [P, DC, D])
        bqk2 = sb("bqk2", [P, 2, D])
        bv2 = sb("bv2", [P, DC])
        bp2 = sb("bp2", [1, D])
        sv2 = sb("sv2", [P, DC])
        isv2 = sb("isv2", [P, DC])
        ones_row = sb("ones_row", [1, P])
        r = Region(arena, ARENA)
        qT2 = r.bf16(H2 // 2, T)
        kT2 = r.bf16(H2 // 2, T)
        v2 = r.bf16(NT, D)
        am2 = r.f32(NT * H2)
        s2 = r.f32(NT * H2)
        is2 = r.f32(NT * H2)
        zs2 = r.f32(H2, NT)
        rz2 = r.f32(H2, NT)
        nmax2 = r.f32(H2 * NT)
        bias2 = r.f32(H2 * NT)
        rv = Region(wring, 10 * 1024)
        rv.at = RING0 * 768
        vT2 = rv.f32(DC, T)
        vi2 = rv.bf16(DC, T)
        amk2 = rv.f32(NT * H2)
        sk2 = rv.f32(NT * H2)
        isk2 = rv.f32(NT * H2)
        rv = Region(wring, RING0 * 768)
        kf2 = rv.f32(NT, D)
        ka2 = rv.bf16(NT, H2, ROWS)
        overlay = r.at
        qf2 = r.f32(NT, D)
        qa2 = r.bf16(NT, H2, ROWS)
        r = Region(arena, ARENA)
        r.at = overlay
        SLOTS2 = 3
        e2 = r.f32(SLOTS2, T)
        r2 = r.bf16(SLOTS2, T)
        rT2 = r.bf16(SLOTS2, T)
        o2 = r.f32(NT, D)
        oT2 = r.f32(DC, T)

        def bf(i):
            return bank[i].bitcast(BF16)

        GH2 = 512 // (NT * HD2)

        def l1x_sync(sp):
            for dst, src in ((wq2[:], A["l1_wq"].rearrange("(c p) n -> p c n", p=P)),
                             (wkv2[:], A["l1_wkv"].rearrange("(c p) n -> p c n", p=P)),
                             (wp2[:], A["l1_wp"].rearrange("(c p) n -> p c n", p=P)),
                             (bqk2[:, 0, :], A["l1_bq"].rearrange("(o n) -> o n", o=1).to_broadcast([P, D])),
                             (bqk2[:, 1, :], A["l1_bkv"][0:D].rearrange("(o n) -> o n", o=1).to_broadcast([P, D])),
                             (bv2[:], A["l1_bv"]),
                             (bp2[:], A["l1_bp"].rearrange("(o n) -> o n", o=1))):
                sp.dma_start(dst, src).then_inc(sem("l1x_loaded"), 16)

        L1X_LOADS = 16 * 7

        def l1x_gpsimd(pool):
            nc.gpsimd.memset(ones_row[:], 1.0).then_inc(sem("small_consts"), 1)
            moe0.wait(pool, "added", NT * K0)
            nc.gpsimd.memset(qa2.rearrange("p t h r -> p (t h) r")[:, :, 3 * HD2:ROWS], 0.0).then_inc(sem("pads2_ready"), 1)

        def copied_by_vector(n):
            return n > H2 // 2 and n % 2 == 1

        def pair_copied(eng, n):
            of_vector = sum(copied_by_vector(m) for m in range(n + 1))
            if copied_by_vector(n):
                eng.wait_ge(sem("qT2_ready"), of_vector)
            else:
                eng.wait_ge(sem("qkT2_ready"), n + 1 - of_vector)

        def l1x_values_tensor(pe):
            pe.wait_ge(sem("l1x_loaded"), L1X_LOADS)
            for f in range(DC):
                for half in range(2):
                    for c in range(DC):
                        last = nc.tensor.matmul(bank[2 * f + half], wkv2[:, c, D + f * P:D + (f + 1) * P],
                                                cT[:, c, half * 512:(half + 1) * 512], start=(c == 0), stop=(c == DC - 1))
                    last.then_inc(sem("v2_done"), 1)
            pe.wait_ge(sem("vf2_ready"), 4)

        def l1x_tensor(pe):
            def project(first, src, w):
                for t in range(NT):
                    for c in range(DC):
                        last = nc.tensor.matmul(bank[first + t // 2][:, t % 2 * D:(t % 2 + 1) * D], src[:, c, t * P:(t + 1) * P],
                                                w[:, c, :], start=(c == 0), stop=(c == DC - 1))
                    if t % 2:
                        last.then_inc(sem("qk2_done"), 1)

            def turn_pairs(src, numbers):
                for n in numbers:
                    if n >= 4:
                        pair_copied(pe, n - 4)
                    for t in range(NT):
                        last = nc.tensor.transpose(bf(4 + n % 4)[:, t * P:(t + 1) * P],
                                                   src[:, t, 2 * (n % 8):2 * (n % 8) + 2, :].rearrange("p a b -> p (a b)"), identb[:])
                    last.then_inc(sem("qkT2_blocks"), 1)

            project(4, cT, wkv2[:, :, 0:D])
            pe.wait_ge(sem("ka2_ready"), 1)
            turn_pairs(ka2, range(4))
            ln_tensor(pe, 2)
            pe.wait_ge(sem("xnT_ready"), 12)
            project(0, xnT, wq2[:])
            turn_pairs(ka2, range(4, H2 // 2))
            pe.wait_ge(sem("qkf2_ready"), 8)
            for t in range(NT):
                for c in range(DC):
                    last = nc.tensor.transpose(bf(t // 4)[:, (t % 4 * DC + c) * P:(t % 4 * DC + c + 1) * P],
                                               vi2[:, c, t * P:(t + 1) * P], identb[:])
                if t % 4 == 3:
                    last.then_inc(sem("v2_blocks"), 1)
            pe.wait_ge(sem("pads2_ready"), 1)
            pe.wait_ge(sem("qa2_ready"), 2)
            turn_pairs(qa2, range(H2 // 2, H2))
            pe.wait_ge(sem("v2_ready"), 2)
            pair_copied(pe, H2 - 2)
            pair_copied(pe, H2 - 1)

            def scores(n):
                h, t = n // NT, n % NT
                lo = ROWS * (h % 2)
                if n >= 2:
                    pe.wait_ge(sem("e2_ready"), n - 1)
                for half in range(2):
                    last = nc.tensor.matmul(bank[2 * (n % 2) + half], qT2[lo:lo + 3 * HD2, h // 2, t * P:(t + 1) * P],
                                            kT2[lo:lo + 3 * HD2, h // 2, half * 512:(half + 1) * 512], start=True, stop=True)
                last.then_inc(sem("scores2_done"), 1)

            def turn(n):
                pe.wait_ge(sem("r2_ready"), n + 1)
                if n >= SLOTS2:
                    pe.wait_ge(sem("rT2_ready"), n - SLOTS2 + 1)
                for j in range(NT):
                    last = nc.tensor.transpose(bf(4 + n % SLOTS2)[:, j * P:(j + 1) * P], r2[:, n % SLOTS2, j * P:(j + 1) * P], identb[:])
                last.then_inc(sem("rT2_blocks"), 1)

            def values(n):
                h, t = n // NT, n % NT
                pe.wait_ge(sem("rT2_ready"), n + 1)
                if t == 0 and h % GH2 == 0 and h:
                    pe.wait_ge(sem("o2_ready"), h // GH2)
                for j in range(NT):
                    last = nc.tensor.matmul(bank[7][:, (h % GH2 * NT + t) * HD2:(h % GH2 * NT + t + 1) * HD2], rT2[:, n % SLOTS2, j * P:(j + 1) * P],
                                            v2[:, j, h * HD2:(h + 1) * HD2], start=(j == 0), stop=(j == NT - 1))
                last.then_inc(sem("values2_done"), 1)

            U = H2 * NT
            for n in range(U + 4):
                if n < U:
                    scores(n)
                if 2 <= n < U + 2:
                    turn(n - 2)
                if n >= 4:
                    values(n - 4)
            pe.wait_ge(sem("o2_ready"), H2 // GH2)
            pe.wait_ge(sem("small_consts"), 3)
            transpose_T(pe, o2, sem("oT2_blocks"))
            pe.wait_ge(sem("oT2_ready"), 4)
            for t in range(NT):
                ps = bank[4 + t // 2][:, t % 2 * D:(t % 2 + 1) * D]
                nc.tensor.matmul(ps, ones_row[:], bp2[:], start=True, stop=False)
                for c in range(DC):
                    last = nc.tensor.matmul(ps, oT2[:, c, t * P:(t + 1) * P], wp2[:, c, :], start=False, stop=(c == DC - 1))
                if t % 2:
                    last.then_inc(sem("proj2_done"), 1)

        def l1x_values_scalar(act):
            act.wait_ge(sem("l1x_loaded"), L1X_LOADS)
            for f in range(DC):
                for half in range(2):
                    act.wait_ge(sem("v2_done"), 2 * f + half + 1)
                    nc.scalar.activation(vT2[:, f, half * 512:(half + 1) * 512], bank[2 * f + half], ACT.Identity,
                                         bias=bv2[:, f:f + 1]).then_inc(sem("vf2_ready"), 1)

        def l1x_scalar(act):
            kd = kf2.rearrange("p t (h d) -> p (t h) d", h=H2)
            ka = ka2.rearrange("p t h r -> p (t h) r")
            for i in range(2):
                act.wait_ge(sem("kd2_ready"), i + 1)
                nc.scalar.copy(ka[:, :, i * HD2:(i + 1) * HD2], kd).then_inc(sem("ka2_high"), 1)

            def copy_pairs(numbers):
                for n in numbers:
                    if not copied_by_vector(n):
                        act.wait_ge(sem("qkT2_blocks"), n + 1)
                        dst = (kT2 if n < H2 // 2 else qT2)[:, n % 8, :]
                        nc.scalar.copy(dst, bf(4 + n % 4)).then_inc(sem("qkT2_ready"), 1)

            ln_scalar(act, 2, lambda: copy_pairs(range(4)))
            copy_pairs(range(4, H2 // 2))
            for b in range(2):
                act.wait_ge(sem("v2_blocks"), b + 1)
                nc.scalar.copy(v2[:, 4 * b:4 * b + 4, :].rearrange("p t d -> p (t d)"), bf(b)).then_inc(sem("v2_ready"), 1)
            copy_pairs(range(H2 // 2, H2))

            def exp(n):
                h, t = n // NT, n % NT
                act.wait_ge(sem("bias2_ready"), n + 1)
                if n >= SLOTS2:
                    act.wait_ge(sem("r2_ready"), n - SLOTS2 + 1)
                nc.scalar.activation(e2[:, n % SLOTS2, :], psum[:, n % 2 * T:(n % 2 + 1) * T], ACT.Exp, bias=bias2[:, n:n + 1],
                                     scale=s2[:, t * H2 + h:t * H2 + h + 1], accum_out=zs2[:, h, t:t + 1]).then_inc(sem("e2_ready"), 1)

            def copy_T(n):
                act.wait_ge(sem("rT2_blocks"), n + 1)
                if n >= SLOTS2:
                    act.wait_ge(sem("values2_done"), n - SLOTS2 + 1)
                nc.scalar.copy(rT2[:, n % SLOTS2, :], bf(4 + n % SLOTS2)).then_inc(sem("rT2_ready"), 1)

            U = H2 * NT
            for n in range(U + 2):
                if n < U:
                    exp(n)
                if n >= 2:
                    copy_T(n - 2)
            for half in range(2):
                for c in range(DC):
                    act.wait_ge(sem("oT2_blocks"), 2 * half + c + 1)
                    nc.scalar.activation(oT2[:, c, half * 512:(half + 1) * 512], bank[2 * half + c], ACT.Copy,
                                         scale=sv2[:, c:c + 1]).then_inc(sem("oT2_ready"), 1)

        def l1x_values_vector(dve, seq):
            dve.wait_ge(sem("vf2_ready"), 4)
            seq.step(nc.vector.tensor_reduce(sv2[:], vT2, AX.X, ALU.max, apply_absolute_value=True))
            seq.step(nc.vector.tensor_scalar(sv2[:], sv2[:], 1.0 / 127.0, 1e-8, ALU.mult, ALU.max))
            seq.step(nc.vector.reciprocal(isv2[:], sv2[:]))
            for c in range(DC):
                seq.mark(nc.vector.tensor_scalar(vT2[:, c, :], vT2[:, c, :], isv2[:, c:c + 1], MAGIC, ALU.mult, ALU.add))
            seq.wait()
            nc.vector.tensor_scalar(vi2, vT2, MAGIC, None, ALU.subtract).then_inc(sem("vi2_ready"), 1)

        def take2(dve, seq, j, dst, first, n, banks=4):
            for b in range(banks):
                dve.wait_ge(sem("qk2_done"), n + b + 1)
                seq.mark(nc.vector.tensor_tensor(dst[:, 2 * b:2 * b + 2, :], bank[first + b].rearrange("p (a d) -> p a d", a=2),
                                                 bcast(bqk2[:, j, :], 1, 2), ALU.add))
            seq.wait()
            nc.vector.engine_nop().then_inc(sem("qkf2_ready"), banks)

        def steps2(seq, src, am, s, inv, scale):
            seq.step(nc.vector.tensor_reduce(am, src.rearrange("p t (h d) -> p (t h) d", h=H2), AX.X, ALU.max, apply_absolute_value=True))
            seq.step(nc.vector.tensor_scalar(s, am, scale / 127.0, 1e-8, ALU.mult, ALU.max))
            seq.step(nc.vector.reciprocal(inv, s))
            if scale != 1.0:
                seq.step(nc.vector.tensor_scalar(inv, inv, scale, None, ALU.mult))

        def times2(src, by):
            v3 = src.rearrange("p t (h d) -> p (t h) d", h=H2)
            return nc.vector.tensor_tensor(v3, v3, bcast(by, 2, HD2), ALU.mult)

        def round2(src):
            flat = src.rearrange("p t d -> p (t d)")
            return nc.vector.tensor_scalar(flat, flat, MAGIC, MAGIC, ALU.add, ALU.subtract)

        def combine0_vector(dve, seq):
            k3 = kf2.rearrange("p t (h d) -> p (t h) d", h=H2)
            ka = ka2.rearrange("p t h r -> p (t h) r")

            def part(i):
                dve.wait_ge(sem("ka2_high"), i + 1)
                dve.wait_ge(sem("kd2_ready"), i + 1)
                return nc.vector.tensor_tensor(k3 if i == 0 else ka[:, :, 2 * HD2:3 * HD2], k3,
                                               ka[:, :, i * HD2:(i + 1) * HD2], ALU.subtract)

            meanwhile = (
                (2, lambda: seq.mark(nc.vector.memset(ka[:, :, 3 * HD2:ROWS], 0.0))),
                (4, lambda: take2(dve, seq, 1, kf2, 4, 0)),
                (8, lambda: steps2(seq, kf2, amk2, sk2, isk2, 1.0)),
                (13, lambda: seq.step(times2(kf2, isk2))),
                (16, lambda: seq.step(round2(kf2))),
                (19, lambda: times2(kf2, sk2).then_inc(sem("kd2_ready"), 1)),
                (24, lambda: part(0).then_inc(sem("kd2_ready"), 1)),
                (29, lambda: part(1).then_inc(sem("ka2_ready"), 1)))
            done = 0
            for n, step in meanwhile:
                moe0.combine_vector(dve, done, n, seq)
                step()
                done = n
            moe0.combine_vector(dve, done, seq=seq)

        def l1x_vector(dve, seq):
            ln_vector(dve, seq, 2)
            for half in range(2):
                four, some = slice(4 * half, 4 * half + 4), slice(4 * half * H2, (4 * half + 4) * H2)
                qf = qf2[:, four, :]
                take2(dve, seq, 0, qf, 2 * half, 4 + 2 * half, 2)
                steps2(seq, qf, am2[:, some], s2[:, some], is2[:, some], HD2 ** -0.5)
                seq.step(times2(qf, is2[:, some]))
                seq.step(round2(qf))
                nc.vector.tensor_copy(qa2[:, four, :, 0:3 * HD2].rearrange("p t h (a d) -> p (t h) a d", a=3),
                                      bcast(qf.rearrange("p t (h d) -> p (t h) d", h=H2), 2, 3)).then_inc(sem("qa2_ready"), 1)
            for n in range(H2):
                if copied_by_vector(n):
                    dve.wait_ge(sem("qkT2_blocks"), n + 1)
                    nc.vector.tensor_copy(qT2[:, n % 8, :], bf(4 + n % 4)).then_inc(sem("qT2_ready"), 1)

            def top(n):
                h, t = n // NT, n % NT
                dve.wait_ge(sem("scores2_done"), n + 1)
                seq.step(nc.vector.tensor_reduce(nmax2[:, n:n + 1], psum[:, n % 2 * T:(n % 2 + 1) * T], AX.X, ALU.max, negate=True))
                nc.vector.tensor_scalar(bias2[:, n:n + 1], nmax2[:, n:n + 1], s2[:, t * H2 + h:t * H2 + h + 1], LN255,
                                        ALU.mult, ALU.add).then_inc(sem("bias2_ready"), 1)

            def to_integers(n):
                dve.wait_ge(sem("e2_ready"), n + 1)
                if n >= SLOTS2:
                    dve.wait_ge(sem("rT2_blocks"), n - SLOTS2 + 1)
                nc.vector.tensor_scalar(r2[:, n % SLOTS2, :], e2[:, n % SLOTS2, :], MAGIC, MAGIC, ALU.add, ALU.subtract)\
                  .then_inc(sem("r2_ready"), 1)

            def scale_out(g):
                seq.step(nc.vector.reciprocal(rz2[:, g * GH2:(g + 1) * GH2, :], zs2[:, g * GH2:(g + 1) * GH2, :]))
                dve.wait_ge(sem("values2_done"), GH2 * NT * (g + 1))
                nc.vector.tensor_tensor(
                    o2.rearrange("p t (h d) -> p h t d", d=HD2)[:, g * GH2:(g + 1) * GH2],
                    bank[7].rearrange("p (h t d) -> p h t d", h=GH2, t=NT),
                    bcast(rz2[:, g * GH2:(g + 1) * GH2, :], 3, HD2), ALU.mult).then_inc(sem("o2_ready"), 1)

            pair_copied(dve, H2 - 2)
            dve.wait_ge(sem("vi2_ready"), 1)
            U = H2 * NT
            for n in range(U + 1):
                if n > 4 and (n - 4) % (GH2 * NT) == 0:
                    scale_out((n - 4) // (GH2 * NT) - 1)
                if n < U:
                    top(n)
                if n:
                    to_integers(n - 1)
            scale_out(H2 // GH2 - 1)
            for b in range(4):
                if b:
                    seq.wait()
                    tile_stats(seq, (2 * b - 2, 2 * b - 1))
                dve.wait_ge(sem("proj2_done"), b + 1)
                seq.mark(nc.vector.scalar_tensor_tensor(x[:, 2 * b:2 * b + 2, :].rearrange("p a d -> p (a d)"), bank[4 + b],
                                                        tg[:, 1:2], x[:, 2 * b:2 * b + 2, :].rearrange("p a d -> p (a d)"),
                                                        ALU.mult, ALU.add))
            seq.wait()
            tile_stats(seq, (NT - 2, NT - 1))

        def small_softmax_vector(dve, seq, n, E, ps, shifted, probs, mx, total):
            dve.wait_ge(sem("router_logits"), n)
            lg = ps[:, 0:NT * E].rearrange("p (t e) -> p t e", t=NT)
            seq.step(nc.vector.tensor_reduce(mx, lg, AX.X, ALU.max))
            nc.vector.tensor_tensor(shifted, lg, bcast(mx, 2, E), ALU.subtract).then_inc(sem("router_shifted"), 1)
            dve.wait_ge(sem("router_exp"), n)
            seq.step(nc.vector.tensor_reduce(total, probs, AX.X, ALU.add))
            seq.step(nc.vector.reciprocal(total, total))
            seq.step(nc.vector.tensor_tensor(probs, probs, bcast(total, 2, E), ALU.mult))

        def small_softmax_scalar(act, n, shifted, probs):
            act.wait_ge(sem("router_shifted"), n)
            nc.scalar.activation(probs, shifted, ACT.Exp).then_inc(sem("router_exp"), 1)

        def router_tensor(pe, E, w, ps):
            for t in range(NT):
                for c in range(DC):
                    last = nc.tensor.matmul(ps[:, t * E:(t + 1) * E], xnT[:, c, t * P:(t + 1) * P], w[:, c, :],
                                            start=(c == 0), stop=(c == DC - 1))
            last.then_inc(sem("router_logits"), 1)

        E3, N3 = 16, 18
        rw3 = sb("rw3", [P, DC, E3])
        rbias3 = sb("rbias3", [P, E3])
        r = Region(arena, ARENA)
        probs3 = r.f32(NT, E3)
        shifted3 = r.f32(NT, E3)
        mx3 = r.f32(NT)
        total3 = r.f32(NT)
        val3 = r.f32(NT, E3 + 8)
        top3 = r.f32(NT, 8)
        rep3 = r.f32(NT, E3 + 8)
        mix3 = r.f32(NT, E3)
        hid3 = r.f32(2, T)
        scr3 = r.f32(2, 512)
        W3 = 10 * 1024 // 768
        w3_at = [(RING0 + s) % W3 for s in range(W3)]

        def w3(m):
            a = w3_at[m % W3] * 768
            return wring[:, a:a + 768]

        def loaded3(pe, m):
            slot = w3_at[m % W3]
            pe.wait_ge(sem(f"ring_loaded{slot}"), 16 * (m // W3 + 1 + (E0 // RING0 if slot < RING0 else 0)))

        def scale3(m, t):
            return mix3[:, t, m:m + 1] if m < E3 else tg[:, 5:6]

        dense3 = Dense("dense3", N3, 5, w3, loaded3, hid3, scr3, scale=scale3, earlier=2, ends=True)

        def l1f_sync(sp):
            sp.dma_start(rw3[:], A["l1_router"].rearrange("(c p) e -> p c e", p=P)).then_inc(sem("l1f_small_loaded"), 16)
            sp.dma_start(rbias3[:], A["l1_rbias"].rearrange("(o n) -> o n", o=1).to_broadcast([P, E3])).then_inc(sem("l1f_small_loaded"), 16)

        def l1f_sync2(sp):
            sp.wait_ge(sem("v2_blocks"), 2)
            for m in range(N3):
                if m == W3 - RING0:
                    sp.wait_ge(sem("qkT2_blocks"), H2 // 2)
                if m >= W3:
                    dense3.wait(sp, "down_done", 4 * (m - W3) + 4)
                sp.dma_start(w3(m), A["l1_experts"][m]).then_inc(sem(f"ring_loaded{w3_at[m % W3]}"), 16)

        def l1f_tensor(pe):
            ln_tensor(pe, 3)
            pe.wait_ge(sem("xnT_ready"), 16)
            pe.wait_ge(sem("l1f_small_loaded"), 32)
            router_tensor(pe, E3, rw3, bank[6])
            dense3.tensor(pe)
            wsum_tensor(pe)

        def l1f_scalar(act):
            ln_scalar(act, 3)
            small_softmax_scalar(act, 1, shifted3, probs3)
            dense3.scalar(act)
            wabs_scalar(act)

        def l1f_vector(dve, seq):
            ln_vector(dve, seq, 3)
            dve.wait_ge(sem("l1f_small_loaded"), 32)
            small_softmax_vector(dve, seq, 1, E3, bank[6], shifted3, probs3, mx3, total3)
            seq.mark(nc.vector.memset(val3[:, :, E3:E3 + 8], NONE))
            seq.step(nc.vector.tensor_tensor(val3[:, :, 0:E3], bank[6][:, 0:NT * E3].rearrange("p (t e) -> p t e", t=NT),
                                             bcast(rbias3[:], 1, NT), ALU.add))
            top_mask(seq, val3, top3, rep3, E3, 2, mix3)
            seq.step(nc.vector.tensor_tensor(mix3, mix3, probs3, ALU.mult))
            seq.step(nc.vector.tensor_reduce(total3, mix3, AX.X, ALU.add))
            seq.step(nc.vector.reciprocal(total3, total3))
            seq.step(nc.vector.scalar_tensor_tensor(mix3, mix3, tg[:, 5:6], bcast(total3, 2, E3), ALU.mult, ALU.mult))
            nc.vector.engine_nop().then_inc(sem("mix3_ready"), 1)
            bias5_vector(dve, seq)
            dense3.vector(dve, seq)
            gam_vector(dve, seq)

        wx4 = SH0[:].rearrange("p m n -> p (m n)").rearrange("p (j c n) -> p j c n", j=3, c=DC)
        bqk4 = sb("bqk4", [P, 2, DC])
        bv4 = sb("bv4", [1, D])
        HID = 4 * D
        r = Region(arena, ARENA)
        r.at = 19 * 1024
        mask4 = r.f32(NT, P)
        mask6u = r.f32(NT * P // 4).bitcast(U8)
        mask6 = r.f32(NT, P)
        off6 = r.f32(NT, P)
        PARTS5 = 3
        ROWS5 = PARTS5 * PARTS5
        biasT5 = r.bf16(2, HID)
        bias5 = sb("bias5", [P, 2, HID // P])
        bias5_left = sb("bias5_left", [P, 2, HID // P])
        bias5_parts = sb("bias5_parts", [P, PARTS5, 2, HID // P], BF16)
        bias5_dram = nc.dram_tensor("bias5_dram", [PARTS5, 2, HID], BF16)
        bout5 = r.f32(D)
        r = Region(arena, ARENA)
        qT4 = r.f32(DC, T)
        kT4 = r.f32(DC, T)
        v4 = r.f32(NT, D)
        s4 = r.f32(NT, P)
        p4 = r.f32(NT, P)
        pT4 = r.f32(NT, P)
        nmax4 = r.f32(NT)
        sum4 = r.f32(NT)
        coef4 = r.f32(NT)
        valid6 = r.f32(NT)

        class Attention:

            def __init__(self, name, gate, q, k, v, earlier):
                self.name, self.gate, self.q, self.k, self.v, self.earlier = name, gate, q, k, v, earlier

            def sem(self, what):
                return sem(f"attn_{what}")

            def wait(self, eng, what, n):
                per_run = NT if what in ("p_ready", "out_done") else 2
                eng.wait_ge(self.sem(what), n + per_run * self.earlier)

            def tensor(self, pe):
                for b in range(NT):
                    for c in range(DC):
                        last = nc.tensor.matmul(bank[4 + b // 4][:, b % 4 * P:(b % 4 + 1) * P], self.q[:, c, b * P:(b + 1) * P],
                                                self.k[:, c, b * P:(b + 1) * P], start=(c == 0), stop=(c == DC - 1))
                    if b % 4 == 3:
                        last.then_inc(self.sem("scores_done"), 1)
                for b in range(NT):
                    self.wait(pe, "p_ready", b + 1)
                    last = nc.tensor.transpose(bank[6 + b // 4][:, b % 4 * P:(b % 4 + 1) * P], p4[:, b, :], ident[:])
                    if b % 4 == 3:
                        last.then_inc(self.sem("p_blocks"), 1)
                for b in range(NT):
                    self.wait(pe, "pT_ready", b // 4 + 1)
                    nc.tensor.matmul(bank[b // 2][:, b % 2 * D:(b % 2 + 1) * D], pT4[:, b, :], self.v[:, b, :],
                                     start=True, stop=True).then_inc(self.sem("out_done"), 1)

            def scalar(self, act):
                for b in range(NT):
                    self.wait(act, "nmax_ready", b // 4 + 1)
                    nc.scalar.activation(p4[:, b, :], s4[:, b, :], ACT.Exp, bias=nmax4[:, b:b + 1],
                                         accum_out=sum4[:, b:b + 1]).then_inc(self.sem("p_ready"), 1)
                for i in range(2):
                    self.wait(act, "p_blocks", i + 1)
                    nc.scalar.copy(pT4[:, 4 * i:4 * i + 4, :].rearrange("p b q -> p (b q)"), bank[6 + i]).then_inc(self.sem("pT_ready"), 1)

            def vector(self, dve, seq, mask, offset=None, valid=None):
                for i in range(2):
                    four = slice(4 * i, 4 * i + 4)
                    self.wait(dve, "scores_done", i + 1)
                    seq.step(nc.vector.scalar_tensor_tensor(s4[:, four, :], bank[4 + i].rearrange("p (b k) -> p b k", b=4), D ** -0.5,
                                                            mask[:, four, :], ALU.mult, ALU.add if offset is None else ALU.mult))
                    if offset is not None:
                        seq.step(nc.vector.tensor_tensor(s4[:, four, :], s4[:, four, :], offset[:, four, :], ALU.add))
                    nc.vector.tensor_reduce(nmax4[:, four], s4[:, four, :], AX.X, ALU.max, negate=True).then_inc(self.sem("nmax_ready"), 1)
                self.wait(dve, "p_ready", NT)
                seq.step(nc.vector.reciprocal(coef4, sum4))
                seq.step(nc.vector.tensor_scalar(coef4, coef4, tg[:, self.gate:self.gate + 1], None, ALU.mult))
                if valid is not None:
                    seq.step(nc.vector.tensor_tensor(coef4, coef4, valid, ALU.mult))
                for b in range(NT):
                    if b and b % 2 == 0:
                        seq.wait()
                        tile_stats(seq, (b - 2, b - 1))
                    self.wait(dve, "out_done", b // 2 * 2 + 2)
                    seq.mark(nc.vector.scalar_tensor_tensor(x[:, b, :], bank[b // 2][:, b % 2 * D:(b % 2 + 1) * D], coef4[:, b:b + 1],
                                                            x[:, b, :], ALU.mult, ALU.add))
                seq.wait()
                tile_stats(seq, (NT - 2, NT - 1))

        attn4 = Attention("attn4", 2, qT4, kT4, v4, 0)
        attn6 = Attention("attn6", 3, xnT[:], cT[:], ctok[:], 1)

        def l2x_sync(sp):
            sp.wait_ge(sem("proj2_done"), 4)
            for dst, src in ((mask4, A["mask4"].rearrange("b q k -> q b k")),
                             (mask6u, A["mask6"].rearrange("(o b) k -> o (b k)", o=1).to_broadcast([P, NT * P])),
                             (bqk4[:, 0, :], A["l2_bq"]), (bqk4[:, 1, :], A["l2_bk"]),
                             (bv4[:], A["l2_bv"].rearrange("(o n) -> o n", o=1))):
                sp.dma_start(dst, src).then_inc(sem("l2x_loaded"), 16)

        def l2x_sync2(sp):
            shared0.wait(sp, "down_done", 8)
            for j, name in enumerate(("l2_wq", "l2_wk", "l2_wv")):
                sp.dma_start(wx4[:, j], A[name].rearrange("(c p) n -> p c n", p=P)).then_inc(sem("l2x_loaded"), 16)

        L2X_LOADS = 16 * 8

        def l2x_tensor(pe):
            ln_tensor(pe, 4)
            pe.wait_ge(sem("xnT_ready"), 20)
            pe.wait_ge(sem("l2x_loaded"), L2X_LOADS)
            for j in range(2):
                for f in range(DC):
                    for half in range(2):
                        for c in range(DC):
                            last = nc.tensor.matmul(bank[4 * j + 2 * f + half], wx4[:, j, c, f * P:(f + 1) * P],
                                                    xnT[:, c, half * 512:(half + 1) * 512], start=(c == 0), stop=(c == DC - 1))
                        last.then_inc(sem("qk4_done"), 1)
            for t in range(NT):
                if t % 2 == 0:
                    pe.wait_ge(sem("qk4_ready"), t // 2 + 1)
                ps = bank[t // 2][:, t % 2 * D:(t % 2 + 1) * D]
                nc.tensor.matmul(ps, ones_row[:], bv4[:], start=True, stop=False)
                for c in range(DC):
                    last = nc.tensor.matmul(ps, xnT[:, c, t * P:(t + 1) * P], wx4[:, 2, c, :], start=False, stop=(c == DC - 1))
                if t % 2:
                    last.then_inc(sem("v4_done"), 1)
            pe.wait_ge(sem("qk4_ready"), 8)
            pe.wait_ge(sem("v4_ready"), 4)
            attn4.tensor(pe)

        def l2x_scalar(act):
            ln_scalar(act, 4)
            act.wait_ge(sem("l2x_loaded"), L2X_LOADS)
            for j, dst in enumerate((qT4, kT4)):
                for f in range(DC):
                    for half in range(2):
                        act.wait_ge(sem("qk4_done"), 4 * j + 2 * f + half + 1)
                        nc.scalar.activation(dst[:, f, half * 512:(half + 1) * 512], bank[4 * j + 2 * f + half], ACT.Identity,
                                             bias=bqk4[:, j, f:f + 1]).then_inc(sem("qk4_ready"), 1)
            for b in range(4):
                act.wait_ge(sem("v4_done"), b + 1)
                nc.scalar.copy(v4[:, 2 * b:2 * b + 2, :].rearrange("p t d -> p (t d)"), bank[b]).then_inc(sem("v4_ready"), 1)
            attn4.scalar(act)

        def l2x_vector(dve, seq):
            ln_vector(dve, seq, 4)
            ternary_vector(dve, seq)
            dve.wait_ge(sem("l2x_loaded"), L2X_LOADS)
            attn4.vector(dve, seq, mask4)

        HC = HID // P
        NW = DC * HID
        w5 = wring[:, 0:3 * NW].rearrange("p (j n) -> p j n", j=3)
        onesf = sb("onesf", [P, P])
        wabs5 = sb("wabs5", [P, 3])
        gam5 = sb("gam5", [P, 3])
        igam5 = sb("igam5", [P, 3])
        r = Region(arena, ARENA)
        r.at = 14 * 1024
        wjunk5 = r.f32(NW)
        xq5 = r.bf16(NT, D)
        xqT5 = r.bf16(DC, T)
        gx5 = r.f32(NT)
        igx5 = r.f32(NT)
        inv5_f = r.f32(NT, 2)
        inv5_left = r.f32(NT, 2)
        inv5_parts = r.bf16(PARTS5, NT, 2)
        inv5 = r.bf16(NT, 2, PARTS5, PARTS5)
        invT5 = r.bf16(T)
        sx5 = r.f32(2, NT)
        r = Region(arena, 14 * 1024)
        r.at = 10 * 1024
        w5q = r.bf16(3, NW)
        r = Region(arena, 10 * 1024)
        g5 = r.f32(2, HID)
        h5 = r.f32(2, HID)
        hq5 = r.bf16(2, HID)
        hqT5 = r.bf16(2, HID)
        gh5 = r.f32(2)
        igh5 = r.f32(2)
        so5 = r.f32(4)
        y5 = r.f32(2, D)

        def l2f_bias_sync(sp):
            for j in range(2):
                sp.dma_start(bias5[:, j, :], A[("l2_gate_b", "l2_val_b")[j]].rearrange("(p n) -> p n", p=P)).then_inc(sem("l2f_bias_loaded"), 16)

        def l2f_sync(sp):
            sp.wait_ge(sem("bias5_split"), 2)
            for i in range(PARTS5):
                sp.dma_start(bias5_dram[i].rearrange("j (p n) -> p j n", p=P), bias5_parts[:, i]).then_inc(sem("l2f_bias_loaded"), 16)
            sp.dma_start(bout5, A["l2_out_b"].rearrange("(o n) -> o n", o=1).to_broadcast([P, D])).then_inc(sem("l2f_bias_loaded"), 16)
            sp.wait_ge(sem("l2f_bias_loaded"), 16 * 6)
            for j in range(2):
                for a in range(PARTS5):
                    row = ROWS5 * j + PARTS5 * a
                    sp.dma_start(biasT5[row:row + PARTS5, j, :], bias5_dram[:, j, :]).then_inc(sem("l2f_bias_loaded"), 16)

        BIAS5_LOADS = 16 * 12

        def split3(seq, part, left, src):
            seq.step(nc.vector.tensor_copy(part(0), src))
            seq.step(nc.vector.tensor_tensor(left, src, part(0), ALU.subtract))
            seq.step(nc.vector.tensor_copy(part(1), left))
            seq.step(nc.vector.tensor_tensor(left, left, part(1), ALU.subtract))
            return nc.vector.tensor_copy(part(2), left)

        def bias5_vector(dve, seq):
            dve.wait_ge(sem("l2f_bias_loaded"), 32)
            nc.vector.memset(biasT5[0:2 * ROWS5], 0.0).then_inc(sem("bias5_split"), 1)
            split3(seq, lambda i: bias5_parts[:, i], bias5_left[:], bias5[:]).then_inc(sem("bias5_split"), 1)

        def l2f_sync2(sp):
            assert w3_at[(N3 - 1) % W3] * 768 >= 3 * NW and all(w3_at[m % W3] * 768 >= 3 * NW for m in range(W3, N3))
            dense3.wait(sp, "down_done", 4 * W3)
            for j, name in enumerate(("l2_gate_w", "l2_val_w", "l2_out_w")):
                sp.dma_start(w5[:, j, :].rearrange("p (c n) -> p c n", n=HID if j < 2 else D),
                             A[name].rearrange("(c p) n -> p c n", p=P)).then_inc(sem(f"w5_loaded{j}"), 16)

        def wabs_scalar(act):
            for j in range(3):
                act.wait_ge(sem(f"w5_loaded{j}"), 16)
                if j:
                    act.wait_ge(sem("wabs_done"), j)
                nc.scalar.activation(wjunk5, w5[:, j, :], ACT.Abs, accum_out=wabs5[:, j:j + 1]).then_inc(sem("wabs_done"), 1)

        def wsum_tensor(pe):
            pe.wait_ge(sem("wabs_done"), 3)
            pe.wait_ge(sem("small_consts"), 4)
            dense3.wait(pe, "h_ready", 2 * N3)
            nc.tensor.matmul(bank[0][:, 0:3], onesf[:], wabs5[:], start=True, stop=True).then_inc(sem("wsum_done"), 1)

        def l2f_gpsimd(pool):
            nc.gpsimd.memset(onesf[:], 1.0).then_inc(sem("small_consts"), 1)

        def ternary_vector(dve, seq):
            dve.wait_ge(sem("gam5_ready"), 1)
            for j in range(3):
                seq.mark(nc.vector.tensor_scalar(w5[:, j, :], w5[:, j, :], igam5[:, j:j + 1], 1.0, ALU.mult, ALU.min))
            seq.wait()
            for j in range(3):
                seq.mark(nc.vector.tensor_scalar(w5[:, j, :], w5[:, j, :], -1.0, MAGIC, ALU.max, ALU.add))
            seq.wait()
            for j in range(3):
                nc.vector.tensor_scalar(w5q[:, j, :], w5[:, j, :], MAGIC, None, ALU.subtract).then_inc(sem("w5q_ready"), 1)

        def l2f_tensor(pe):
            for n in range(2):
                pe.wait_ge(sem("xq5_ready"), n + 1)
                for t in range(4):
                    for c in range(DC):
                        last = nc.tensor.transpose(bf(n)[:, (c * 4 + t) * P:(c * 4 + t + 1) * P], xq5[:, 4 * n + t, c * P:(c + 1) * P], identb[:])
                last.then_inc(sem("xqT5_blocks"), 1)
            pe.wait_ge(sem("xq5_ready"), 3)
            for t in range(NT):
                last = nc.tensor.transpose(bf(2)[0:2 * ROWS5, t * P:(t + 1) * P], inv5[:, t].rearrange("p j a b -> p (j a b)"), identb[:])
            last.then_inc(sem("xqT5_blocks"), 1)
            pe.wait_ge(sem("xqT5_ready"), 3)
            pe.wait_ge(sem("w5q_ready"), 2)
            pe.wait_ge(sem("l2f_bias_loaded"), BIAS5_LOADS)

            def up(t):
                for j in range(2):
                    if t:
                        pe.wait_ge(sem(("silu5_ready", "h5_made")[j]), t)
                    for half in range(2):
                        cols = slice(half * 512, (half + 1) * 512)
                        nc.tensor.matmul(bank[2 * j + half], invT5[0:2 * ROWS5, t * P:(t + 1) * P], biasT5[0:2 * ROWS5, j, cols],
                                         start=True, stop=False)
                        for c in range(DC):
                            last = nc.tensor.matmul(bank[2 * j + half], xqT5[:, c, t * P:(t + 1) * P],
                                                    w5q[:, j, c * HID + half * 512:c * HID + (half + 1) * 512],
                                                    start=False, stop=(c == DC - 1))
                    last.then_inc(sem("up5_done"), 1)

            def turn(t):
                pe.wait_ge(sem("hq5_ready"), t + 1)
                if t >= 2:
                    pe.wait_ge(sem("hqT5_ready"), t - 1)
                for c in range(HC):
                    last = nc.tensor.transpose(bf(4 + t % 2)[:, c * P:(c + 1) * P], hq5[:, t % 2, c * P:(c + 1) * P], identb[:])
                last.then_inc(sem("hqT5_blocks"), 1)

            def down(t):
                pe.wait_ge(sem("hqT5_ready"), t + 1)
                if t == 0:
                    pe.wait_ge(sem("w5q_ready"), 3)
                if t >= 2:
                    pe.wait_ge(sem("y5_ready"), t - 1)
                for c in range(HC):
                    last = nc.tensor.matmul(bank[6 + t % 2][:, 0:D], hqT5[:, t % 2, c * P:(c + 1) * P],
                                            w5q[:, 2, c * D:(c + 1) * D], start=(c == 0), stop=(c == HC - 1))
                last.then_inc(sem("down5_done"), 1)

            for t in range(NT + 3):
                if t < NT:
                    up(t)
                if 2 <= t < NT + 2:
                    turn(t - 2)
                if t >= 3:
                    down(t - 3)

        def l2f_scalar(act):
            ln_scalar(act, 5)
            for n in range(2):
                act.wait_ge(sem("xqT5_blocks"), n + 1)
                nc.scalar.copy(xqT5[:, :, n * 512:(n + 1) * 512], bf(n).rearrange("p (c t) -> p c t", c=DC)).then_inc(sem("xqT5_ready"), 1)
            act.wait_ge(sem("xqT5_blocks"), 3)
            nc.scalar.copy(invT5[0:2 * ROWS5, :], bf(2)[0:2 * ROWS5, :]).then_inc(sem("xqT5_ready"), 1)
            for t in range(NT + 2):
                if t < NT:
                    act.wait_ge(sem("up5_done"), 2 * t + 1)
                    if t >= 2:
                        act.wait_ge(sem("h5_made"), t - 1)
                    nc.scalar.activation(g5[:, t % 2, :], psum[:, 0:HID], ACT.Silu, scale=sx5[:, 0, t:t + 1]).then_inc(sem("silu5_ready"), 1)
                if t >= 2:
                    act.wait_ge(sem("hqT5_blocks"), t - 1)
                    if t >= 4:
                        act.wait_ge(sem("down5_done"), t - 3)
                    nc.scalar.copy(hqT5[:, t % 2, :], bf(4 + t % 2)).then_inc(sem("hqT5_ready"), 1)
                if 1 <= t <= NT:
                    act.wait_ge(sem("h5_shifted"), t)
                    if t >= 3:
                        act.wait_ge(sem("hqT5_blocks"), t - 2)
                    nc.scalar.activation(hq5[:, (t - 1) % 2, :], h5[:, (t - 1) % 2, :], ACT.Copy, bias=-MAGIC).then_inc(sem("hq5_ready"), 1)

        def gam_vector(dve, seq):
            dve.wait_ge(sem("wsum_done"), 1)
            seq.step(nc.vector.tensor_scalar(gam5[:], bank[0][:, 0:3], 1.0 / (D * HID), 1e-5, ALU.mult, ALU.max))
            nc.vector.reciprocal(igam5[:], gam5[:]).then_inc(sem("gam5_ready"), 1)

        def l2f_vector(dve, seq):
            ln_vector(dve, seq, 5)
            dve.wait_ge(sem("xn_ready"), NT * 6)
            dve.wait_ge(sem("gam5_ready"), 1)
            for half in range(2):
                four = slice(4 * half, 4 * half + 4)
                seq.step(nc.vector.tensor_reduce(gx5[:, four], xn[:, four, :], AX.X, ALU.max, apply_absolute_value=True))
                seq.step(nc.vector.tensor_scalar(gx5[:, four], gx5[:, four], 1e-5, 1.0 / 127.0, ALU.max, ALU.mult))
                seq.step(nc.vector.reciprocal(igx5[:, four], gx5[:, four]))
                for t in range(4 * half, 4 * half + 4):
                    seq.mark(nc.vector.tensor_scalar(xn[:, t, :], xn[:, t, :], igx5[:, t:t + 1], MAGIC, ALU.mult, ALU.add))
                seq.wait()
                nc.vector.tensor_scalar(xq5[:, four, :], xn[:, four, :], MAGIC, None, ALU.subtract).then_inc(sem("xq5_ready"), 1)
            for j in range(2):
                seq.mark(nc.vector.tensor_scalar(sx5[:, j, :], gx5, gam5[:, j:j + 1], None, ALU.mult))
            for j in range(2):
                seq.mark(nc.vector.tensor_scalar(inv5_f[:, :, j], igx5, igam5[:, j:j + 1], None, ALU.mult))
            seq.wait()
            split3(seq, lambda i: inv5_parts[:, i], inv5_left, inv5_f).then_inc(sem("vector_steps"), 1)
            seq.n += 1
            seq.wait()
            nc.vector.tensor_copy(inv5, bcast(inv5_parts.rearrange("p a t j -> p t j a"), 4, PARTS5)).then_inc(sem("xq5_ready"), 1)

            def hidden(t):
                i = t % 2
                dve.wait_ge(sem("silu5_ready"), t + 1)
                dve.wait_ge(sem("up5_done"), 2 * t + 2)
                if t >= 2:
                    dve.wait_ge(sem("hq5_ready"), t - 1)
                nc.vector.scalar_tensor_tensor(h5[:, i, :], psum[:, HID:2 * HID], sx5[:, 1, t:t + 1], g5[:, i, :], ALU.mult, ALU.mult)\
                  .then_inc(sem("h5_made"), 1)
                dve.wait_ge(sem("h5_made"), t + 1)
                seq.step(nc.vector.tensor_reduce(gh5[:, i:i + 1], h5[:, i, :], AX.X, ALU.max, apply_absolute_value=True))
                seq.step(nc.vector.tensor_scalar(gh5[:, i:i + 1], gh5[:, i:i + 1], 1e-5, 1.0 / 127.0, ALU.max, ALU.mult))
                seq.step(nc.vector.reciprocal(igh5[:, i:i + 1], gh5[:, i:i + 1]))
                seq.mark(nc.vector.tensor_scalar(so5[:, t % 4:t % 4 + 1], gh5[:, i:i + 1], gam5[:, 2:3], None, ALU.mult))
                nc.vector.tensor_scalar(h5[:, i, :], h5[:, i, :], igh5[:, i:i + 1], MAGIC, ALU.mult, ALU.add).then_inc(sem("h5_shifted"), 1)

            def output(t):
                i = t % 2
                dve.wait_ge(sem("down5_done"), t + 1)
                nc.vector.scalar_tensor_tensor(y5[:, i, :], bank[6 + i][:, 0:D], so5[:, t % 4:t % 4 + 1], bout5, ALU.mult, ALU.add)\
                  .then_inc(sem("y5_ready"), 1)

            def output_end(t):
                dve.wait_ge(sem("y5_ready"), t + 1)
                seq.mark(nc.vector.scalar_tensor_tensor(x[:, t, :], y5[:, t % 2, :], tg[:, 6:7], x[:, t, :], ALU.mult, ALU.add))

            dve.wait_ge(sem("l2f_bias_loaded"), BIAS5_LOADS)
            for t in range(NT + 3):
                if t < NT:
                    hidden(t)
                if t >= 3:
                    output(t - 3)
                if t >= 4:
                    seq.wait()
                    tile_stats(seq, (t - 4,))
                if t >= 3:
                    output_end(t - 3)
            seq.wait()
            tile_stats(seq, (NT - 1,))

        def l3x_gpsimd(pool):
            pool.wait_ge(sem("l2x_loaded"), L2X_LOADS)
            nc.gpsimd.tensor_copy(mask6.rearrange("p b k -> p (b k)"), mask6u).then_inc(sem("mask6_steps"), 1)
            pool.wait_ge(sem("mask6_steps"), 1)
            nc.gpsimd.tensor_scalar(off6, mask6, -1.0, 1e30, ALU.add, ALU.mult).then_inc(sem("mask6_steps"), 1)

        def l3x_tensor(pe):
            ln_tensor(pe, 6)
            pe.wait_ge(sem("xnT_ready"), 24)
            attn6.tensor(pe)

        def l3x_scalar(act):
            ln_scalar(act, 6)
            attn6.scalar(act)

        def l3x_vector(dve, seq):
            ln_vector(dve, seq, 6)
            dve.wait_ge(sem("mask6_steps"), 2)
            seq.step(nc.vector.tensor_reduce(valid6, mask6, AX.X, ALU.max))
            attn6.vector(dve, seq, mask6, off6, valid6)

        E7, K7, C7, FF7 = 8, 2, 320, 1024
        FC7 = FF7 // P
        JT7 = [(0, P), (P, P), (2 * P, C7 - 2 * P)]
        rw7 = sb("rw7", [P, DC, E7])
        WN7 = DC * FF7 + FC7 * D
        w7 = wring[:, 0:2 * WN7].rearrange("p (s n) -> p s n", s=2)
        r = Region(arena, ARENA)
        moe7 = Moe("moe7", E7, K7, C7, 7, r.f32(E7 * C7 // P, D), r, 0, earlier=moe0)
        probs7 = r.f32(NT, E7)
        shifted7 = r.f32(NT, E7)
        mx7 = r.f32(NT)
        total7 = r.f32(NT)
        val7 = r.f32(NT, E7 + 8)
        top7 = r.f32(NT, 8)
        rep7 = r.f32(NT, E7 + 8)
        h7 = r.f32(2, FC7, C7)
        y7 = r.f32(2, 3, D)

        def l3f_sync(sp):
            sp.dma_start(rw7[:], A["l3_router"].rearrange("(c p) e -> p c e", p=P)).then_inc(sem("rw7_loaded"), 16)
            moe7.clear_rows(sp)

        def l3f_sync2(sp):
            sp.wait_ge(sem("down5_done"), NT)
            for i in range(2):
                sp.dma_start(w7[:, i, :], A["l3_experts"][i]).then_inc(sem(f"w7_loaded{i}"), 16)
            moe7.load_rows_sync(sp)
            with sp.Fori(1, E7 // 2) as it:
                for i in range(2):
                    sp.wait_ge(sem("down7_done"), (it - 1) * 6 + 3 * i + 3)
                    sp.dma_start(w7[:, i, :], A["l3_experts"][bass.ds(it * 2 + i, 1)].rearrange("o p n -> p (o n)"))\
                      .then_inc(sem(f"w7_loaded{i}"), 16)

        def l3f_tensor(pe):
            ln_tensor(pe, 7)
            pe.wait_ge(sem("xnT_ready"), 28)
            pe.wait_ge(sem("rw7_loaded"), 16)
            router_tensor(pe, E7, rw7, bank[4])
            moe7.positions_tensor(pe, bank[5])
            moe7.rows_tensor(pe)
            with pe.Fori(0, E7 // 2) as it:
                for i in range(2):
                    pe.wait_ge(sem(f"w7_loaded{i}"), (it + 1) * 16)
                    for f in range(FC7):
                        u = (it * 2 + i) * FC7 + f
                        if i or f >= 4:
                            pe.wait_ge(sem("h7_ready"), u - 3)
                        for c in range(DC):
                            last = nc.tensor.matmul(bank[f % 4][:, 0:C7], w7[:, i, c * FF7 + f * P:c * FF7 + (f + 1) * P],
                                                    moe7.rowsT[:, c, bass.ds((it * 2 + i) * C7, C7)], start=(c == 0), stop=(c == DC - 1))
                        last.then_inc(sem("up7_done"), 1)
                for i in range(2):
                    pe.wait_ge(sem("h7_ready"), (it * 2 + i + 1) * FC7)
                    for j, (lo, n) in enumerate(JT7):
                        if i:
                            pe.wait_ge(sem("y7_ready"), it * 6 + j + 1)
                        for f in range(FC7):
                            last = nc.tensor.matmul(bank[4 + j][0:n, 0:D], h7[:, i, f, lo:lo + n],
                                                    w7[:, i, DC * FF7 + f * D:DC * FF7 + (f + 1) * D], start=(f == 0), stop=(f == FC7 - 1))
                        last.then_inc(sem("down7_done"), 1)
                pe.wait_ge(sem("y7_ready"), it * 6 + 6)

        def l3f_scalar(act):
            ln_scalar(act, 7)
            small_softmax_scalar(act, 2, shifted7, probs7)
            moe7.rows_scalar(act)
            with act.Fori(0, E7 // 2) as it:
                for i in range(2):
                    for f in range(FC7):
                        act.wait_ge(sem("up7_done"), (it * 2 + i) * FC7 + f + 1)
                        nc.scalar.activation(h7[:, i, f, :], bank[f % 4][:, 0:C7], ACT.Relu).then_inc(sem("h7_ready"), 1)

        def l3f_vector(dve, seq):
            ln_vector(dve, seq, 7)
            small_softmax_vector(dve, seq, 2, E7, bank[4], shifted7, probs7, mx7, total7)
            seq.mark(nc.vector.memset(val7[:, :, E7:E7 + 8], NONE))
            seq.step(nc.vector.tensor_copy(val7[:, :, 0:E7], probs7))
            top_mask(seq, val7, top7, rep7, E7, K7, moe7.sel)
            nc.vector.tensor_copy(moe7.selb, moe7.sel).then_inc(moe7.sem("sel_ready"), 1)
            seq.step(nc.vector.tensor_tensor(moe7.weight, moe7.sel, probs7, ALU.mult))
            moe7.slots_vector(dve, seq, bank[5])
            with dve.Fori(0, E7 // 2) as it:
                for i in range(2):
                    for j, (lo, n) in enumerate(JT7):
                        dve.wait_ge(sem("down7_done"), (it * 2 + i) * 3 + j + 1)
                        nc.vector.tensor_copy(y7[0:n, i, j, :], bank[4 + j][0:n, 0:D]).then_inc(sem("y7_ready"), 1)
                for i in range(2):
                    dve.wait_ge(sem(f"y7_stored{i}"), it * 32 + 32)
            moe7.combine_vector(dve, 0, NT * K7 // 2)
            nc.vector.engine_nop().then_inc(sem("x_final"), 1)
            moe7.combine_vector(dve, NT * K7 // 2)
            nc.vector.engine_nop().then_inc(sem("x_final"), 1)

        def l3f_gpsimd(pool):
            moe7.constants(pool)

        def l3f_gpsimd2(pool):
            moe7.scatter_gpsimd(pool)
            with pool.Fori(0, E7 // 2) as it:
                for i in range(2):
                    pool.wait_ge(sem("y7_ready"), (it * 2 + i) * 3 + 3)
                    row = (it * 2 + i) * C7
                    pool.dma_start(moe7.y_dram[bass.ds(row, 2 * P), :].rearrange("(j p) d -> p j d", p=P), y7[:, i, 0:2, :])\
                        .then_inc(sem(f"y7_stored{i}"), 16)
                    pool.dma_start(moe7.y_dram[bass.ds(row + 2 * P, C7 - 2 * P), :], y7[0:C7 - 2 * P, i, 2, :])\
                        .then_inc(sem(f"y7_stored{i}"), 16)
            for i in range(2):
                pool.wait_ge(sem(f"y7_stored{i}"), 32 * (E7 // 2))
            moe7.gather_gpsimd(pool)


        block = ctx.enter_context(nc.Block())

        @block.sync
        def _(sp):
            l0x_sync(sp)
            l0f_sync(sp)
            l1x_sync(sp)
            l0f_sync2(sp)
            l2f_bias_sync(sp)
            l1f_sync(sp)
            l1f_sync2(sp)
            l2x_sync(sp)
            l2x_sync2(sp)
            l2f_sync(sp)
            l2f_sync2(sp)
            l3f_sync(sp)
            l3f_sync2(sp)
            for half in range(2):
                tiles = slice(half * NT // 2, (half + 1) * NT // 2)
                sp.wait_ge(sem("x_final"), half + 1)
                sp.dma_start(out[tiles].rearrange("b s d -> s b d"), x[:, tiles, :]).then_inc(sem("out_stored"), 16)
            sp.wait_ge(sem("out_stored"), 32)

        @block.gpsimd
        def _(pool):
            l0x_gpsimd(pool)
            l0f_gpsimd(pool)
            l0f_gpsimd2(pool)
            l1x_gpsimd(pool)
            l2f_gpsimd(pool)
            l3x_gpsimd(pool)
            l3f_gpsimd(pool)
            l3f_gpsimd2(pool)

        @block.scalar
        def _(act):
            l0x_scalar(act)
            l0f_scalar(act)
            l1x_scalar(act)
            l1f_scalar(act)
            l2x_scalar(act)
            l2f_scalar(act)
            l3x_scalar(act)
            l3f_scalar(act)

        @block.tensor
        def _(pe):
            l0x_tensor(pe)
            l0f_tensor(pe)
            l1x_tensor(pe)
            l1f_tensor(pe)
            l2x_tensor(pe)
            l2f_tensor(pe)
            l3x_tensor(pe)
            l3f_tensor(pe)

        @block.vector
        def _(dve):
            seq = Chain(dve, sem("vector_steps"))
            l0x_vector(dve, seq)
            l0f_vector(dve, seq)
            l1x_vector(dve, seq)
            l1f_vector(dve, seq)
            l2x_vector(dve, seq)
            l2f_vector(dve, seq)
            l3x_vector(dve, seq)
            l3f_vector(dve, seq)


def kernel(**inputs):
    import numpy as np
    import concourse.bacc as bacc
    from concourse.bass_utils import run_bass_kernel_spmd

    def tr(name):
        return np.ascontiguousarray(np.asarray(inputs[name]).T)

    def same(name):
        return np.ascontiguousarray(inputs[name])

    def columns(b):
        return np.ascontiguousarray(b.reshape(-1, P).T)

    def chunks(w):
        return w.reshape(D, -1, P).transpose(1, 0, 2)

    def packed(a, b, down):
        n = a.shape[0]
        parts = [w.reshape(n, DC, P, P).transpose(0, 2, 1, 3).reshape(n, P, DC * P) for w in (a, b)]
        return np.ascontiguousarray(np.concatenate([*parts, down], axis=2))

    given = {
        "x": same("x"), "ctx": same("ctx_2048"), "g_xattn": same("g_xattn"), "g_ffn": same("g_ffn"),
        "ssm": same("L0_xattn_ssm_kernel"), "ssm_d": same("L0_xattn_D").reshape(16, 1),
        "l0_router": tr("L0_ffn_router_w"), "l0_ebias": same("L0_ffn_e_bias"),
        "l0_experts": packed(same("L0_ffn_W_gate"), same("L0_ffn_W_up"), same("L0_ffn_W_down")),
        "l0_shared": packed(*(chunks(tr("L0_ffn_shared_gate")), chunks(tr("L0_ffn_shared_up")), tr("L0_ffn_shared_down").reshape(2, P, D))),
        "l1_wq": same("L1_xattn_Wq"), "l1_wkv": same("L1_xattn_Wkv"), "l1_wp": same("L1_xattn_Wp"),
        "l1_bq": same("L1_xattn_bq"), "l1_bkv": same("L1_xattn_bkv"), "l1_bp": same("L1_xattn_bp"),
        "l1_bv": columns(same("L1_xattn_bkv")[D:]),
        "l1_router": tr("L1_ffn_router_w"), "l1_rbias": same("L1_ffn_router_bias"),
        "l1_experts": np.concatenate([
            packed(same("L1_ffn_Wu"), same("L1_ffn_Wg"), same("L1_ffn_Wd")),
            packed(chunks(same("L1_ffn_Su")[0]), chunks(same("L1_ffn_Sg")[0]), same("L1_ffn_Sd")[0].reshape(2, P, D))]),
        "l2_wq": tr("L2_xattn_Wq"), "l2_wk": tr("L2_xattn_Wk"), "l2_wv": tr("L2_xattn_Wv"),
        "l2_bq": columns(same("L2_xattn_bq")), "l2_bk": columns(same("L2_xattn_bk")), "l2_bv": same("L2_xattn_bv"),
        "mask4": same("mask_BxSxS2_ff0"), "mask6": same("mask_BxS2_bk0"),
        "l2_gate_w": tr("L2_ffn_gate_w"), "l2_val_w": tr("L2_ffn_val_w"), "l2_out_w": tr("L2_ffn_out_w"),
        "l2_gate_b": same("L2_ffn_gate_b"), "l2_val_b": same("L2_ffn_val_b"), "l2_out_b": same("L2_ffn_out_b"),
        "l3_router": same("L3_ffn_Wg"),
        "l3_experts": np.ascontiguousarray(np.concatenate([
            same("L3_ffn_w1").reshape(8, DC, P, 4 * D).transpose(0, 2, 1, 3).reshape(8, P, -1),
            same("L3_ffn_w2").reshape(8, 4 * D // P, P, D).transpose(0, 2, 1, 3).reshape(8, P, -1)], axis=2)),
    }
    nc = bacc.Bacc("TRN2", target_bir_lowering=False, num_devices=1)
    arrays, aps = {}, {}
    for name, a in given.items():
        arrays[f"in_{name}"] = a
        aps[name] = nc.dram_tensor(f"in_{name}", a.shape, mybir.dt.from_np(a.dtype), kind="ExternalInput").ap()
    out = nc.dram_tensor("out_0", (NT, P, D), F32, kind="ExternalOutput").ap()
    build(nc, aps, out)
    r = run_bass_kernel_spmd(nc, [arrays], core_ids=[0])
    return r.results[0]["out_0"]
```
